# Optimizing a Trainium2 kernel written in Bass

```python
import numpy as np
import jax
import jax.numpy as jnp

def _softmax(x, axis=-1):
    return jax.nn.softmax(x, axis=axis)

def _gelu(x):
    return jax.nn.gelu(x, approximate=True)

def _silu(x):
    return jax.nn.silu(x)

def _sigmoid(x):
    return jax.nn.sigmoid(x)

def _layernorm(x, axis=-1, eps=1e-05):
    m = jnp.mean(x, axis=axis, keepdims=True)
    v = jnp.var(x, axis=axis, keepdims=True)
    return (x - m) / jnp.sqrt(v + eps)

def _scatter_add(tgt, idx, src, axis=0):
    return tgt.at[idx].add(src)

def _segment_sum(src, seg, n):
    return jax.ops.segment_sum(src, seg, n)
kernel_name = 'mk_prb_d2_jaxref_r8_8ba154'

def setup_inputs(seed: int=0):
    np.random.seed(seed)
    _w = jnp.asarray

    def _L0_attn_setup():
        import jax, jax.numpy as jnp
        import numpy as np
        B, S, DIM = (2, 1024, 128)
        NH, NKV, HD = (16, 4, 64)
        GROUPS = NH // NKV
        CHUNK = 128
        THETA = 10000.0

        def _slopes(h):
            return jnp.asarray([2.0 ** (-8.0 / h * (i + 1)) for i in range(h)], dtype=jnp.float32)

        def _rope_tables(s, d):
            inv = 1.0 / THETA ** (np.arange(0, d, 2, dtype=np.float64) / d)
            freqs = np.outer(np.arange(s, dtype=np.float64), inv)
            emb = np.concatenate([freqs, freqs], axis=-1)
            return (jnp.asarray(np.cos(emb), jnp.float32), jnp.asarray(np.sin(emb), jnp.float32))

        def _apply_rope(x, cos, sin):
            x1, x2 = jnp.split(x, 2, axis=-1)
            rot = jnp.concatenate([-x2, x1], axis=-1)
            return x * cos + rot * sin

        def _lightning_attn(q, k, v, slopes, chunk):
            b, h, s, d = q.shape
            nc = s // chunk
            t = jnp.arange(chunk, dtype=jnp.float32)
            sl = slopes[:, None, None]
            mask = jnp.where(t[:, None] >= t[None, :], jnp.exp(-sl * (t[:, None] - t[None, :])), 0.0)
            q_dec = jnp.exp(-slopes[:, None] * (t + 1.0))[..., None]
            k_dec = jnp.exp(-slopes[:, None] * (chunk - 1.0 - t))[..., None]
            blk_dec = jnp.exp(-slopes * chunk)[None, :, None, None]

            def to_chunks(x):
                return x.reshape(b, h, nc, chunk, d).transpose(2, 0, 1, 3, 4)
            qc, kc, vc = (to_chunks(q), to_chunks(k), to_chunks(v))

            def step(kv, inp):
                qi, ki, vi = inp
                scores = jnp.einsum('bhtd,bhsd->bhts', qi, ki) * mask
                o = jnp.einsum('bhts,bhsd->bhtd', scores, vi) + jnp.einsum('bhtd,bhde->bhte', qi * q_dec, kv)
                kv = blk_dec * kv + jnp.einsum('bhtd,bhte->bhde', ki * k_dec, vi)
                return (kv, o)
            kv0 = jnp.zeros((b, h, d, d), q.dtype)
            _, outs = jax.lax.scan(step, kv0, (qc, kc, vc))
            return outs.transpose(1, 2, 0, 3, 4).reshape(b, h, s, d)
        key = jax.random.key(seed)
        k0, k1, k2, k3, k4 = jax.random.split(key, 5)
        x = jax.random.normal(k0, (B, S, DIM), jnp.float32)
        Wq = jax.random.normal(k1, (NH * HD, DIM), jnp.float32) * 0.02
        Wk = jax.random.normal(k2, (NKV * HD, DIM), jnp.float32) * 0.02
        Wv = jax.random.normal(k3, (NKV * HD, DIM), jnp.float32) * 0.02
        Wo = jax.random.normal(k4, (DIM, NH * HD), jnp.float32) * 0.02
        return {'x': x, 'Wq': Wq, 'Wk': Wk, 'Wv': Wv, 'Wo': Wo}
    _L0_attn_in = _L0_attn_setup()

    def _L0_ffn_setup():
        import jax, jax.numpy as jnp
        import numpy as np

        def _binarize(w):
            alpha = jax.lax.stop_gradient(jnp.mean(jnp.abs(w), axis=1, keepdims=True))
            bw = alpha * jnp.sign(w)
            return w + jax.lax.stop_gradient(bw - w)
        key = jax.random.key(seed)
        k1, k2, k3, k4, k5 = jax.random.split(key, 5)
        D, H = (128, 512)
        x = jax.random.normal(k1, (64, 196, D), dtype=jnp.float32)
        w1 = jax.random.normal(k2, (H, D), dtype=jnp.float32) * 0.02
        b1 = jax.random.normal(k3, (H,), dtype=jnp.float32) * 0.02
        w2 = jax.random.normal(k4, (D, H), dtype=jnp.float32) * 0.02
        b2 = jax.random.normal(k5, (D,), dtype=jnp.float32) * 0.02
        return {'x': x, 'w1': w1, 'b1': b1, 'w2': w2, 'b2': b2}
    _L0_ffn_in = _L0_ffn_setup()

    def _L1_attn_setup():
        import jax, jax.numpy as jnp
        import numpy as np
        from jax import lax
        H = 256
        N = 8
        B, L, D_MODEL = (4, 512, 128)
        D_CONV = 4

        def _s4d_kernel(log_dt, log_A_real, A_imag, C_re, C_im, L):
            dt = jnp.exp(log_dt)
            A = -jnp.exp(log_A_real) + 1j * A_imag
            C = C_re + 1j * C_im
            dtA = dt[:, None] * A
            Ct = C * (jnp.exp(dtA) - 1.0) / A
            t = jnp.arange(L, dtype=jnp.float32)
            vand = jnp.exp(dtA[:, :, None] * t)
            return 2.0 * jnp.einsum('hn,hnl->hl', Ct, vand).real
        key = jax.random.key(seed)
        ks = jax.random.split(key, 10)
        hidden_states = jax.random.normal(ks[0], (B, L, D_MODEL), dtype=jnp.float32)
        W_in = jax.random.normal(ks[1], (2 * H, D_MODEL), dtype=jnp.float32) / np.sqrt(D_MODEL)
        conv_w = jax.random.normal(ks[2], (H, D_CONV), dtype=jnp.float32) / np.sqrt(D_CONV)
        conv_b = jax.random.normal(ks[3], (H,), dtype=jnp.float32) * 0.1
        u = jax.random.uniform(ks[4], (H,), dtype=jnp.float32)
        log_dt = jnp.log(0.001) + u * (jnp.log(0.1) - jnp.log(0.001))
        log_A_real = jnp.log(0.5 * jnp.ones((H, N), dtype=jnp.float32))
        A_imag = jnp.pi * jnp.broadcast_to(jnp.arange(N, dtype=jnp.float32), (H, N)).copy()
        C_re = jax.random.normal(ks[5], (H, N), dtype=jnp.float32)
        C_im = jax.random.normal(ks[6], (H, N), dtype=jnp.float32)
        D = jnp.ones((H,), dtype=jnp.float32)
        W_out = jax.random.normal(ks[7], (D_MODEL, H), dtype=jnp.float32) / np.sqrt(H)
        return dict(hidden_states=hidden_states, W_in=W_in, conv_w=conv_w, conv_b=conv_b, log_dt=log_dt, log_A_real=log_A_real, A_imag=A_imag, C_re=C_re, C_im=C_im, D=D, W_out=W_out)
    _L1_attn_in = _L1_attn_setup()

    def _L1_ffn_setup():
        import jax, jax.numpy as jnp
        import numpy as np
        EPS = 1e-06
        TOP_K = 2
        key = jax.random.key(seed)
        k0, k1, k2, k3, k4 = jax.random.split(key, 5)
        B, S, H, I, E = (1, 256, 128, 448, 8)
        return {'hidden_states': jax.random.normal(k0, (B, S, H), jnp.float32), 'rms_weight': jnp.ones((H,), jnp.float32), 'gate_w': jax.random.normal(k1, (E, H), jnp.float32) * H ** (-0.5), 'w1': jax.random.normal(k2, (E, I, H), jnp.float32) * H ** (-0.5), 'w2': jax.random.normal(k3, (E, H, I), jnp.float32) * I ** (-0.5), 'w3': jax.random.normal(k4, (E, I, H), jnp.float32) * H ** (-0.5)}
    _L1_ffn_in = _L1_ffn_setup()
    _d = {'L0_attn_x': _L0_attn_in['x'], 'L0_attn_Wq': _L0_attn_in['Wq'], 'L0_attn_Wk': _L0_attn_in['Wk'], 'L0_attn_Wv': _L0_attn_in['Wv'], 'L0_attn_Wo': _L0_attn_in['Wo'], 'L0_ffn_w1': _L0_ffn_in['w1'], 'L0_ffn_b1': _L0_ffn_in['b1'], 'L0_ffn_w2': _L0_ffn_in['w2'], 'L0_ffn_b2': _L0_ffn_in['b2'], 'L1_attn_W_in': _L1_attn_in['W_in'], 'L1_attn_conv_w': _L1_attn_in['conv_w'], 'L1_attn_conv_b': _L1_attn_in['conv_b'], 'L1_attn_log_dt': _L1_attn_in['log_dt'], 'L1_attn_log_A_real': _L1_attn_in['log_A_real'], 'L1_attn_A_imag': _L1_attn_in['A_imag'], 'L1_attn_C_re': _L1_attn_in['C_re'], 'L1_attn_C_im': _L1_attn_in['C_im'], 'L1_attn_D': _L1_attn_in['D'], 'L1_attn_W_out': _L1_attn_in['W_out'], 'L1_ffn_rms_weight': _L1_ffn_in['rms_weight'], 'L1_ffn_gate_w': _L1_ffn_in['gate_w'], 'L1_ffn_w1': _L1_ffn_in['w1'], 'L1_ffn_w2': _L1_ffn_in['w2'], 'L1_ffn_w3': _L1_ffn_in['w3']}
    _x0 = _d['L0_attn_x']
    _d['L0_attn_x'] = jax.random.normal(jax.random.fold_in(jax.random.key(seed), 1), (32, 256, 128), dtype=_x0.dtype)
    del _x0
    return _d

def reference(L0_attn_x, L0_attn_Wq, L0_attn_Wk, L0_attn_Wv, L0_attn_Wo, L0_ffn_w1, L0_ffn_b1, L0_ffn_w2, L0_ffn_b2, L1_attn_W_in, L1_attn_conv_w, L1_attn_conv_b, L1_attn_log_dt, L1_attn_log_A_real, L1_attn_A_imag, L1_attn_C_re, L1_attn_C_im, L1_attn_D, L1_attn_W_out, L1_ffn_rms_weight, L1_ffn_gate_w, L1_ffn_w1, L1_ffn_w2, L1_ffn_w3):

    def _L0_attn_ref(x, Wq, Wk, Wv, Wo):
        import jax, jax.numpy as jnp
        import numpy as np
        B, S, DIM = (2, 1024, 128)
        NH, NKV, HD = (16, 4, 64)
        GROUPS = NH // NKV
        CHUNK = 128
        THETA = 10000.0

        def _slopes(h):
            return jnp.asarray([2.0 ** (-8.0 / h * (i + 1)) for i in range(h)], dtype=jnp.float32)

        def _rope_tables(s, d):
            inv = 1.0 / THETA ** (np.arange(0, d, 2, dtype=np.float64) / d)
            freqs = np.outer(np.arange(s, dtype=np.float64), inv)
            emb = np.concatenate([freqs, freqs], axis=-1)
            return (jnp.asarray(np.cos(emb), jnp.float32), jnp.asarray(np.sin(emb), jnp.float32))

        def _apply_rope(x, cos, sin):
            x1, x2 = jnp.split(x, 2, axis=-1)
            rot = jnp.concatenate([-x2, x1], axis=-1)
            return x * cos + rot * sin

        def _lightning_attn(q, k, v, slopes, chunk):
            b, h, s, d = q.shape
            nc = s // chunk
            t = jnp.arange(chunk, dtype=jnp.float32)
            sl = slopes[:, None, None]
            mask = jnp.where(t[:, None] >= t[None, :], jnp.exp(-sl * (t[:, None] - t[None, :])), 0.0)
            q_dec = jnp.exp(-slopes[:, None] * (t + 1.0))[..., None]
            k_dec = jnp.exp(-slopes[:, None] * (chunk - 1.0 - t))[..., None]
            blk_dec = jnp.exp(-slopes * chunk)[None, :, None, None]

            def to_chunks(x):
                return x.reshape(b, h, nc, chunk, d).transpose(2, 0, 1, 3, 4)
            qc, kc, vc = (to_chunks(q), to_chunks(k), to_chunks(v))

            def step(kv, inp):
                qi, ki, vi = inp
                scores = jnp.einsum('bhtd,bhsd->bhts', qi, ki) * mask
                o = jnp.einsum('bhts,bhsd->bhtd', scores, vi) + jnp.einsum('bhtd,bhde->bhte', qi * q_dec, kv)
                kv = blk_dec * kv + jnp.einsum('bhtd,bhte->bhde', ki * k_dec, vi)
                return (kv, o)
            kv0 = jnp.zeros((b, h, d, d), q.dtype)
            _, outs = jax.lax.scan(step, kv0, (qc, kc, vc))
            return outs.transpose(1, 2, 0, 3, 4).reshape(b, h, s, d)
        b, s, _ = x.shape
        q = (x @ Wq.T).reshape(b, s, NH, HD).transpose(0, 2, 1, 3)
        k = (x @ Wk.T).reshape(b, s, NKV, HD).transpose(0, 2, 1, 3)
        v = (x @ Wv.T).reshape(b, s, NKV, HD).transpose(0, 2, 1, 3)
        cos, sin = _rope_tables(s, HD)
        q = _apply_rope(q, cos, sin)
        k = _apply_rope(k, cos, sin)
        k = jnp.repeat(k, GROUPS, axis=1)
        v = jnp.repeat(v, GROUPS, axis=1)
        out = _lightning_attn(q, k, v, _slopes(NH), CHUNK)
        out = out.transpose(0, 2, 1, 3).reshape(b, s, NH * HD)
        return out @ Wo.T

    def _L0_ffn_ref(x, w1, b1, w2, b2):
        import jax, jax.numpy as jnp
        import numpy as np

        def _binarize(w):
            alpha = jax.lax.stop_gradient(jnp.mean(jnp.abs(w), axis=1, keepdims=True))
            bw = alpha * jnp.sign(w)
            return w + jax.lax.stop_gradient(bw - w)
        bw1 = _binarize(w1)
        h = jnp.einsum('bsd,hd->bsh', x, bw1) + b1
        h = jax.nn.gelu(h, approximate=False)
        bw2 = _binarize(w2)
        out = jnp.einsum('bsh,dh->bsd', h, bw2) + b2
        return out

    def _L1_attn_ref(hidden_states, W_in, conv_w, conv_b, log_dt, log_A_real, A_imag, C_re, C_im, D, W_out):
        import jax, jax.numpy as jnp
        import numpy as np
        from jax import lax
        H = 256
        N = 8
        B, L, D_MODEL = (4, 512, 128)
        D_CONV = 4

        def _s4d_kernel(log_dt, log_A_real, A_imag, C_re, C_im, L):
            dt = jnp.exp(log_dt)
            A = -jnp.exp(log_A_real) + 1j * A_imag
            C = C_re + 1j * C_im
            dtA = dt[:, None] * A
            Ct = C * (jnp.exp(dtA) - 1.0) / A
            t = jnp.arange(L, dtype=jnp.float32)
            vand = jnp.exp(dtA[:, :, None] * t)
            return 2.0 * jnp.einsum('hn,hnl->hl', Ct, vand).real
        B, L, _ = hidden_states.shape
        xz = jnp.einsum('bld,ed->bel', hidden_states, W_in)
        x, z = jnp.split(xz, 2, axis=1)
        w = conv_w.shape[-1]
        xp = jnp.pad(x, ((0, 0), (0, 0), (w - 1, 0)))
        x = lax.conv_general_dilated(xp, conv_w[:, None, :], (1,), 'VALID', dimension_numbers=('NCH', 'OIH', 'NCH'), feature_group_count=x.shape[1])
        x = jax.nn.silu(x + conv_b[None, :, None])
        k = _s4d_kernel(log_dt, log_A_real, A_imag, C_re, C_im, L)
        n = 2 * L
        y = jnp.fft.irfft(jnp.fft.rfft(x, n=n) * jnp.fft.rfft(k, n=n), n=n)[..., :L]
        y = y + x * D[None, :, None]
        y = y * jax.nn.silu(z)
        return jnp.einsum('bhl,dh->bld', y, W_out)

    def _L1_ffn_ref(hidden_states, rms_weight, gate_w, w1, w2, w3):
        import jax, jax.numpy as jnp
        import numpy as np
        EPS = 1e-06
        TOP_K = 2
        B, S, H = hidden_states.shape
        E = gate_w.shape[0]
        x = hidden_states.astype(jnp.float32)
        var = jnp.mean(x * x, axis=-1, keepdims=True)
        h = rms_weight * (x * jax.lax.rsqrt(var + EPS))
        logits = jnp.einsum('bsh,eh->bse', h, gate_w)
        scores = jax.nn.softmax(logits.astype(jnp.float32), axis=-1)
        top_w, top_i = jax.lax.top_k(scores, TOP_K)
        top_w = top_w / jnp.sum(top_w, axis=-1, keepdims=True)
        top_w = top_w.astype(h.dtype)
        hf = h.reshape(-1, H)
        oh = jax.nn.one_hot(top_i.reshape(-1, TOP_K), E, dtype=h.dtype)
        cw = jnp.einsum('tke,tk->te', oh, top_w.reshape(-1, TOP_K))
        a = jnp.einsum('th,eih->eti', hf, w1)
        g = jnp.einsum('th,eih->eti', hf, w3)
        eo = jnp.einsum('eti,ehi->eth', jax.nn.silu(a) * g, w2)
        out = jnp.einsum('eth,te->th', eo, cw)
        return hidden_states + out.reshape(B, S, H)
    x = L0_attn_x
    xn = _layernorm(x, axis=-1)
    x = x + _L0_attn_ref(xn, L0_attn_Wq, L0_attn_Wk, L0_attn_Wv, L0_attn_Wo) + _L0_ffn_ref(xn, L0_ffn_w1, L0_ffn_b1, L0_ffn_w2, L0_ffn_b2)
    xn = _layernorm(x, axis=-1)
    x = x + _L1_attn_ref(xn, L1_attn_W_in, L1_attn_conv_w, L1_attn_conv_b, L1_attn_log_dt, L1_attn_log_A_real, L1_attn_A_imag, L1_attn_C_re, L1_attn_C_im, L1_attn_D, L1_attn_W_out) + _L1_ffn_ref(xn, L1_ffn_rms_weight, L1_ffn_gate_w, L1_ffn_w1, L1_ffn_w2, L1_ffn_w3)
    return x

_drawn_inputs = setup_inputs


def setup_inputs(seed=0):
    import zlib

    import numpy as np

    out = dict(_drawn_inputs(seed))
    spreads = {'L1_attn_log_A_real': (-0.6931471824645996, 0.6),
     'L1_attn_D': (1.0, 0.2),
     'L1_ffn_rms_weight': (1.0, 0.2)}
    factors = {'L0_ffn_b1': 7.219}
    for name, (base, spread) in spreads.items():
        noise = np.random.default_rng([zlib.crc32(name.encode()), seed]).standard_normal(out[name].shape)
        drawn = base * np.exp(spread * noise) if base else spread * noise
        out[name] = jnp.asarray(drawn.astype(out[name].dtype))
    for name, factor in factors.items():
        out[name] = (out[name] * factor).astype(out[name].dtype)
    return out
```

```python
import math
from contextlib import ExitStack

import concourse.bass as bass
import concourse.mybir as mybir
import numpy as np

F32 = mybir.dt.float32
I32 = mybir.dt.int32
U32 = mybir.dt.uint32
ALU = mybir.AluOpType
ACT = mybir.ActivationFunctionType
AX = mybir.AxisListType

P = 128
B, S, D = 32, 256, 128
TILES = B * S // P
TPS = S // P
NH, NKV, HD = 16, 4, 64
PAIRS = NH // 2
HID = 512
HB = HID // P
CH, NS, TAPS = 256, 8, 4
CB = CH // P
E, EI = 8, 448
EC = 112
ES = EI // EC
SLOT_TILES = 2 * TILES + E
SLOTS = SLOT_TILES * P
SCW = S + P
EPS_LN, EPS_RMS = 1e-5, 1e-6
GB = 8
GROUPS = CH // GB


def reach(eng, semaphore, value):
    if isinstance(value, int) and value <= 0:
        return
    eng.wait_ge(semaphore, value)


def wait_apart(eng, started, *waits):
    counts = [(s, v if isinstance(v, int) else eng.to_reg(v)) for s, v in waits]
    eng.wait_ge(*started)
    for semaphore, value in counts:
        reach(eng, semaphore, value)


class Chain:

    def __init__(self, eng, semaphore):
        self.eng, self.semaphore, self.count = eng, semaphore, 0

    def __call__(self, instruction):
        self.count += 1
        instruction.then_inc(self.semaphore, 1)
        self.eng.wait_ge(self.semaphore, self.count)


def setup_block(nc, d, w):
    with ExitStack() as ctx:
        def sb(name, shape, dt=F32):
            return ctx.enter_context(nc.sbuf_tensor(name, shape, dt))

        def sem(name):
            return ctx.enter_context(nc.semaphore(name))

        w1 = sb("w1_rows", [P, HB, D])
        w2 = sb("w2_rows", [P, HID])
        ta, tb = sb("sign_pos", [P, HID]), sb("sign_neg", [P, HID])
        alpha = sb("alpha", [P, HB + 1])
        bw = sb("bw_rows", [P, 2, HID])
        ident = sb("ident_setup", [P, P])
        ld = sb("log_dt_sb", [P, CB])
        lar, aim = sb("log_a_real_sb", [P, CB, NS]), sb("a_imag_sb", [P, CB, NS])
        cre, cim = sb("c_re_sb", [P, CB, NS]), sb("c_im_sb", [P, CB, NS])
        dskip = sb("d_skip_sb", [P, CB])
        dt = sb("dt_sb", [P, CB])
        s4 = sb("s4_small", [P, 20, CB * NS])
        turns = sb("turns", [P, CB * NS], I32)
        wr, wi = sb("w_re", [P, CB * NS, S]), sb("w_im", [P, CB * NS, S])
        pr, pi = sb("prod_re", [P, CB * NS, S // 2]), sb("prod_im", [P, CB * NS, S // 2])
        kpad = sb("kpad_sb", [P, CB, P + S])
        win, cw = sb("win_x", [P, CH]), sb("conv_w_bc", [P, TAPS, CH])
        wtap = sb("wtap_sb", [P, TAPS, CH])
        zero = sb("zero_rows", [P, 8, D])
        pt = [ctx.enter_context(nc.psum_tensor(f"bw_turn{i}", [P, HID], F32)) for i in range(2)]

        s_in, s_step = sem("s_setup_loaded"), sem("s_setup_step")
        s_bw, s_turn = sem("s_bw_ready"), sem("s_bw_turned")
        s_exp, s_sinarg, s_sin, s_areal = sem("s_exp"), sem("s_sin_args"), sem("s_sin"), sem("s_a_real")
        s_k, s_out, s_zero, s_cp = sem("s_kernel_ready"), sem("s_setup_stored"), sem("s_zero_ready"), sem("s_bw_copied")
        loads = [
            (w1[:], d["ffn_w1"].rearrange("(c p) d -> p c d", p=P)), (w2[:], d["ffn_w2"]),
            (ident[:], d["ident"]),
            (ld[:], d["log_dt"]),
            (lar[:], d["log_A_real"].rearrange("(c p) n -> p c n", p=P)),
            (aim[:], d["A_imag"].rearrange("(c p) n -> p c n", p=P)),
            (cre[:], d["C_re"].rearrange("(c p) n -> p c n", p=P)),
            (cim[:], d["C_im"].rearrange("(c p) n -> p c n", p=P)),
            (dskip[:], d["D_skip"]),
            (win[:], d["W_inT"][:, 0:CH]),
            (cw[:], d["conv_wT"].partition_broadcast(P)),
        ]
        block = ctx.enter_context(nc.Block())

        @block.sync
        def _(sp):
            for dst, src in loads:
                sp.dma_start(dst, src).then_inc(s_in, 16)
            sp.wait_ge(s_zero, 1)
            rows = d["slot_in"].rearrange("(g j p) d -> g p j d", p=P, j=8)
            for g in range(SLOT_TILES // 8):
                sp.dma_start(rows[g], zero[:]).then_inc(s_out, 16)
            sp.wait_ge(s_k, 1)
            sp.dma_start(d["kpad"].rearrange("(c p) l -> p c l", p=P), kpad[:]).then_inc(s_out, 16)
            sp.wait_ge(s_k, 2)
            sp.dma_start(d["wtap"], wtap[:]).then_inc(s_out, 16)
            sp.wait_ge(s_out, 16 * (SLOT_TILES // 8 + 2))

        @block.gpsimd
        def _(pool):
            nc.gpsimd.memset(zero[:], 0.0).then_inc(s_zero, 1)

        @block.tensor
        def _(pe):
            pe.wait_ge(s_in, 16 * len(loads))
            pe.wait_ge(s_bw, 2)
            for m in range(2):
                for c in range(HB):
                    last = nc.tensor.transpose(pt[m][:, c * P:(c + 1) * P], bw[:, m, c * P:(c + 1) * P], ident[:])
                last.then_inc(s_turn, 1)

        @block.scalar
        def _(act):
            act.wait_ge(s_in, 16 * len(loads))
            nc.scalar.activation(dt[:], ld[:], ACT.Exp).then_inc(s_exp, 1)
            nc.scalar.activation(s4[:, 0, :], lar[:].rearrange("p c n -> p (c n)"), ACT.Exp).then_inc(s_exp, 1)
            act.wait_ge(s_areal, 1)
            nc.scalar.activation(s4[:, 4, :], s4[:, 2, :], ACT.Exp).then_inc(s_exp, 1)
            act.wait_ge(s_sinarg, 1)
            nc.scalar.activation(s4[:, 7, :], s4[:, 5, :], ACT.Sin).then_inc(s_sin, 1)
            nc.scalar.activation(s4[:, 8, :], s4[:, 6, :], ACT.Sin).then_inc(s_sin, 1)
            act.wait_ge(s_turn, 1)
            nc.scalar.activation(w["bw1T"][:], pt[0][:], ACT.Copy).then_inc(s_cp, 1)
            act.wait_ge(s_turn, 2)
            nc.scalar.activation(w["bw2T"][:], pt[1][:], ACT.Copy).then_inc(s_cp, 1)

        @block.vector
        def _(dve):
            v = nc.vector
            step = Chain(dve, s_step)
            dve.wait_ge(s_in, 16 * len(loads))
            rows = w1[:].rearrange("p c d -> p (c d)")
            step(v.scalar_tensor_tensor(ta[:], rows, -1.0, rows, ALU.mult, ALU.max))
            step(v.tensor_reduce(alpha[:, 0:HB], ta[:].rearrange("p (c d) -> p c d", c=HB), AX.X, ALU.add))
            step(v.scalar_tensor_tensor(tb[:], w2[:], -1.0, w2[:], ALU.mult, ALU.max))
            step(v.tensor_reduce(alpha[:, HB:HB + 1], tb[:], AX.X, ALU.add))
            step(v.tensor_scalar(alpha[:, 0:HB], alpha[:, 0:HB], 1.0 / D, None, ALU.mult))
            step(v.tensor_scalar(alpha[:, HB:HB + 1], alpha[:, HB:HB + 1], 1.0 / HID, None, ALU.mult))
            for m, src in ((0, w1[:].rearrange("p c d -> p (c d)")), (1, w2[:])):
                step(v.tensor_scalar(ta[:], src, 0.0, None, ALU.is_gt))
                step(v.tensor_scalar(tb[:], src, 0.0, None, ALU.is_lt))
                step(v.tensor_tensor(ta[:], ta[:], tb[:], ALU.subtract))
                for c in range(HB):
                    a = alpha[:, c:c + 1] if m == 0 else alpha[:, HB:HB + 1]
                    q = slice(c * P, (c + 1) * P)
                    step(v.scalar_tensor_tensor(tb[:, q], ta[:, q], a, src[:, q], ALU.mult, ALU.subtract))
                v.tensor_tensor(bw[:, m, :], tb[:], src, ALU.add).then_inc(s_bw, 1)
                dve.wait_ge(s_bw, m + 1)

            flat = lambda t: t[:].rearrange("p c n -> p (c n)")
            half = lambda i, c: s4[:, i, c * NS:(c + 1) * NS]
            dve.wait_ge(s_exp, 2)
            step(v.tensor_scalar(s4[:, 1, :], s4[:, 0, :], -1.0, None, ALU.mult))
            for c in range(CB):
                step(v.tensor_scalar(half(2, c), half(1, c), dt[:, c:c + 1], None, ALU.mult))
                step(v.tensor_scalar(half(3, c), aim[:, c, :], dt[:, c:c + 1], None, ALU.mult))
            v.tensor_copy(s4[:, 9, :], s4[:, 2, :]).then_inc(s_areal, 1)
            hi, lo = 6.28125, 2 * math.pi - 6.28125
            for out, shift in ((5, 0.0), (6, math.pi / 2)):
                step(v.tensor_scalar(s4[:, 10, :], s4[:, 3, :], 1.0 / (2 * math.pi), shift / (2 * math.pi), ALU.mult, ALU.add))
                step(v.tensor_copy(turns[:], s4[:, 10, :]))
                step(v.tensor_copy(s4[:, 10, :], turns[:]))
                step(v.scalar_tensor_tensor(s4[:, 11, :], s4[:, 10, :], -hi, s4[:, 3, :], ALU.mult, ALU.add))
                step(v.scalar_tensor_tensor(s4[:, 11, :], s4[:, 10, :], -lo, s4[:, 11, :], ALU.mult, ALU.add))
                step(v.tensor_scalar(s4[:, 11, :], s4[:, 11, :], shift, 3.1415925, ALU.add, ALU.min))
                step(v.tensor_scalar(s4[:, out, :], s4[:, 11, :], -3.1415925, None, ALU.max))
            v.tensor_copy(s4[:, 12, :], s4[:, 5, :]).then_inc(s_sinarg, 1)
            dve.wait_ge(s_sin, 2)
            dve.wait_ge(s_exp, 3)
            step(v.tensor_tensor(s4[:, 13, :], s4[:, 4, :], s4[:, 8, :], ALU.mult))
            step(v.tensor_tensor(s4[:, 14, :], s4[:, 4, :], s4[:, 7, :], ALU.mult))
            step(v.tensor_scalar(s4[:, 15, :], s4[:, 13, :], -1.0, None, ALU.add))
            step(v.tensor_tensor(s4[:, 16, :], flat(cre), s4[:, 15, :], ALU.mult))
            step(v.tensor_tensor(s4[:, 17, :], flat(cim), s4[:, 14, :], ALU.mult))
            step(v.tensor_tensor(s4[:, 16, :], s4[:, 16, :], s4[:, 17, :], ALU.subtract))
            step(v.tensor_tensor(s4[:, 17, :], flat(cre), s4[:, 14, :], ALU.mult))
            step(v.tensor_tensor(s4[:, 18, :], flat(cim), s4[:, 15, :], ALU.mult))
            step(v.tensor_tensor(s4[:, 17, :], s4[:, 17, :], s4[:, 18, :], ALU.add))
            step(v.tensor_tensor(s4[:, 18, :], s4[:, 1, :], s4[:, 1, :], ALU.mult))
            step(v.tensor_tensor(s4[:, 19, :], flat(aim), flat(aim), ALU.mult))
            step(v.tensor_tensor(s4[:, 18, :], s4[:, 18, :], s4[:, 19, :], ALU.add))
            step(v.reciprocal(s4[:, 19, :], s4[:, 18, :]))
            step(v.tensor_scalar(s4[:, 19, :], s4[:, 19, :], 2.0, None, ALU.mult))
            step(v.tensor_tensor(s4[:, 10, :], s4[:, 16, :], s4[:, 1, :], ALU.mult))
            step(v.tensor_tensor(s4[:, 11, :], s4[:, 17, :], flat(aim), ALU.mult))
            step(v.tensor_tensor(s4[:, 10, :], s4[:, 10, :], s4[:, 11, :], ALU.add))
            step(v.tensor_tensor(wr[:, :, 0], s4[:, 10, :], s4[:, 19, :], ALU.mult))
            step(v.tensor_tensor(s4[:, 10, :], s4[:, 17, :], s4[:, 1, :], ALU.mult))
            step(v.tensor_tensor(s4[:, 11, :], s4[:, 16, :], flat(aim), ALU.mult))
            step(v.tensor_tensor(s4[:, 10, :], s4[:, 10, :], s4[:, 11, :], ALU.subtract))
            step(v.tensor_tensor(wi[:, :, 0], s4[:, 10, :], s4[:, 19, :], ALU.mult))
            n, zr, zi = 1, 13, 14
            while n < S:
                bc = lambda i: s4[:, i, :].unsqueeze(2).to_broadcast([P, CB * NS, n])
                a, b, c, e = wr[:, :, 0:n], wi[:, :, 0:n], pr[:, :, 0:n], pi[:, :, 0:n]
                step(v.tensor_tensor(c, a, bc(zr), ALU.mult))
                step(v.tensor_tensor(e, b, bc(zi), ALU.mult))
                step(v.tensor_tensor(wr[:, :, n:2 * n], c, e, ALU.subtract))
                step(v.tensor_tensor(c, a, bc(zi), ALU.mult))
                step(v.tensor_tensor(e, b, bc(zr), ALU.mult))
                step(v.tensor_tensor(wi[:, :, n:2 * n], c, e, ALU.add))
                step(v.tensor_tensor(s4[:, 15, :], s4[:, zr, :], s4[:, zr, :], ALU.mult))
                step(v.tensor_tensor(s4[:, 16, :], s4[:, zi, :], s4[:, zi, :], ALU.mult))
                step(v.tensor_tensor(s4[:, 17, :], s4[:, zr, :], s4[:, zi, :], ALU.mult))
                step(v.tensor_tensor(s4[:, zr, :], s4[:, 15, :], s4[:, 16, :], ALU.subtract))
                step(v.tensor_scalar(s4[:, zi, :], s4[:, 17, :], 2.0, None, ALU.mult))
                n *= 2
            step(v.memset(kpad[:, :, 0:P], 0.0))
            for c in range(CB):
                step(v.tensor_reduce(kpad[:, c, P:P + S], wr[:, c * NS:(c + 1) * NS, :].rearrange("p n l -> p l n"),
                                     AX.X, ALU.add))
            v.tensor_tensor(kpad[:, :, P], kpad[:, :, P], dskip[:], ALU.add).then_inc(s_k, 1)
            for t in range(TAPS):
                last = v.tensor_tensor(wtap[:, t, :], win[:], cw[:, t, :], ALU.mult)
            last.then_inc(s_k, 1)


def layer0_block(nc, d, w):
    with ExitStack() as ctx:
        def sb(name, shape, dt=F32):
            return ctx.enter_context(nc.sbuf_tensor(name, shape, dt))

        def psum(name, shape=(P, 512)):
            return ctx.enter_context(nc.psum_tensor(name, list(shape), F32))

        def sem(name):
            return ctx.enter_context(nc.semaphore(name))

        x1, logits = w["x1"], w["logits"]
        wq, wk, wv = sb("wq_stack", [P, NH, P]), sb("wk_stack", [P, 4, P]), sb("wvT", [P, NKV * HD])
        wo = sb("woT", [P, PAIRS, D])
        rope_q = sb("rope_q", [P, S])
        rope_kc, rope_ks = sb("rope_k_cos", [P, S]), sb("rope_k_sin", [P, S])
        decay = sb("decay", [P, NH, SCW])
        b1, b2 = sb("b1_cols", [P, HB]), sb("b2_rows", [P, D])
        gate = sb("gateT", [P, E])
        rmsw = sb("rms_w", [P, 1])
        ident = sb("ident", [P, P])
        mhalf = sb("minus_half", [P, TPS])
        xn, xn2 = sb("xn", [P, TPS, D]), sb("xn2", [P, TPS, D])
        sq = sb("squares", [P, TPS, D])
        st, mv = sb("ln_stats", [P, 2, TPS, 6]), sb("ln_mean_var", [P, 2, TPS, 2])
        ve, rstd = sb("ln_var_eps", [P, 3, TPS]), sb("ln_rstd", [P, 3, TPS])
        ss = sb("square_sums", [P, TPS])
        xnT = [sb(f"xnT{i}", [P, S]) for i in range(2)]
        flip = sb("flip", [P, P])
        x2T = [sb(f"x2T{i}", [P, 2 * S]) for i in range(2)]
        hh = [sb(f"h_rows{i}", [P, TPS, D]) for i in range(2)]
        kc, ks = sb("k_cos", [P, 2, S]), sb("k_sin", [P, 2, S])
        kk = [sb(f"k_twice{i}", [P, NKV, S]) for i in range(2)]
        vv = [sb(f"v_rows{i}", [P, TPS, NKV * HD]) for i in range(2)]
        gh = [sb(f"gelu_h{i}", [P, HB, S]) for i in range(2)]
        oT = [sb(f"attn_outT{i}", [P, PAIRS, S]) for i in range(2)]
        qs = [sb(f"q_stack{i}", [P, 2, S]) for i in range(2)]
        pp = [sb(f"probs{i}", [P, 2, SCW]) for i in range(2)]

        bank_q = psum("bank_q")
        bank_s = [psum(f"bank_s{i}") for i in range(2)]
        bank_av = [psum(f"bank_av{i}") for i in range(2)]
        m0, m1, bank_o = psum("bank_m0"), psum("bank_m1"), psum("bank_out")

        s_w, s_x = sem("s_weights"), sem("s_x_loaded")
        s_c, s_gate = sem("s_exponent_ready"), sem("s_gate_ready")
        q_done, qs_ready = sem("q_done"), sem("qs_ready")
        s_done, mask_ready = sem("s_done"), sem("mask_ready")
        av_done, ot_ready = sem("av_done"), sem("ot_ready")
        f_done, gh_ready = sem("f_done"), sem("gh_ready")
        o_done = sem("o_done")
        t_done, xnT_ready = sem("t_done"), sem("xnT_ready")
        k_done, kc_done, kk_ready = sem("k_done"), sem("kc_done"), sem("kk_ready")
        vp_done, v_ready = sem("vp_done"), sem("v_ready")
        t2_done, x2T_ready = sem("t2_done"), sem("x2T_ready")
        lg_done, lg_ready = sem("lg_done"), sem("lg_ready")
        st1, agg1, ve1, rs1, xn_ready = sem("st1"), sem("agg1"), sem("ve1"), sem("rstd1_ready"), sem("xn_ready")
        xres_ready = sem("xres_ready")
        x1a, x1_ready = sem("x1_sum"), sem("x1_ready")
        st2, agg2, ve2, rs2, xn2_ready = sem("st2"), sem("agg2"), sem("ve2"), sem("rstd2_ready"), sem("xn2_ready")
        ss_ready, ve3, r_ready, hh_ready = sem("ss_ready"), sem("ve3"), sem("r_ready"), sem("hh_ready")
        x2T_stored, hh_stored = ([sem(f"{n}_stored{i}") for i in range(2)] for n in ("x2T", "hh"))

        loads = [(wq[:], d["wq"]), (wk[:], d["wk"]), (wv[:], d["wv"]), (wo[:], d["wo"]),
                 (rope_q[:], d["rope_q"]), (rope_kc[:], d["rope_kc"]), (rope_ks[:], d["rope_ks"]),
                 (decay[:], d["decay"]), (b1[:], d["ffn_b1"]),
                 (b2[:], d["ffn_b2"].partition_broadcast(P)),
                 (gate[:], d["gateT"]), (rmsw[:], d["rms_w"]),
                 (ident[:], d["ident"]), (flip[:], d["flip"])]
        block = ctx.enter_context(nc.Block())

        def iterations(eng, body):
            body(-1, 1, cur=False, prev=False, nxt=True)
            body(0, 0, cur=True, prev=False, nxt=True)
            body(1, 1, cur=True, prev=True, nxt=True)
            body(2, 0, cur=True, prev=True, nxt=True)
            with eng.Fori(3, B - 2, 2) as b:
                body(b, 1, cur=True, prev=True, nxt=True)
                body(b + 1, 0, cur=True, prev=True, nxt=True)
            body(B - 1, 1, cur=True, prev=True, nxt=False)
            body(B, 0, cur=False, prev=True, nxt=False)

        @block.sync
        def _(sp):
            xr = d["x"].rearrange("b (t p) d -> p (b t) d", p=P)
            for q in range(8):
                a = q * TILES // 8
                sp.dma_start(x1[:, a:a + TILES // 8, :], xr[:, a:a + TILES // 8, :]).then_inc(s_x, 16)
                if q == 0:
                    for dst, src in loads:
                        sp.dma_start(dst, src).then_inc(s_w, 16)

            def body(b, par, cur, prev, nxt):
                if not prev:
                    return
                sp.wait_ge(x2T_ready, b)
                sp.dma_start(d["x2T"][bass.ds(b - 1, 1)].rearrange("a p t -> p (a t)"), x2T[1 - par][:]).then_inc(x2T_stored[1 - par], 16)
                sp.wait_ge(hh_ready, b)
                sp.dma_start(d["h_rows"][bass.ds(b - 1, 1)].rearrange("a (t p) d -> p (a t) d", p=P),
                             hh[1 - par][:]).then_inc(hh_stored[1 - par], 16)

            iterations(sp, body)
            for stored in x2T_stored + hh_stored:
                sp.wait_ge(stored, 16 * (B // 2))

        @block.gpsimd
        def _(pool):
            g = nc.gpsimd
            g.memset(mhalf[:], -0.5).then_inc(s_c, 1)
            pool.wait_ge(s_c, 1)
            pool.wait_ge(s_w, 16 * len(loads))

            def rsqrt(n, src, add, counted, value, ready):
                if n < 2:
                    g.tensor_scalar(ve[:, n, :], src, add, None, ALU.add).then_inc(counted, 1)
                else:
                    g.tensor_scalar(ve[:, n, :], src, 1.0 / D, add, ALU.mult, ALU.add).then_inc(counted, 1)
                pool.wait_ge(counted, value)
                g.tensor_tensor(rstd[:, n, :], ve[:, n, :], mhalf[:], ALU.pow).then_inc(ready, 1)

            def body(b, par, cur, prev, nxt):
                if nxt:
                    wait_apart(pool, (s_c, 1), (agg1, b + 2), (xn_ready, b + 1))
                    rsqrt(0, mv[:, 0, :, 1], EPS_LN, ve1, b + 2, rs1)
                if prev:
                    wait_apart(pool, (s_c, 1), (agg2, b), (xn2_ready, b - 1))
                    rsqrt(1, mv[:, 1, :, 1], EPS_LN, ve2, b, rs2)
                    wait_apart(pool, (s_c, 1), (ss_ready, b), (hh_ready, b - 1), (lg_ready, b - 1))
                    rsqrt(2, ss[:], EPS_RMS, ve3, b, r_ready)

            iterations(pool, body)

        @block.tensor
        def _(pe):
            t = nc.tensor
            pe.wait_ge(s_w, 16 * len(loads))
            pe.wait_ge(s_gate, 1)

            def body(b, par, cur, prev, nxt):
                nb = 1 - par
                for j in range(PAIRS):
                    n = b * PAIRS + j
                    if cur:
                        if j == 0:
                            pe.wait_ge(kk_ready, b + 1)
                        pe.wait_ge(qs_ready, n + 1)
                        reach(pe, mask_ready, 2 * n)
                        for h in range(2):
                            g = (2 * j + h) // (NH // NKV)
                            t.matmul(bank_s[h][:, 0:S], kk[par][:, g, 0:P], qs[j % 2][:, h, :], start=True, stop=True)
                            t.matmul(bank_s[h][:, S:SCW], kk[par][:, g, P:S], qs[j % 2][:, h, P:S],
                                     start=True, stop=True).then_inc(s_done, 1)
                    if (cur and j < PAIRS - 1) or (nxt and j == PAIRS - 1):
                        src, nj = (xnT[par], j + 1) if j < PAIRS - 1 else (xnT[nb], 0)
                        if j == PAIRS - 1:
                            pe.wait_ge(xnT_ready, b + 2)
                        for h in range(2):
                            last = t.matmul(bank_q[:, h * S:(h + 1) * S], wq[:, 2 * nj + h, :], src[:], start=True, stop=True)
                        last.then_inc(q_done, 1)
                    if (cur and j > 0) or (prev and j == 0):
                        pj, vb, vseq = (j - 1, vv[par], b) if j else (PAIRS - 1, vv[nb], b - 1)
                        reach(pe, mask_ready, 2 * n)
                        reach(pe, ot_ready, n - 2)
                        if j < 2:
                            pe.wait_ge(v_ready, vseq + 1)
                        bank = bank_av[(j + 1) % 2]
                        for c in range(TPS):
                            for h in range(2):
                                g = (2 * pj + h) // (NH // NKV)
                                cols = slice(0, S) if c == 0 else slice(P, S)
                                rhs = pp[pj % 2][:, h, 0:S] if c == 0 else pp[pj % 2][:, h, S:SCW]
                                last = t.matmul(bank[h * HD:(h + 1) * HD, cols], vb[:, c, g * HD:(g + 1) * HD], rhs,
                                                start=(c == 0), stop=(c == 1), skip_group_check=True)
                        last.then_inc(av_done, 1)
                    if j in (0, 1) and cur:
                        if j == 0:
                            pe.wait_ge(v_ready, b + 1)
                        else:
                            reach(pe, lg_ready, b - 1)
                        for c in range(2):
                            last = t.matmul((m0, m1)[j][:, c * S:(c + 1) * S], w["bw1T"][:, (2 * j + c) * P:(2 * j + c + 1) * P],
                                            xnT[par][:], start=True, stop=True)
                        last.then_inc(f_done, 1)
                    if j == 2 and prev:
                        pe.wait_ge(ot_ready, PAIRS * b)
                        pe.wait_ge(gh_ready, 2 * b)
                        reach(pe, x1a, b - 1)
                        for c in range(TPS):
                            q = slice(c * P, (c + 1) * P)
                            for k in range(PAIRS):
                                t.matmul(bank_o[:, q], oT[nb][:, k, q], wo[:, k, :], start=(k == 0), stop=False)
                            for k in range(HB):
                                last = t.matmul(bank_o[:, q], gh[nb][:, k, q], w["bw2T"][:, k * P:(k + 1) * P],
                                                start=False, stop=(k == HB - 1))
                        last.then_inc(o_done, 1)
                    if j == 3 and nxt:
                        pe.wait_ge(xn_ready, b + 2)
                        reach(pe, gh_ready, 2 * b + 2)
                        for c in range(TPS):
                            last = t.transpose(m0[:, c * P:(c + 1) * P], xn[:, c, :], ident[:])
                        last.then_inc(t_done, 1)
                    if j == 4 and nxt:
                        pe.wait_ge(xnT_ready, b + 2)
                        for c in range(4):
                            last = t.matmul((m0, m1)[c // 2][:, (c % 2) * S:(c % 2 + 1) * S], wk[:, c, :], xnT[nb][:],
                                            start=True, stop=True)
                        last.then_inc(k_done, 1)
                    if j == 5 and nxt:
                        pe.wait_ge(kc_done, b + 2)
                        for c in range(TPS):
                            last = t.matmul(m0[:, c * S:(c + 1) * S], xnT[nb][:, c * P:(c + 1) * P], wv[:], start=True, stop=True)
                        last.then_inc(vp_done, 1)
                    if j == 6 and prev:
                        pe.wait_ge(xn2_ready, b)
                        if not nxt:
                            reach(pe, gh_ready, 2 * B)
                        for c in range(TPS):
                            t.transpose(m1[:, c * P:(c + 1) * P], xn2[:, c, :], ident[:])
                            back = S + (TPS - 1 - c) * P
                            last = t.transpose(m1[:, back:back + P], xn2[:, c, :], flip[:])
                        last.then_inc(t2_done, 1)
                    if j == 7 and prev:
                        pe.wait_ge(x2T_ready, b)
                        for c in range(TPS):
                            last = t.matmul(m1[:, c * E:(c + 1) * E], x2T[nb][:, c * P:(c + 1) * P], gate[:], start=True, stop=True)
                        last.then_inc(lg_done, 1)

            iterations(pe, body)

        @block.scalar
        def _(act):
            a = nc.scalar
            act.wait_ge(s_w, 16 * len(loads))

            def body(b, par, cur, prev, nxt):
                nb = 1 - par
                for j in range(PAIRS):
                    n = b * PAIRS + j
                    if (cur and j > 0) or (prev and j == 0):
                        pj, dst = (j - 1, oT[par]) if j else (PAIRS - 1, oT[nb])
                        act.wait_ge(av_done, n)
                        if j == 1:
                            reach(act, o_done, b - 1)
                        a.activation(dst[:, pj, :], bank_av[(j + 1) % 2][:, 0:S], ACT.Copy).then_inc(ot_ready, 1)
                    if j in (0, 1) and cur:
                        act.wait_ge(f_done, 2 * b + j + 1)
                        reach(act, o_done, b - 1)
                        for c in range(2):
                            k = 2 * j + c
                            last = a.activation(gh[par][:, k, :], (m0, m1)[j][:, c * S:(c + 1) * S], ACT.Gelu, bias=b1[:, k:k + 1])
                        last.then_inc(gh_ready, 1)
                    if j == 3 and nxt:
                        act.wait_ge(t_done, b + 2)
                        a.activation(xnT[nb][:], m0[:, 0:S], ACT.Copy).then_inc(xnT_ready, 1)
                    if j == 5 and nxt:
                        act.wait_ge(vp_done, b + 2)
                        a.activation(vv[nb][:].rearrange("p t n -> p (t n)"), m0[:], ACT.Copy).then_inc(v_ready, 1)
                    if j == 6 and prev:
                        act.wait_ge(t2_done, b)
                        reach(act, lg_done, b - 2)
                        reach(act, x2T_stored[nb], 8 * (b - 1 - nb))
                        a.activation(x2T[nb][:], m1[:], ACT.Copy).then_inc(x2T_ready, 1)
                        reach(act, r_ready, b - 1)
                        reach(act, ss_ready, b - 1)
                        for c in range(TPS):
                            last = a.activation(sq[:, c, :], xn2[:, c, :], ACT.Square, accum_out=ss[:, c:c + 1])
                        last.then_inc(ss_ready, 1)

            iterations(act, body)

        @block.vector
        def _(dve):
            v = nc.vector
            dve.wait_ge(s_w, 16 * len(loads))
            v.tensor_scalar(gate[:], gate[:], rmsw[:, 0:1], None, ALU.mult).then_inc(s_gate, 1)

            def body(b, par, cur, prev, nxt):
                nb = 1 - par
                for j in range(PAIRS):
                    n = b * PAIRS + j
                    if cur:
                        for h in range(2):
                            dve.wait_ge(s_done, 2 * n + h + 1)
                            if h == 0:
                                reach(dve, av_done, n - 1)
                            v.tensor_tensor(pp[j % 2][:, h, :], bank_s[h][:, 0:SCW], decay[:, 2 * j + h, :],
                                            ALU.mult).then_inc(mask_ready, 1)
                    if (cur and j < PAIRS - 1) or (nxt and j == PAIRS - 1):
                        dve.wait_ge(q_done, n + 2)
                        v.tensor_tensor(qs[(j + 1) % 2][:], bank_q[:].rearrange("p (h t) -> p h t", h=2),
                                        rope_q[:].unsqueeze(1).to_broadcast([P, 2, S]), ALU.mult).then_inc(qs_ready, 1)
                    if j == 0 and nxt:
                        wait_apart(dve, (s_x, 128), (rs1, b + 1), (agg1, b + 1))
                        for c in range(TPS):
                            last = v.bn_stats(st[:, 0, c, :], x1[:, bass.ds(2 * b + 2 + c, 1), :].rearrange("p a d -> p (a d)"))
                        last.then_inc(st1, 1)
                        wait_apart(dve, (s_x, 128), (st1, b + 2), (xn_ready, b + 1))
                        for c in range(TPS):
                            last = v.bn_aggr(mv[:, 0, c, :], st[:, 0, c, :])
                        last.then_inc(agg1, 1)
                    if j == 2 and nxt:
                        dve.wait_ge(rs1, b + 2)
                        reach(dve, t_done, b + 1)
                        for c in range(TPS):
                            last = v.tensor_scalar(xn[:, c, :], x1[:, bass.ds(2 * b + 2 + c, 1), :].rearrange("p a d -> p (a d)"),
                                                   mv[:, 0, c, 0:1], rstd[:, 0, c:c + 1], ALU.subtract, ALU.mult)
                        last.then_inc(xn_ready, 1)
                    if j == 3 and prev:
                        rows = x1[:, bass.ds(2 * b - 2, 2), :]
                        dve.wait_ge(o_done, b)
                        v.tensor_tensor(rows, bank_o[:, 0:S].rearrange("p (t d) -> p t d", t=TPS), rows, ALU.add).then_inc(x1a, 1)
                        dve.wait_ge(x1a, b)
                        v.tensor_tensor(rows, rows, b2[:].unsqueeze(1).to_broadcast([P, TPS, D]), ALU.add).then_inc(x1_ready, 1)
                        wait_apart(dve, (s_x, 128), (x1_ready, b), (agg2, b - 1))
                        for c in range(TPS):
                            last = v.bn_stats(st[:, 1, c, :], x1[:, bass.ds(2 * b - 2 + c, 1), :].rearrange("p a d -> p (a d)"))
                        last.then_inc(st2, 1)
                        wait_apart(dve, (s_x, 128), (st2, b), (xn2_ready, b - 1), (rs2, b - 1))
                        for c in range(TPS):
                            last = v.bn_aggr(mv[:, 1, c, :], st[:, 1, c, :])
                        last.then_inc(agg2, 1)
                    if j == 4 and nxt:
                        dve.wait_ge(k_done, b + 2)
                        reach(dve, kk_ready, b + 1)
                        bc = lambda r: r[:].unsqueeze(1).to_broadcast([P, 2, S])
                        v.tensor_tensor(kc[:], m0[:].rearrange("p (u t) -> p u t", u=2), bc(rope_kc), ALU.mult)
                        v.tensor_tensor(ks[:], m1[:].rearrange("p (u t) -> p u t", u=2), bc(rope_ks), ALU.mult).then_inc(kc_done, 1)
                        dve.wait_ge(kc_done, b + 2)
                        for g in range(NKV):
                            r = slice((g % 2) * HD, (g % 2 + 1) * HD)
                            for half in range(2):
                                last = v.tensor_tensor(kk[nb][half * HD:(half + 1) * HD, g, :], kc[r, g // 2, :], ks[r, g // 2, :], ALU.add)
                        last.then_inc(kk_ready, 1)
                    if j == 5 and prev:
                        dve.wait_ge(rs2, b)
                        reach(dve, t2_done, b - 1)
                        reach(dve, hh_ready, b - 1)
                        reach(dve, xres_ready, b - 1)
                        reach(dve, ss_ready, b - 1)
                        for c in range(TPS):
                            last = v.tensor_scalar(xn2[:, c, :], x1[:, bass.ds(2 * b - 2 + c, 1), :].rearrange("p a d -> p (a d)"),
                                                   mv[:, 1, c, 0:1], rstd[:, 1, c:c + 1], ALU.subtract, ALU.mult)
                        last.then_inc(xn2_ready, 1)
                    if j == 7 and prev:
                        rows = x1[:, bass.ds(2 * b - 2, 2), :]
                        dve.wait_ge(xn2_ready, b)
                        v.tensor_tensor(rows, rows, xn2[:], ALU.add).then_inc(xres_ready, 1)
                        dve.wait_ge(r_ready, b)
                        reach(dve, hh_stored[nb], 8 * (b - 1 - nb))
                        for c in range(TPS):
                            last = v.tensor_scalar(hh[nb][:, c, :], xn2[:, c, :], rstd[:, 2, c:c + 1], None, ALU.mult)
                        last.then_inc(hh_ready, 1)
                        dve.wait_ge(lg_done, b)
                        for c in range(TPS):
                            last = v.tensor_scalar(logits[:, bass.ds(2 * b - 2 + c, 1), :].rearrange("p a e -> p (a e)"),
                                                   m1[:, c * E:(c + 1) * E], rstd[:, 2, c:c + 1], None, ALU.mult)
                        last.then_inc(lg_ready, 1)

            iterations(dve, body)


SCRATCH = {"slot_in": (SLOTS, D), "slot_out": (SLOTS, D), "kpad": (CH, P + S), "wtap": (P, TAPS, CH),
           "x2T": (B, P, 2 * S), "h_rows": (B, S, D)}


def routing_block(nc, d, w):
    with ExitStack() as ctx:
        def sb(name, shape, dt=F32):
            return ctx.enter_context(nc.sbuf_tensor(name, shape, dt))

        def sem(name):
            return ctx.enter_context(nc.semaphore(name))

        logits, slot, weight, tile_expert = w["logits"], w["slot"], w["weight"], w["tile_expert"]
        full = [P, TILES, E]
        earlier, ones = sb("earlier_sb", [P, P]), sb("ones_sb", [P, P])
        eid, tid = sb("expert_minus", [P, E]), sb("tile_ids", [1, SLOT_TILES])
        scores, work, one0, one1, taken = (sb(n, full) for n in ("scores", "work", "is_first", "is_second", "is_taken"))
        before, scan_a, scan_b = (sb(n, full) for n in ("rank_before", "scan_a", "scan_b"))
        top, low, tot = sb("top", [P, 3, TILES]), sb("low", [P, TILES]), sb("total", [P, TILES])
        cnt, cnt_i = sb("tiles_of", [P, 4, E]), sb("tiles_of_int", [P, E], I32)
        te = sb("tile_expert_f", [1, SLOT_TILES])
        bank_r = ctx.enter_context(nc.psum_tensor("bank_rank", [P, 512], F32))
        bank_t = ctx.enter_context(nc.psum_tensor("bank_total", [P, 512], F32))
        s_in, s_step = sem("s_route_loaded"), sem("s_route_step")
        s_sh, s_ex, s_oh, s_cnt = sem("s_shifted"), sem("s_exps"), sem("s_onehots"), sem("s_counts")
        block = ctx.enter_context(nc.Block())

        @block.sync
        def _(sp):
            for dst, src in ((earlier[:], d["earlier"]), (ones[:], d["ones"]), (eid[:], d["expert_minus"]), (tid[:], d["tile_ids"])):
                sp.dma_start(dst, src).then_inc(s_in, 16)

        @block.scalar
        def _(act):
            act.wait_ge(s_sh, 1)
            nc.scalar.activation(scores[:], work[:], ACT.Exp).then_inc(s_ex, 1)

        @block.tensor
        def _(pe):
            flat = taken[:].rearrange("p t e -> p (t e)")
            pe.wait_ge(s_in, 64)
            pe.wait_ge(s_oh, 1)
            nc.tensor.matmul(bank_r[:], earlier[:], flat, start=True, stop=True).then_inc(s_cnt, 1)
            nc.tensor.matmul(bank_t[:], ones[:], flat, start=True, stop=True).then_inc(s_cnt, 1)

        @block.vector
        def _(dve):
            v = nc.vector
            step = Chain(dve, s_step)
            over_e = lambda a: a.unsqueeze(2).to_broadcast(full)
            over_t = lambda a: a.unsqueeze(1).to_broadcast(full)
            dve.wait_ge(s_in, 64)
            step(v.tensor_reduce(low[:], logits[:], AX.X, ALU.max))
            v.tensor_tensor(work[:], logits[:], over_e(low[:]), ALU.subtract).then_inc(s_sh, 1)
            dve.wait_ge(s_ex, 1)
            step(v.tensor_reduce(tot[:], scores[:], AX.X, ALU.add))
            step(v.reciprocal(tot[:], tot[:]))
            step(v.tensor_tensor(scores[:], scores[:], over_e(tot[:]), ALU.mult))
            for k, pick in ((0, one0), (1, one1)):
                step(v.tensor_reduce(top[:, k, :], scores[:], AX.X, ALU.max))
                step(v.tensor_tensor(work[:], scores[:], over_e(top[:, k, :]), ALU.is_equal))
                step(v.tensor_tensor(work[:], work[:], over_t(eid[:]), ALU.mult))
                step(v.tensor_reduce(low[:], work[:], AX.X, ALU.min))
                step(v.tensor_tensor(pick[:], over_t(eid[:]), over_e(low[:]), ALU.is_equal))
                if k == 0:
                    step(v.scalar_tensor_tensor(scores[:].rearrange("p t e -> p (t e)"), pick[:].rearrange("p t e -> p (t e)"), -2.0,
                                                scores[:].rearrange("p t e -> p (t e)"), ALU.mult, ALU.add))
            v.tensor_tensor(taken[:], one0[:], one1[:], ALU.add).then_inc(s_oh, 1)
            step(v.tensor_tensor(top[:, 2, :], top[:, 0, :], top[:, 1, :], ALU.add))
            step(v.reciprocal(top[:, 2, :], top[:, 2, :]))
            for k in range(2):
                step(v.tensor_tensor(weight[:, k, :], top[:, k, :], top[:, 2, :], ALU.mult))
            dve.wait_ge(s_cnt, 2)
            step(v.tensor_copy(before[:], bank_r[:].rearrange("p (t e) -> p t e", e=E)))
            step(v.tensor_copy(scan_a[:], bank_t[:].rearrange("p (t e) -> p t e", e=E)))
            step(v.tensor_tensor(before[:], before[:], scan_a[:], ALU.subtract))
            src, dst, n = scan_a, scan_b, 1
            while n < TILES:
                step(v.tensor_copy(dst[:, 0:n, :], src[:, 0:n, :]))
                step(v.tensor_tensor(dst[:, n:, :], src[:, n:, :], src[:, :TILES - n, :], ALU.add))
                src, dst, n = dst, src, 2 * n
            step(v.tensor_tensor(before[:], before[:], src[:], ALU.add))
            step(v.tensor_scalar(cnt[:, 0, :], src[:, TILES - 1, :], float(P - 1), None, ALU.add))
            step(v.tensor_copy(cnt_i[:], cnt[:, 0, :]))
            step(v.tensor_scalar(cnt_i[:], cnt_i[:], P.bit_length() - 1, None, ALU.arith_shift_right))
            step(v.tensor_copy(cnt[:, 0, :], cnt_i[:]))
            step(v.tensor_copy(cnt[:, 1, :], cnt[:, 0, :]))
            for e in range(1, E):
                step(v.tensor_tensor(cnt[:, 1, e:e + 1], cnt[:, 1, e:e + 1], cnt[:, 1, e - 1:e], ALU.add))
            step(v.tensor_tensor(cnt[:, 2, :], cnt[:, 1, :], cnt[:, 0, :], ALU.subtract))
            step(v.tensor_scalar(cnt[:, 2, :], cnt[:, 2, :], float(P), None, ALU.mult))
            step(v.tensor_tensor(before[:], before[:], over_t(cnt[:, 2, :]), ALU.add))
            for k, pick in ((0, one0), (1, one1)):
                step(v.tensor_tensor(work[:], before[:], pick[:], ALU.mult))
                step(v.tensor_reduce(low[:], work[:], AX.X, ALU.add))
                step(v.tensor_copy(slot[:, k, :], low[:]))
            step(v.tensor_scalar(te[:], tid[:], cnt[0:1, 1, 0:1], None, ALU.is_ge))
            for e in range(1, E - 1):
                step(v.scalar_tensor_tensor(te[:], tid[:], cnt[0:1, 1, e:e + 1], te[:], ALU.is_ge, ALU.add))
            step(v.tensor_copy(tile_expert[:], te[:]))


def mixer_block(nc, d, w):
    with ExitStack() as ctx:
        def sb(name, shape, dt=F32):
            return ctx.enter_context(nc.sbuf_tensor(name, shape, dt))

        def psum(name):
            return ctx.enter_context(nc.psum_tensor(name, [P, 512], F32))

        def sem(name):
            return ctx.enter_context(nc.semaphore(name))

        x1, slot = w["x1"], w["slot"]
        wtap, wz = sb("wtap", [P, TAPS, CH]), sb("w_in_z", [P, CH])
        cb = sb("conv_b_rows", [P, CH])
        wout = sb("w_outT", [P, CB, D])
        ident = sb("ident_mixer", [P, P])
        xp = [sb(f"x2T_padded{i}", [P, 2 * S + TAPS - 1]) for i in range(2)]
        pre = [sb(f"conv_sum{i}", [P, TPS, CH]) for i in range(2)]
        xs = sb("conv_out", [P, CH, TPS, B])
        zs = sb("gate_z", [P, B, TPS, CH])
        tt = [sb(f"toeplitz{i}", [P, GB, S]) for i in range(2)]
        hrow = [sb(f"route_rows{i}", [P, D]) for i in range(2)]
        idx = [sb(f"route_index{i}", [P, 2], I32) for i in range(2)]
        gg = [sb(f"gated{i}", [P, TPS, CH]) for i in range(2)]
        gT = [sb(f"gatedT{i}", [P, TPS * CB, P]) for i in range(2)]
        bank_x = [psum(f"bank_x{i}") for i in range(2)]
        bank_z = [psum(f"bank_z{i}") for i in range(2)]
        bank_y = [psum(f"bank_y{i}") for i in range(2)]
        bank_t, bank_m = psum("bank_gT"), psum("bank_mix")

        s_in, s_pad = sem("s_mixer_loaded"), sem("s_pad_zero")
        xp_loaded = [sem(f"xp_loaded{i}") for i in range(2)]
        x_done, z_done, pre_ready, xs_ready, z_ready = (sem(n) for n in ("x_done", "z_done", "pre_ready", "xs_ready", "z_ready"))
        t_loaded = [sem(f"toeplitz_loaded{i}") for i in range(2)]
        y_done, y_ready = sem("y_done"), sem("y_ready")
        g_ready, gt_done, gT_ready, mix_done, mix_added = (sem(n) for n in ("g_ready", "gt_done", "gT_ready", "mix_done", "mix_added"))
        row_loaded = [sem(f"route_row_loaded{i}") for i in range(2)]
        idx_ready = sem("route_index_ready")
        row_sent = [sem(f"route_row_sent{i}") for i in range(2)]
        loads = [(wtap[:], d["wtap"]), (wz[:], d["W_inT"][:, CH:2 * CH]), (cb[:], d["conv_b"].partition_broadcast(P)),
                 (wout[:], d["W_outT"]), (ident[:], d["ident"])]
        kp = d["kpad"]
        block = ctx.enter_context(nc.Block())

        def pairwise(eng, count, body):
            body(0, 0)
            body(1, 1)
            with eng.Fori(2, count - 1, 2) as i:
                body(i, 0)
                body(i + 1, 1)

        @block.sync
        def _(sp):
            for dst, src in loads:
                sp.dma_start(dst, src).then_inc(s_in, 16)
            sp.wait_ge(s_pad, 2)

            def load_x(b, par):
                reach(sp, z_done, b - 1)
                sp.dma_start(xp[par][:, 0:2 * S], d["x2T"][bass.ds(b, 1)].rearrange("a p t -> p (a t)")).then_inc(xp_loaded[par], 16)

            pairwise(sp, B, load_x)

            def load_t(g, par):
                reach(sp, y_done, g - 1)
                rows = bass.AP(kp.tensor, g * (GB * (P + S)) + 1, [[1, P], [P + S, GB], [1, S]])
                sp.dma_start(tt[par][:], rows).then_inc(t_loaded[par], 16)

            pairwise(sp, GROUPS, load_t)

        @block.gpsimd
        def _(pool):
            g = nc.gpsimd
            for i in range(2):
                g.memset(xp[i][:, 2 * S:], 0.0).then_inc(s_pad, 1)

            def route(t, par):
                reach(pool, row_sent[par], 16 * (t - par))
                pool.dma_start(hrow[par][:], d["h_rows"].rearrange("b (t p) d -> (b t) p d", p=P)[bass.ds(t, 1)]
                               .rearrange("a p d -> p (a d)")).then_inc(row_loaded[par], 16)
                g.tensor_copy(idx[par][:].unsqueeze(2), slot[:, :, bass.ds(t, 1)]).then_inc(idx_ready, 1)
                wait_apart(pool, (s_pad, 2), (idx_ready, t + 1), (row_loaded[par], 8 * (t - par) + 16))
                for k in range(2):
                    g.indirect_dma_start(d["slot_in"], bass.IndirectOffsetOnAxis(ap=idx[par][:, k:k + 1], axis=0),
                                         hrow[par][:], None).then_inc(row_sent[par], 16)

            pairwise(pool, TILES, route)
            for par in range(2):
                pool.wait_ge(row_sent[par], 16 * TILES)

        @block.tensor
        def _(pe):
            t = nc.tensor
            pe.wait_ge(s_in, 16 * len(loads))

            def project(b, par):
                pe.wait_ge(xp_loaded[par], 8 * (b - par) + 16)
                reach(pe, pre_ready, b - 1)
                for c in range(TPS):
                    for k in range(TAPS):
                        o = S + (TPS - 1 - c) * P + TAPS - 1 - k
                        last = t.matmul(bank_x[par][:, c * CH:(c + 1) * CH], xp[par][:, o:o + P], wtap[:, k, :],
                                        start=(k == 0), stop=(k == TAPS - 1))
                last.then_inc(x_done, 1)
                reach(pe, z_ready, b - 1)
                for c in range(TPS):
                    last = t.matmul(bank_z[par][:, c * CH:(c + 1) * CH], xp[par][:, c * P:(c + 1) * P], wz[:], start=True, stop=True)
                last.then_inc(z_done, 1)

            pairwise(pe, B, project)
            pe.wait_ge(xs_ready, B)

            def convolve(g, par):
                pe.wait_ge(t_loaded[par], 8 * (g - par) + 16)
                reach(pe, y_ready, g - 1)
                for i in range(GB):
                    x = xs[:, bass.ds(g * GB + i, 1), :, :]
                    o = i * TPS * B
                    t.matmul(bank_y[par][:, o:o + TPS * B], tt[par][:, i, 0:P], x.rearrange("p a c b -> p (a c b)"),
                             start=True, stop=False)
                    last = t.matmul(bank_y[par][:, o + B:o + TPS * B], tt[par][:, i, P:S], x[:, :, 0, :].rearrange("p a b -> p (a b)"),
                                    start=False, stop=True)
                last.then_inc(y_done, 1)

            pairwise(pe, GROUPS, convolve)

            def turn(b, par):
                pe.wait_ge(g_ready, b + 1)
                reach(pe, gT_ready, b)
                for c in range(TPS):
                    for k in range(CB):
                        q = c * CB + k
                        last = t.transpose(bank_t[:, q * P:(q + 1) * P], gg[par][:, c, k * P:(k + 1) * P], ident[:])
                last.then_inc(gt_done, 1)
                pe.wait_ge(gT_ready, b + 1)
                reach(pe, mix_added, b)
                for c in range(TPS):
                    for k in range(CB):
                        last = t.matmul(bank_m[:, c * P:(c + 1) * P], gT[par][:, c * CB + k, :], wout[:, k, :],
                                        start=(k == 0), stop=(k == CB - 1))
                last.then_inc(mix_done, 1)

            pairwise(pe, B, turn)

        @block.scalar
        def _(act):
            a = nc.scalar

            def silu(b, par):
                act.wait_ge(pre_ready, b + 1)
                a.activation(xs[:, :, :, bass.ds(b, 1)].rearrange("p h c a -> p c (h a)"), pre[par][:], ACT.Silu).then_inc(xs_ready, 1)
                act.wait_ge(z_done, b + 1)
                a.activation(zs[:, bass.ds(b, 1), :, :].rearrange("p a c h -> p (a c h)"), bank_z[par][:], ACT.Silu).then_inc(z_ready, 1)

            pairwise(act, B, silu)

            def copy_t(b, par):
                act.wait_ge(gt_done, b + 1)
                reach(act, mix_done, b - 1)
                a.activation(gT[par][:].rearrange("p q t -> p (q t)"), bank_t[:], ACT.Copy).then_inc(gT_ready, 1)

            pairwise(act, B, copy_t)

        @block.vector
        def _(dve):
            v = nc.vector
            dve.wait_ge(s_in, 16 * len(loads))

            def bias(b, par):
                dve.wait_ge(x_done, b + 1)
                reach(dve, xs_ready, b - 1)
                v.tensor_tensor(pre[par][:], bank_x[par][:].rearrange("p (c h) -> p c h", c=TPS),
                                cb[:].unsqueeze(1).to_broadcast([P, TPS, CH]), ALU.add).then_inc(pre_ready, 1)

            pairwise(dve, B, bias)

            def copy_y(g, par):
                dve.wait_ge(y_done, g + 1)
                v.tensor_copy(xs[:, bass.ds(g * GB, GB), :, :].rearrange("p h c b -> p (h c b)"), bank_y[par][:]).then_inc(y_ready, 1)

            pairwise(dve, GROUPS, copy_y)
            dve.wait_ge(z_ready, B)
            dve.wait_ge(y_ready, GROUPS)

            def gate(b, par):
                reach(dve, gt_done, b - 1)
                v.tensor_tensor(gg[par][:], xs[:, :, :, bass.ds(b, 1)].rearrange("p h c a -> p c (h a)"),
                                zs[:, bass.ds(b, 1), :, :].rearrange("p a c h -> p (a c) h"), ALU.mult).then_inc(g_ready, 1)
                rows = x1[:, bass.ds(2 * b, 2), :]
                dve.wait_ge(mix_done, b + 1)
                v.tensor_tensor(rows, bank_m[:, 0:S].rearrange("p (t d) -> p t d", t=TPS), rows, ALU.add).then_inc(mix_added, 1)

            pairwise(dve, B, gate)


def experts_block(nc, d, w):
    with ExitStack() as ctx:
        def sb(name, shape, dt=F32):
            return ctx.enter_context(nc.sbuf_tensor(name, shape, dt))

        def psum(name):
            return ctx.enter_context(nc.psum_tensor(name, [P, 512], F32))

        def sem(name):
            return ctx.enter_context(nc.semaphore(name))

        w13 = sb("w13T", [P, E, 2, EI])
        w2 = sb("w2T", [EC, E, ES, D])
        rmsw = sb("rms_w_experts", [P, 1])
        ident = sb("ident_experts", [P, P])
        hrow = [sb(f"slot_rows{i}", [P, D]) for i in range(2)]
        hT = [sb(f"slot_rowsT{i}", [P, P]) for i in range(2)]
        si = [sb(f"silu_a{i}", [P, EI]) for i in range(2)]
        ac = [sb(f"hidden{i}", [P, EI]) for i in range(2)]
        aT = [sb(f"hiddenT{i}", [EC, ES, P]) for i in range(2)]
        orow = [sb(f"slot_result{i}", [P, D]) for i in range(2)]
        bank_a = [psum(f"bank_a{i}") for i in range(2)]
        bank_g = [psum(f"bank_g{i}") for i in range(2)]
        bank_h, bank_t, bank_o = psum("bank_rowsT"), psum("bank_hiddenT"), psum("bank_result")
        s_in, s_w, s_wr = sem("s_experts_const"), sem("s_w13_loaded"), sem("s_w13_ready")
        row_loaded = [sem(f"slot_row_loaded{i}") for i in range(2)]
        stored = [sem(f"slot_result_stored{i}") for i in range(2)]
        ht_done, hT_ready, ag_done, si_ready, ac_ready, at_done, aT_ready, o_done, o_ready = (
            sem(n) for n in ("ht_done", "hT_ready", "ag_done", "si_ready", "ac_ready", "at_done", "aT_ready", "slot_done", "slot_ready"))
        block = ctx.enter_context(nc.Block())
        last_tile = SLOT_TILES - 1

        def pairwise(eng, body):
            body(-1, 1, cur=False, prev=False, nxt=True)
            body(0, 0, cur=True, prev=False, nxt=True)
            body(1, 1, cur=True, prev=True, nxt=True)
            body(2, 0, cur=True, prev=True, nxt=True)
            with eng.Fori(3, last_tile - 1, 2) as m:
                body(m, 1, cur=True, prev=True, nxt=True)
                body(m + 1, 0, cur=True, prev=True, nxt=True)
            body(last_tile, 1, cur=True, prev=True, nxt=False)
            body(last_tile + 1, 0, cur=False, prev=True, nxt=False)

        @block.sync
        def _(sp):
            sp.dma_start(rmsw[:], d["rms_w"]).then_inc(s_in, 16)
            sp.dma_start(ident[:], d["ident"]).then_inc(s_in, 16)
            for k, name in enumerate(("w1T", "w3T")):
                sp.dma_start(w13[:, :, k, :], d[name]).then_inc(s_w, 16)
            sp.dma_start(w2[:], d["w2T"]).then_inc(s_in, 16)

            def body(m, par, cur, prev, nxt):
                nb = 1 - par
                if nxt:
                    reach(sp, ht_done, m)
                    sp.dma_start(hrow[nb][:], d["slot_in"].rearrange("(m p) d -> m p d", p=P)[bass.ds(m + 1, 1)]
                                 .rearrange("a p d -> p (a d)")).then_inc(row_loaded[nb], 16)
                if prev:
                    sp.wait_ge(o_ready, m)
                    sp.dma_start(d["slot_out"].rearrange("(m p) d -> m p d", p=P)[bass.ds(m - 1, 1)]
                                 .rearrange("a p d -> p (a d)"), orow[nb][:]).then_inc(stored[nb], 16)

            pairwise(sp, body)
            for par in range(2):
                sp.wait_ge(stored[par], 8 * SLOT_TILES)

        @block.tensor
        def _(pe):
            t = nc.tensor
            pe.wait_ge(s_in, 48)

            def expert(m):
                index = m if isinstance(m, int) else m
                return pe.value_load(w["tile_expert"][0:1, bass.ds(index, 1)], min_val=0, max_val=E - 1)

            def body(m, par, cur, prev, nxt):
                nb = 1 - par
                if cur:
                    e = expert(m)
                    pe.wait_ge(hT_ready, m + 1)
                    reach(pe, ac_ready, m - 1)
                    if isinstance(m, int) and m == 0:
                        pe.wait_ge(s_wr, E)
                    t.matmul(bank_a[par][:, 0:EI], hT[par][:], w13[:, bass.ds(e, 1), 0, :].rearrange("p a i -> p (a i)"), start=True, stop=True)
                    t.matmul(bank_g[par][:, 0:EI], hT[par][:], w13[:, bass.ds(e, 1), 1, :].rearrange("p a i -> p (a i)"),
                             start=True, stop=True).then_inc(ag_done, 1)
                if nxt:
                    pe.wait_ge(row_loaded[nb], 8 * (m + 1 - nb) + 16)
                    t.transpose(bank_h[:, 0:P], hrow[nb][:], ident[:]).then_inc(ht_done, 1)
                if prev:
                    e = expert(m - 1)
                    pe.wait_ge(ac_ready, m)
                    for k in range(ES):
                        last = t.transpose(bank_t[0:EC, k * P:(k + 1) * P], ac[nb][:, k * EC:(k + 1) * EC], ident[:])
                    last.then_inc(at_done, 1)
                    pe.wait_ge(aT_ready, m)
                    reach(pe, o_ready, m - 1)
                    for k in range(ES):
                        last = t.matmul(bank_o[:, 0:P], aT[nb][:, k, :], w2[:, bass.ds(e, 1), k, :].rearrange("p a n -> p (a n)"),
                                        start=(k == 0), stop=(k == ES - 1))
                    last.then_inc(o_done, 1)

            pairwise(pe, body)

        @block.scalar
        def _(act):
            a = nc.scalar

            def body(m, par, cur, prev, nxt):
                nb = 1 - par
                if cur:
                    act.wait_ge(ag_done, m + 1)
                    reach(act, ac_ready, m - 1)
                    a.activation(si[par][:], bank_a[par][:, 0:EI], ACT.Silu).then_inc(si_ready, 1)
                if nxt:
                    act.wait_ge(ht_done, m + 2)
                    reach(act, ag_done, m)
                    a.activation(hT[nb][:], bank_h[:, 0:P], ACT.Copy).then_inc(hT_ready, 1)
                if prev:
                    act.wait_ge(at_done, m)
                    reach(act, o_done, m - 2)
                    a.activation(aT[nb][:].rearrange("p k t -> p (k t)"), bank_t[0:EC, :], ACT.Copy).then_inc(aT_ready, 1)

            pairwise(act, body)

        @block.vector
        def _(dve):
            v = nc.vector
            dve.wait_ge(s_in, 48)
            dve.wait_ge(s_w, 32)
            for e in range(E):
                we = w13[:, e, :, :].rearrange("p k i -> p (k i)")
                v.tensor_scalar(we, we, rmsw[:, 0:1], None, ALU.mult).then_inc(s_wr, 1)

            def body(m, par, cur, prev, nxt):
                nb = 1 - par
                if prev:
                    dve.wait_ge(o_done, m)
                    reach(dve, stored[nb], 8 * (m - 1 - nb))
                    v.tensor_copy(orow[nb][:], bank_o[:, 0:P]).then_inc(o_ready, 1)
                if cur:
                    dve.wait_ge(si_ready, m + 1)
                    reach(dve, at_done, m - 1)
                    v.tensor_tensor(ac[par][:], bank_g[par][:, 0:EI], si[par][:], ALU.mult).then_inc(ac_ready, 1)

            pairwise(dve, body)


def combine_block(nc, d, w):
    with ExitStack() as ctx:
        def sb(name, shape, dt=F32):
            return ctx.enter_context(nc.sbuf_tensor(name, shape, dt))

        def sem(name):
            return ctx.enter_context(nc.semaphore(name))

        x1, slot, weight = w["x1"], w["slot"], w["weight"]
        minor = sb("combine_start", [P, 1])
        got = [sb(f"gathered{i}", [P, 2, D]) for i in range(2)]
        idx = [sb(f"gather_index{i}", [P, 2], I32) for i in range(2)]
        idx_ready, s_ready = sem("gather_index_ready"), sem("s_combine_ready")
        gathered = [sem(f"gathered_sem{i}") for i in range(2)]
        added0, added1, out_sent = sem("first_added"), sem("second_added"), sem("out_sent")
        block = ctx.enter_context(nc.Block())

        def pairwise(eng, body):
            body(0, 0)
            body(1, 1)
            with eng.Fori(2, TILES - 1, 2) as t:
                body(t, 0)
                body(t + 1, 1)

        @block.gpsimd
        def _(pool):
            g = nc.gpsimd

            def body(t, par):
                reach(pool, added1, t - 1)
                g.tensor_copy(idx[par][:].unsqueeze(2), slot[:, :, bass.ds(t, 1)]).then_inc(idx_ready, 1)
                wait_apart(pool, (s_ready, 1), (idx_ready, t + 1))
                for k in range(2):
                    g.indirect_dma_start(got[par][:, k, :], None, d["slot_out"],
                                         bass.IndirectOffsetOnAxis(ap=idx[par][:, k:k + 1], axis=0)).then_inc(gathered[par], 16)

            g.memset(minor[:], 0.0).then_inc(s_ready, 1)
            pairwise(pool, body)

        @block.vector
        def _(dve):
            v = nc.vector

            def body(t, par):
                dve.wait_ge(gathered[par], 16 * (t - par) + 32)
                row = x1[:, bass.ds(t, 1), :].rearrange("p a d -> p (a d)")
                wt = lambda k: weight[:, k, bass.ds(t, 1)]
                v.scalar_tensor_tensor(row, got[par][:, 0, :], wt(0), row, ALU.mult, ALU.add).then_inc(added0, 1)
                dve.wait_ge(added0, t + 1)
                v.scalar_tensor_tensor(row, got[par][:, 1, :], wt(1), row, ALU.mult, ALU.add).then_inc(added1, 1)

            pairwise(dve, body)

        @block.sync
        def _(sp):
            rows = d["out"].rearrange("b (t p) d -> p (b t) d", p=P)
            for q in range(8):
                a, n = q * TILES // 8, TILES // 8
                sp.wait_ge(added1, a + n)
                sp.dma_start(rows[:, a:a + n, :], x1[:, a:a + n, :]).then_inc(out_sent, 16)
            sp.wait_ge(out_sent, 128)


def build_program(nc, d):
    with ExitStack() as ctx:
        def sb(name, shape, dt=F32):
            return ctx.enter_context(nc.sbuf_tensor(name, shape, dt))

        w = {"x1": sb("x1", [P, TILES, D]), "logits": sb("logits", [P, TILES, E]),
             "slot": sb("slot_of_choice", [P, 2, TILES], I32), "weight": sb("choice_weight", [P, 2, TILES]),
             "tile_expert": sb("tile_expert", [1, SLOT_TILES], I32)}
        with ExitStack() as first:
            w["bw1T"] = first.enter_context(nc.sbuf_tensor("bw1T", [P, HID], F32))
            w["bw2T"] = first.enter_context(nc.sbuf_tensor("bw2T", [P, HID], F32))
            setup_block(nc, d, w)
            layer0_block(nc, d, w)
        routing_block(nc, d, w)
        mixer_block(nc, d, w)
        experts_block(nc, d, w)
        combine_block(nc, d, w)


def shape_constants():
    t = np.arange(S, dtype=np.float64)
    inv = 1.0 / 10000.0 ** (np.arange(0, HD, 2, dtype=np.float64) / HD)
    ang = np.concatenate([np.outer(t, inv)] * 2, axis=-1).T
    cos, sin = np.cos(ang), np.sin(ang)
    sin = np.concatenate([-sin[:HD // 2], sin[HD // 2:]])
    slope = 2.0 ** (-8.0 / NH * (np.arange(NH) + 1))
    lag = t[None, :] - np.arange(P)[:, None]
    m = np.where(lag >= 0, np.exp(-slope[:, None, None] * np.maximum(lag, 0)), 0.0)
    m = np.concatenate([m, m[:, :, :P]], axis=2).transpose(1, 0, 2)
    f = lambda a: np.ascontiguousarray(a, dtype=np.float32)
    return {"rope_q": f(np.concatenate([cos, sin])), "rope_kc": f(np.concatenate([cos, cos])),
            "rope_ks": f(np.concatenate([sin, sin])), "decay": f(m), "ident": np.eye(P, dtype=np.float32),
            "flip": f(np.eye(P)[::-1]),
            "expert_minus": f(np.broadcast_to(np.arange(E) - E, (P, E))), "tile_ids": f(np.arange(SLOT_TILES)[None]),
            "earlier": f(np.triu(np.ones((P, P)), 1)), "ones": np.ones((P, P), np.float32)}


def layout(i):
    g = {k: np.asarray(v) for k, v in i.items()}
    turned = (np.arange(HD) + HD // 2) % HD
    wq = g["L0_attn_Wq"].reshape(NH, HD, D)
    wk = g["L0_attn_Wk"].reshape(NKV, HD, D)
    both = np.concatenate([wq, wq[:, turned]], axis=1)
    kb = np.concatenate([wk.reshape(2, P, D), wk[:, turned].reshape(2, P, D)])
    c = np.ascontiguousarray
    return {
        "x": c(g["L0_attn_x"]), "wq": c(both.transpose(2, 0, 1)), "wk": c(kb.transpose(2, 0, 1)),
        "wv": c(g["L0_attn_Wv"].T), "wo": c(g["L0_attn_Wo"].T.reshape(PAIRS, P, D).transpose(1, 0, 2)),
        "ffn_w1": c(g["L0_ffn_w1"]), "ffn_b1": c(g["L0_ffn_b1"].reshape(HB, P).T), "ffn_w2": c(g["L0_ffn_w2"]), "ffn_b2": c(g["L0_ffn_b2"]),
        "W_inT": c(g["L1_attn_W_in"].T), "conv_wT": c(g["L1_attn_conv_w"].T), "conv_b": c(g["L1_attn_conv_b"]),
        "log_dt": c(g["L1_attn_log_dt"].reshape(CB, P).T), "log_A_real": c(g["L1_attn_log_A_real"]), "A_imag": c(g["L1_attn_A_imag"]),
        "C_re": c(g["L1_attn_C_re"]), "C_im": c(g["L1_attn_C_im"]), "D_skip": c(g["L1_attn_D"].reshape(CB, P).T),
        "W_outT": c(g["L1_attn_W_out"].T.reshape(CB, P, D).transpose(1, 0, 2)),
        "rms_w": c(g["L1_ffn_rms_weight"].reshape(P, 1)), "gateT": c(g["L1_ffn_gate_w"].T),
        "w1T": c(g["L1_ffn_w1"].transpose(2, 0, 1)), "w3T": c(g["L1_ffn_w3"].transpose(2, 0, 1)),
        "w2T": c(g["L1_ffn_w2"].reshape(E, D, ES, EC).transpose(3, 0, 2, 1)),
    }


def kernel(**inputs):
    import concourse.bacc as bacc
    from concourse.bass_utils import run_bass_kernel_spmd

    nc = bacc.Bacc("TRN2", target_bir_lowering=False, num_devices=1)
    arrays = {f"in_{k}": v for k, v in {**layout(inputs), **shape_constants()}.items()}
    d = {k[3:]: nc.dram_tensor(k, v.shape, mybir.dt.from_np(v.dtype), kind="ExternalInput").ap() for k, v in arrays.items()}
    for name, shape in SCRATCH.items():
        d[name] = nc.dram_tensor(f"scratch_{name}", shape, F32, kind="Internal").ap()
    d["out"] = nc.dram_tensor("out_x", (B, S, D), F32, kind="ExternalOutput").ap()
    build_program(nc, d)
    r = run_bass_kernel_spmd(nc, [arrays], core_ids=[0])
    return r.results[0]["out_x"]
```

```python
import math
from contextlib import ExitStack

import concourse.bass as bass
import concourse.mybir as mybir
import numpy as np

F32 = mybir.dt.float32
F32R = mybir.dt.float32r
I32 = mybir.dt.int32
ALU = mybir.AluOpType
ACT = mybir.ActivationFunctionType
AX = mybir.AxisListType

P = 128
B, S, D = 32, 256, 128
TILES = B * S // P
TPS = S // P
NH, NKV, HD = 16, 4, 64
PAIRS = NH // 2
HID = 512
HB = HID // P
CH, NS, TAPS = 256, 8, 4
CB = CH // P
E, EI = 8, 448
EC = 112
ES = EI // EC
SLOT_TILES = 2 * TILES + E
SLOTS = SLOT_TILES * P
SCW = S + P
EPS_LN, EPS_RMS = 1e-5, 1e-6
GB = 8
GROUPS = CH // GB


def reach(eng, semaphore, value):
    if isinstance(value, int) and value <= 0:
        return
    eng.wait_ge(semaphore, value)


def wait_apart(eng, started, *waits):
    counts = [(s, v if isinstance(v, int) else eng.to_reg(v)) for s, v in waits]
    eng.wait_ge(*started)
    for semaphore, value in counts:
        reach(eng, semaphore, value)


class Chain:

    def __init__(self, eng, semaphore):
        self.eng, self.semaphore, self.count = eng, semaphore, 0

    def __call__(self, instruction):
        self.count += 1
        instruction.then_inc(self.semaphore, 1)
        self.eng.wait_ge(self.semaphore, self.count)


def setup_block(nc, d, w):
    with ExitStack() as ctx:
        def sb(name, shape, dt=F32):
            return ctx.enter_context(nc.sbuf_tensor(name, shape, dt))

        def sem(name):
            return ctx.enter_context(nc.semaphore(name))

        w1 = sb("w1_rows", [P, HB, D])
        w2 = sb("w2_rows", [P, HID])
        ta, tb = sb("sign_pos", [P, HID]), sb("sign_neg", [P, HID])
        alpha = sb("alpha", [P, HB + 1])
        bw = sb("bw_rows", [P, 2, HID])
        ident = sb("ident_setup", [P, P])
        poles = w["poles"]
        ld = sb("log_dt_sb", [P, CB])
        lar, aim = sb("log_a_real_sb", [P, CB, NS]), sb("a_imag_sb", [P, CB, NS])
        cre, cim = sb("c_re_sb", [P, CB, NS]), sb("c_im_sb", [P, CB, NS])
        dt = sb("dt_sb", [P, CB])
        s4 = sb("s4_small", [P, 20, CB * NS])
        turns = sb("turns", [P, CB * NS], I32)
        win, cw = sb("win_x", [P, CH]), sb("conv_w_bc", [P, TAPS, CH])
        wtap = sb("wtap_sb", [P, TAPS, CH])
        pt = [ctx.enter_context(nc.psum_tensor(f"bw_turn{i}", [P, HID], F32)) for i in range(2)]

        s_in, s_step = sem("s_setup_loaded"), sem("s_setup_step")
        s_bw, s_turn = sem("s_bw_ready"), sem("s_bw_turned")
        s_exp, s_sinarg, s_sin, s_areal = sem("s_exp"), sem("s_sin_args"), sem("s_sin"), sem("s_a_real")
        s_tap, s_out, s_cp = sem("s_taps_ready"), sem("s_setup_stored"), sem("s_bw_copied")
        loads = [
            (w1[:], d["ffn_w1"].rearrange("(c p) d -> p c d", p=P)), (w2[:], d["ffn_w2"]),
            (ident[:], d["ident"]),
            (ld[:], d["log_dt"]),
            (lar[:], d["log_A_real"].rearrange("(c p) n -> p c n", p=P)),
            (aim[:], d["A_imag"].rearrange("(c p) n -> p c n", p=P)),
            (cre[:], d["C_re"].rearrange("(c p) n -> p c n", p=P)),
            (cim[:], d["C_im"].rearrange("(c p) n -> p c n", p=P)),
            (win[:], d["W_inT"][:, 0:CH]),
            (cw[:], d["conv_wT"].partition_broadcast(P)),
        ]
        block = ctx.enter_context(nc.Block())

        @block.sync
        def _(sp):
            for dst, src in loads:
                sp.dma_start(dst, src).then_inc(s_in, 16)
            sp.wait_ge(s_tap, 1)
            sp.dma_start(d["wtap"], wtap[:]).then_inc(s_out, 16)
            sp.wait_ge(s_out, 16)

        @block.tensor
        def _(pe):
            pe.wait_ge(s_in, 16 * len(loads))
            pe.wait_ge(s_bw, 2)
            for m in range(2):
                for c in range(HB):
                    last = nc.tensor.transpose(pt[m][:, c * P:(c + 1) * P], bw[:, m, c * P:(c + 1) * P], ident[:])
                last.then_inc(s_turn, 1)

        @block.scalar
        def _(act):
            act.wait_ge(s_in, 16 * len(loads))
            nc.scalar.activation(dt[:], ld[:], ACT.Exp).then_inc(s_exp, 1)
            nc.scalar.activation(s4[:, 0, :], lar[:].rearrange("p c n -> p (c n)"), ACT.Exp).then_inc(s_exp, 1)
            act.wait_ge(s_areal, 1)
            nc.scalar.activation(s4[:, 4, :], s4[:, 2, :], ACT.Exp).then_inc(s_exp, 1)
            act.wait_ge(s_sinarg, 1)
            nc.scalar.activation(s4[:, 7, :], s4[:, 5, :], ACT.Sin).then_inc(s_sin, 1)
            nc.scalar.activation(s4[:, 8, :], s4[:, 6, :], ACT.Sin).then_inc(s_sin, 1)
            act.wait_ge(s_turn, 1)
            nc.scalar.activation(w["bw1T"][:], pt[0][:], ACT.Copy).then_inc(s_cp, 1)
            act.wait_ge(s_turn, 2)
            nc.scalar.activation(w["bw2T"][:], pt[1][:], ACT.Copy).then_inc(s_cp, 1)

        @block.vector
        def _(dve):
            v = nc.vector
            step = Chain(dve, s_step)
            dve.wait_ge(s_in, 16 * len(loads))
            rows = w1[:].rearrange("p c d -> p (c d)")
            step(v.scalar_tensor_tensor(ta[:], rows, -1.0, rows, ALU.mult, ALU.max))
            step(v.tensor_reduce(alpha[:, 0:HB], ta[:].rearrange("p (c d) -> p c d", c=HB), AX.X, ALU.add))
            step(v.scalar_tensor_tensor(tb[:], w2[:], -1.0, w2[:], ALU.mult, ALU.max))
            step(v.tensor_reduce(alpha[:, HB:HB + 1], tb[:], AX.X, ALU.add))
            step(v.tensor_scalar(alpha[:, 0:HB], alpha[:, 0:HB], 1.0 / D, None, ALU.mult))
            step(v.tensor_scalar(alpha[:, HB:HB + 1], alpha[:, HB:HB + 1], 1.0 / HID, None, ALU.mult))
            for m, src in ((0, w1[:].rearrange("p c d -> p (c d)")), (1, w2[:])):
                step(v.tensor_scalar(ta[:], src, 0.0, None, ALU.is_gt))
                step(v.tensor_scalar(tb[:], src, 0.0, None, ALU.is_lt))
                step(v.tensor_tensor(ta[:], ta[:], tb[:], ALU.subtract))
                for c in range(HB):
                    a = alpha[:, c:c + 1] if m == 0 else alpha[:, HB:HB + 1]
                    q = slice(c * P, (c + 1) * P)
                    step(v.scalar_tensor_tensor(tb[:, q], ta[:, q], a, src[:, q], ALU.mult, ALU.subtract))
                v.tensor_tensor(bw[:, m, :], tb[:], src, ALU.add).then_inc(s_bw, 1)
                dve.wait_ge(s_bw, m + 1)

            flat = lambda t: t[:].rearrange("p c n -> p (c n)")
            half = lambda i, c: s4[:, i, c * NS:(c + 1) * NS]
            dve.wait_ge(s_exp, 2)
            step(v.tensor_scalar(s4[:, 1, :], s4[:, 0, :], -1.0, None, ALU.mult))
            for c in range(CB):
                step(v.tensor_scalar(half(2, c), half(1, c), dt[:, c:c + 1], None, ALU.mult))
                step(v.tensor_scalar(half(3, c), aim[:, c, :], dt[:, c:c + 1], None, ALU.mult))
            v.tensor_copy(s4[:, 9, :], s4[:, 2, :]).then_inc(s_areal, 1)
            hi, lo = 6.28125, 2 * math.pi - 6.28125
            for out, shift in ((5, 0.0), (6, math.pi / 2)):
                step(v.tensor_scalar(s4[:, 10, :], s4[:, 3, :], 1.0 / (2 * math.pi), shift / (2 * math.pi), ALU.mult, ALU.add))
                step(v.tensor_copy(turns[:], s4[:, 10, :]))
                step(v.tensor_copy(s4[:, 10, :], turns[:]))
                step(v.scalar_tensor_tensor(s4[:, 11, :], s4[:, 10, :], -hi, s4[:, 3, :], ALU.mult, ALU.add))
                step(v.scalar_tensor_tensor(s4[:, 11, :], s4[:, 10, :], -lo, s4[:, 11, :], ALU.mult, ALU.add))
                step(v.tensor_scalar(s4[:, 11, :], s4[:, 11, :], shift, 3.1415925, ALU.add, ALU.min))
                step(v.tensor_scalar(s4[:, out, :], s4[:, 11, :], -3.1415925, None, ALU.max))
            v.tensor_copy(s4[:, 12, :], s4[:, 5, :]).then_inc(s_sinarg, 1)
            dve.wait_ge(s_sin, 2)
            dve.wait_ge(s_exp, 3)
            step(v.tensor_tensor(s4[:, 13, :], s4[:, 4, :], s4[:, 8, :], ALU.mult))
            step(v.tensor_tensor(s4[:, 14, :], s4[:, 4, :], s4[:, 7, :], ALU.mult))
            step(v.tensor_scalar(s4[:, 15, :], s4[:, 13, :], -1.0, None, ALU.add))
            step(v.tensor_tensor(s4[:, 16, :], flat(cre), s4[:, 15, :], ALU.mult))
            step(v.tensor_tensor(s4[:, 17, :], flat(cim), s4[:, 14, :], ALU.mult))
            step(v.tensor_tensor(s4[:, 16, :], s4[:, 16, :], s4[:, 17, :], ALU.subtract))
            step(v.tensor_tensor(s4[:, 17, :], flat(cre), s4[:, 14, :], ALU.mult))
            step(v.tensor_tensor(s4[:, 18, :], flat(cim), s4[:, 15, :], ALU.mult))
            step(v.tensor_tensor(s4[:, 17, :], s4[:, 17, :], s4[:, 18, :], ALU.add))
            step(v.tensor_tensor(s4[:, 18, :], s4[:, 1, :], s4[:, 1, :], ALU.mult))
            step(v.tensor_tensor(s4[:, 19, :], flat(aim), flat(aim), ALU.mult))
            step(v.tensor_tensor(s4[:, 18, :], s4[:, 18, :], s4[:, 19, :], ALU.add))
            step(v.reciprocal(s4[:, 19, :], s4[:, 18, :]))
            step(v.tensor_scalar(s4[:, 19, :], s4[:, 19, :], 2.0, None, ALU.mult))
            step(v.tensor_tensor(s4[:, 10, :], s4[:, 16, :], s4[:, 1, :], ALU.mult))
            step(v.tensor_tensor(s4[:, 11, :], s4[:, 17, :], flat(aim), ALU.mult))
            step(v.tensor_tensor(s4[:, 10, :], s4[:, 10, :], s4[:, 11, :], ALU.add))
            step(v.tensor_tensor(poles[:, 2, :], s4[:, 10, :], s4[:, 19, :], ALU.mult))
            step(v.tensor_tensor(s4[:, 10, :], s4[:, 17, :], s4[:, 1, :], ALU.mult))
            step(v.tensor_tensor(s4[:, 11, :], s4[:, 16, :], flat(aim), ALU.mult))
            step(v.tensor_tensor(s4[:, 10, :], s4[:, 10, :], s4[:, 11, :], ALU.subtract))
            step(v.tensor_tensor(poles[:, 3, :], s4[:, 10, :], s4[:, 19, :], ALU.mult))
            step(v.tensor_copy(poles[:, 0, :], s4[:, 13, :]))
            step(v.tensor_copy(poles[:, 1, :], s4[:, 14, :]))
            for t in range(TAPS):
                last = v.tensor_tensor(wtap[:, t, :], win[:], cw[:, t, :], ALU.mult)
            last.then_inc(s_tap, 1)


def layer0_block(nc, d, w):
    with ExitStack() as ctx:
        def sb(name, shape, dt=F32):
            return ctx.enter_context(nc.sbuf_tensor(name, shape, dt))

        def psum(name, shape=(P, 512)):
            return ctx.enter_context(nc.psum_tensor(name, list(shape), F32))

        def sem(name):
            return ctx.enter_context(nc.semaphore(name))

        x1, logits = w["x1"], w["logits"]
        wq, wk, wv = sb("wq_stack", [P, NH, P]), sb("wk_stack", [P, 4, P]), sb("wvT", [P, NKV * HD])
        wo = sb("woT", [P, PAIRS, D])
        rope_q = sb("rope_q", [P, S])
        rope_kc, rope_ks = sb("rope_k_cos", [P, S]), sb("rope_k_sin", [P, S])
        decay = sb("decay", [P, NH, SCW])
        b1, b2 = sb("b1_cols", [P, HB]), sb("b2_rows", [P, D])
        gate = sb("gateT", [P, E])
        rmsw = sb("rms_w", [P, 1])
        ident = sb("ident", [P, P])
        mhalf = sb("minus_half", [P, TPS])
        zero = sb("zero_rows", [P, 8, D])
        xn, xn2 = sb("xn", [P, TPS, D]), sb("xn2", [P, TPS, D])
        sq = sb("squares", [P, TPS, D])
        st, mv = sb("ln_stats", [P, 2, TPS, 6]), sb("ln_mean_var", [P, 2, TPS, 2])
        ve, rstd = sb("ln_var_eps", [P, 3, TPS]), sb("ln_rstd", [P, 3, TPS])
        ss = sb("square_sums", [P, TPS])
        xnT = [sb(f"xnT{i}", [P, S]) for i in range(2)]
        flip = sb("flip", [P, P])
        x2T = [sb(f"x2T{i}", [P, 2 * S]) for i in range(2)]
        hh = [sb(f"h_rows{i}", [P, TPS, D]) for i in range(2)]
        kc, ks = sb("k_cos", [P, 2, S]), sb("k_sin", [P, 2, S])
        kk = [sb(f"k_twice{i}", [P, NKV, S]) for i in range(2)]
        vv = [sb(f"v_rows{i}", [P, TPS, NKV * HD]) for i in range(2)]
        gh = [sb(f"gelu_h{i}", [P, HB, S]) for i in range(2)]
        oT = [sb(f"attn_outT{i}", [P, PAIRS, S]) for i in range(2)]
        qs = [sb(f"q_stack{i}", [P, 2, S]) for i in range(2)]
        pp = [sb(f"probs{i}", [P, 2, SCW]) for i in range(2)]

        bank_q = psum("bank_q")
        bank_s = [psum(f"bank_s{i}") for i in range(2)]
        bank_av = [psum(f"bank_av{i}") for i in range(2)]
        m0, m1, bank_o = psum("bank_m0"), psum("bank_m1"), psum("bank_out")

        s_w, s_x = sem("s_weights"), sem("s_x_loaded")
        s_zero, s_zeroed = sem("s_zero_ready"), sem("s_slots_zeroed")
        s_c, s_gate = sem("s_exponent_ready"), sem("s_gate_ready")
        q_done, qs_ready = sem("q_done"), sem("qs_ready")
        s_done, mask_ready = sem("s_done"), sem("mask_ready")
        av_done, ot_ready = sem("av_done"), sem("ot_ready")
        f_done, gh_ready = sem("f_done"), sem("gh_ready")
        o_done = sem("o_done")
        t_done, xnT_ready = sem("t_done"), sem("xnT_ready")
        k_done, kc_done, kk_ready = sem("k_done"), sem("kc_done"), sem("kk_ready")
        vp_done, v_ready = sem("vp_done"), sem("v_ready")
        t2_done, x2T_ready = sem("t2_done"), sem("x2T_ready")
        lg_done, lg_ready = sem("lg_done"), sem("lg_ready")
        st1, agg1, ve1, rs1, xn_ready = sem("st1"), sem("agg1"), sem("ve1"), sem("rstd1_ready"), sem("xn_ready")
        xres_ready = sem("xres_ready")
        x1a, x1_ready = sem("x1_sum"), sem("x1_ready")
        st2, agg2, ve2, rs2, xn2_ready = sem("st2"), sem("agg2"), sem("ve2"), sem("rstd2_ready"), sem("xn2_ready")
        ss_ready, ve3, r_ready, hh_ready = sem("ss_ready"), sem("ve3"), sem("r_ready"), sem("hh_ready")
        x2T_stored, hh_stored = ([sem(f"{n}_stored{i}") for i in range(2)] for n in ("x2T", "hh"))

        loads = [(wq[:], d["wq"]), (wk[:], d["wk"]), (wv[:], d["wv"]), (wo[:], d["wo"]),
                 (rope_q[:], d["rope_q"]), (rope_kc[:], d["rope_kc"]), (rope_ks[:], d["rope_ks"]),
                 (decay[:], d["decay"]), (b1[:], d["ffn_b1"]),
                 (b2[:], d["ffn_b2"].partition_broadcast(P)),
                 (gate[:], d["gateT"]), (rmsw[:], d["rms_w"]),
                 (ident[:], d["ident"]), (flip[:], d["flip"])]
        block = ctx.enter_context(nc.Block())

        def iterations(eng, body):
            body(-1, 1, cur=False, prev=False, nxt=True)
            body(0, 0, cur=True, prev=False, nxt=True)
            body(1, 1, cur=True, prev=True, nxt=True)
            body(2, 0, cur=True, prev=True, nxt=True)
            with eng.Fori(3, B - 2, 2) as b:
                body(b, 1, cur=True, prev=True, nxt=True)
                body(b + 1, 0, cur=True, prev=True, nxt=True)
            body(B - 1, 1, cur=True, prev=True, nxt=False)
            body(B, 0, cur=False, prev=True, nxt=False)

        @block.sync
        def _(sp):
            xr = d["x"].rearrange("b (t p) d -> p (b t) d", p=P)
            for q in range(8):
                a = q * TILES // 8
                sp.dma_start(x1[:, a:a + TILES // 8, :], xr[:, a:a + TILES // 8, :]).then_inc(s_x, 16)
                if q == 0:
                    for dst, src in loads:
                        sp.dma_start(dst, src).then_inc(s_w, 16)

            sp.wait_ge(s_zero, 1)
            rows = d["slot_in"].rearrange("(g j p) d -> g p j d", p=P, j=8)
            for g in range(SLOT_TILES // 8):
                sp.dma_start(rows[g], zero[:]).then_inc(s_zeroed, 16)

            def body(b, par, cur, prev, nxt):
                if not prev:
                    return
                sp.wait_ge(x2T_ready, b)
                sp.dma_start(d["x2T"][bass.ds(b - 1, 1)].rearrange("a p t -> p (a t)"), x2T[1 - par][:]).then_inc(x2T_stored[1 - par], 16)
                sp.wait_ge(hh_ready, b)
                sp.dma_start(d["h_rows"][bass.ds(b - 1, 1)].rearrange("a (t p) d -> p (a t) d", p=P),
                             hh[1 - par][:]).then_inc(hh_stored[1 - par], 16)

            iterations(sp, body)
            sp.wait_ge(s_zeroed, 16 * (SLOT_TILES // 8))
            for stored in x2T_stored + hh_stored:
                sp.wait_ge(stored, 16 * (B // 2))

        @block.gpsimd
        def _(pool):
            g = nc.gpsimd
            g.memset(mhalf[:], -0.5).then_inc(s_c, 1)
            g.memset(zero[:], 0.0).then_inc(s_zero, 1)
            pool.wait_ge(s_c, 1)
            pool.wait_ge(s_w, 16 * len(loads))

            def rsqrt(n, src, add, counted, value, ready):
                if n < 2:
                    g.tensor_scalar(ve[:, n, :], src, add, None, ALU.add).then_inc(counted, 1)
                else:
                    g.tensor_scalar(ve[:, n, :], src, 1.0 / D, add, ALU.mult, ALU.add).then_inc(counted, 1)
                pool.wait_ge(counted, value)
                g.tensor_tensor(rstd[:, n, :], ve[:, n, :], mhalf[:], ALU.pow).then_inc(ready, 1)

            def body(b, par, cur, prev, nxt):
                if nxt:
                    wait_apart(pool, (s_c, 1), (agg1, b + 2), (xn_ready, b + 1))
                    rsqrt(0, mv[:, 0, :, 1], EPS_LN, ve1, b + 2, rs1)
                if prev:
                    wait_apart(pool, (s_c, 1), (agg2, b), (xn2_ready, b - 1))
                    rsqrt(1, mv[:, 1, :, 1], EPS_LN, ve2, b, rs2)
                    wait_apart(pool, (s_c, 1), (ss_ready, b), (hh_ready, b - 1), (lg_ready, b - 1))
                    rsqrt(2, ss[:], EPS_RMS, ve3, b, r_ready)

            iterations(pool, body)

        @block.tensor
        def _(pe):
            t = nc.tensor
            pe.wait_ge(s_w, 16 * len(loads))
            pe.wait_ge(s_gate, 1)

            def body(b, par, cur, prev, nxt):
                nb = 1 - par
                for j in range(PAIRS):
                    n = b * PAIRS + j
                    if cur:
                        if j == 0:
                            pe.wait_ge(kk_ready, b + 1)
                        pe.wait_ge(qs_ready, n + 1)
                        reach(pe, mask_ready, 2 * n)
                        for h in range(2):
                            g = (2 * j + h) // (NH // NKV)
                            t.matmul(bank_s[h][:, 0:S], kk[par][:, g, 0:P], qs[j % 2][:, h, :], start=True, stop=True)
                            t.matmul(bank_s[h][:, S:SCW], kk[par][:, g, P:S], qs[j % 2][:, h, P:S],
                                     start=True, stop=True).then_inc(s_done, 1)
                    if (cur and j < PAIRS - 1) or (nxt and j == PAIRS - 1):
                        src, nj = (xnT[par], j + 1) if j < PAIRS - 1 else (xnT[nb], 0)
                        if j == PAIRS - 1:
                            pe.wait_ge(xnT_ready, b + 2)
                        for h in range(2):
                            last = t.matmul(bank_q[:, h * S:(h + 1) * S], wq[:, 2 * nj + h, :], src[:], start=True, stop=True)
                        last.then_inc(q_done, 1)
                    if (cur and j > 0) or (prev and j == 0):
                        pj, vb, vseq = (j - 1, vv[par], b) if j else (PAIRS - 1, vv[nb], b - 1)
                        reach(pe, mask_ready, 2 * n)
                        reach(pe, ot_ready, n - 2)
                        if j < 2:
                            pe.wait_ge(v_ready, vseq + 1)
                        bank = bank_av[(j + 1) % 2]
                        for c in range(TPS):
                            for h in range(2):
                                g = (2 * pj + h) // (NH // NKV)
                                cols = slice(0, S) if c == 0 else slice(P, S)
                                rhs = pp[pj % 2][:, h, 0:S] if c == 0 else pp[pj % 2][:, h, S:SCW]
                                last = t.matmul(bank[h * HD:(h + 1) * HD, cols], vb[:, c, g * HD:(g + 1) * HD], rhs,
                                                start=(c == 0), stop=(c == 1), skip_group_check=True)
                        last.then_inc(av_done, 1)
                    if j in (0, 1) and cur:
                        if j == 0:
                            pe.wait_ge(v_ready, b + 1)
                        else:
                            reach(pe, lg_ready, b - 1)
                        for c in range(2):
                            last = t.matmul((m0, m1)[j][:, c * S:(c + 1) * S], w["bw1T"][:, (2 * j + c) * P:(2 * j + c + 1) * P],
                                            xnT[par][:], start=True, stop=True)
                        last.then_inc(f_done, 1)
                    if j == 2 and prev:
                        pe.wait_ge(ot_ready, PAIRS * b)
                        pe.wait_ge(gh_ready, 2 * b)
                        reach(pe, x1a, b - 1)
                        for c in range(TPS):
                            q = slice(c * P, (c + 1) * P)
                            for k in range(PAIRS):
                                t.matmul(bank_o[:, q], oT[nb][:, k, q], wo[:, k, :], start=(k == 0), stop=False)
                            for k in range(HB):
                                last = t.matmul(bank_o[:, q], gh[nb][:, k, q], w["bw2T"][:, k * P:(k + 1) * P],
                                                start=False, stop=(k == HB - 1))
                        last.then_inc(o_done, 1)
                    if j == 3 and nxt:
                        pe.wait_ge(xn_ready, b + 2)
                        reach(pe, gh_ready, 2 * b + 2)
                        for c in range(TPS):
                            last = t.transpose(m0[:, c * P:(c + 1) * P], xn[:, c, :], ident[:])
                        last.then_inc(t_done, 1)
                    if j == 4 and nxt:
                        pe.wait_ge(xnT_ready, b + 2)
                        for c in range(4):
                            last = t.matmul((m0, m1)[c // 2][:, (c % 2) * S:(c % 2 + 1) * S], wk[:, c, :], xnT[nb][:],
                                            start=True, stop=True)
                        last.then_inc(k_done, 1)
                    if j == 5 and nxt:
                        pe.wait_ge(kc_done, b + 2)
                        for c in range(TPS):
                            last = t.matmul(m0[:, c * S:(c + 1) * S], xnT[nb][:, c * P:(c + 1) * P], wv[:], start=True, stop=True)
                        last.then_inc(vp_done, 1)
                    if j == 6 and prev:
                        pe.wait_ge(xn2_ready, b)
                        if not nxt:
                            reach(pe, gh_ready, 2 * B)
                        for c in range(TPS):
                            t.transpose(m1[:, c * P:(c + 1) * P], xn2[:, c, :], ident[:])
                            back = S + (TPS - 1 - c) * P
                            last = t.transpose(m1[:, back:back + P], xn2[:, c, :], flip[:])
                        last.then_inc(t2_done, 1)
                    if j == 7 and prev:
                        pe.wait_ge(x2T_ready, b)
                        for c in range(TPS):
                            last = t.matmul(m1[:, c * E:(c + 1) * E], x2T[nb][:, c * P:(c + 1) * P], gate[:], start=True, stop=True)
                        last.then_inc(lg_done, 1)

            iterations(pe, body)

        @block.scalar
        def _(act):
            a = nc.scalar
            act.wait_ge(s_w, 16 * len(loads))

            def body(b, par, cur, prev, nxt):
                nb = 1 - par
                for j in range(PAIRS):
                    n = b * PAIRS + j
                    if (cur and j > 0) or (prev and j == 0):
                        pj, dst = (j - 1, oT[par]) if j else (PAIRS - 1, oT[nb])
                        act.wait_ge(av_done, n)
                        if j == 1:
                            reach(act, o_done, b - 1)
                        a.activation(dst[:, pj, :], bank_av[(j + 1) % 2][:, 0:S], ACT.Copy).then_inc(ot_ready, 1)
                    if j in (0, 1) and cur:
                        act.wait_ge(f_done, 2 * b + j + 1)
                        reach(act, o_done, b - 1)
                        for c in range(2):
                            k = 2 * j + c
                            last = a.activation(gh[par][:, k, :], (m0, m1)[j][:, c * S:(c + 1) * S], ACT.Gelu, bias=b1[:, k:k + 1])
                        last.then_inc(gh_ready, 1)
                    if j == 3 and nxt:
                        act.wait_ge(t_done, b + 2)
                        a.activation(xnT[nb][:], m0[:, 0:S], ACT.Copy).then_inc(xnT_ready, 1)
                    if j == 5 and nxt:
                        act.wait_ge(vp_done, b + 2)
                        a.activation(vv[nb][:].rearrange("p t n -> p (t n)"), m0[:], ACT.Copy).then_inc(v_ready, 1)
                    if j == 6 and prev:
                        act.wait_ge(t2_done, b)
                        reach(act, lg_done, b - 2)
                        reach(act, x2T_stored[nb], 8 * (b - 1 - nb))
                        a.activation(x2T[nb][:], m1[:], ACT.Copy).then_inc(x2T_ready, 1)
                        reach(act, r_ready, b - 1)
                        reach(act, ss_ready, b - 1)
                        for c in range(TPS):
                            last = a.activation(sq[:, c, :], xn2[:, c, :], ACT.Square, accum_out=ss[:, c:c + 1])
                        last.then_inc(ss_ready, 1)

            iterations(act, body)

        @block.vector
        def _(dve):
            v = nc.vector
            dve.wait_ge(s_w, 16 * len(loads))
            v.tensor_scalar(gate[:], gate[:], rmsw[:, 0:1], None, ALU.mult).then_inc(s_gate, 1)

            def body(b, par, cur, prev, nxt):
                nb = 1 - par
                for j in range(PAIRS):
                    n = b * PAIRS + j
                    if cur:
                        for h in range(2):
                            dve.wait_ge(s_done, 2 * n + h + 1)
                            if h == 0:
                                reach(dve, av_done, n - 1)
                            v.tensor_tensor(pp[j % 2][:, h, :], bank_s[h][:, 0:SCW], decay[:, 2 * j + h, :],
                                            ALU.mult).then_inc(mask_ready, 1)
                    if (cur and j < PAIRS - 1) or (nxt and j == PAIRS - 1):
                        dve.wait_ge(q_done, n + 2)
                        v.tensor_tensor(qs[(j + 1) % 2][:], bank_q[:].rearrange("p (h t) -> p h t", h=2),
                                        rope_q[:].unsqueeze(1).to_broadcast([P, 2, S]), ALU.mult).then_inc(qs_ready, 1)
                    if j == 0 and nxt:
                        wait_apart(dve, (s_x, 128), (rs1, b + 1), (agg1, b + 1))
                        for c in range(TPS):
                            last = v.bn_stats(st[:, 0, c, :], x1[:, bass.ds(2 * b + 2 + c, 1), :].rearrange("p a d -> p (a d)"))
                        last.then_inc(st1, 1)
                        wait_apart(dve, (s_x, 128), (st1, b + 2), (xn_ready, b + 1))
                        for c in range(TPS):
                            last = v.bn_aggr(mv[:, 0, c, :], st[:, 0, c, :])
                        last.then_inc(agg1, 1)
                    if j == 2 and nxt:
                        dve.wait_ge(rs1, b + 2)
                        reach(dve, t_done, b + 1)
                        for c in range(TPS):
                            last = v.tensor_scalar(xn[:, c, :], x1[:, bass.ds(2 * b + 2 + c, 1), :].rearrange("p a d -> p (a d)"),
                                                   mv[:, 0, c, 0:1], rstd[:, 0, c:c + 1], ALU.subtract, ALU.mult)
                        last.then_inc(xn_ready, 1)
                    if j == 3 and prev:
                        rows = x1[:, bass.ds(2 * b - 2, 2), :]
                        dve.wait_ge(o_done, b)
                        v.tensor_tensor(rows, bank_o[:, 0:S].rearrange("p (t d) -> p t d", t=TPS), rows, ALU.add).then_inc(x1a, 1)
                        dve.wait_ge(x1a, b)
                        v.tensor_tensor(rows, rows, b2[:].unsqueeze(1).to_broadcast([P, TPS, D]), ALU.add).then_inc(x1_ready, 1)
                        wait_apart(dve, (s_x, 128), (x1_ready, b), (agg2, b - 1))
                        for c in range(TPS):
                            last = v.bn_stats(st[:, 1, c, :], x1[:, bass.ds(2 * b - 2 + c, 1), :].rearrange("p a d -> p (a d)"))
                        last.then_inc(st2, 1)
                        wait_apart(dve, (s_x, 128), (st2, b), (xn2_ready, b - 1), (rs2, b - 1))
                        for c in range(TPS):
                            last = v.bn_aggr(mv[:, 1, c, :], st[:, 1, c, :])
                        last.then_inc(agg2, 1)
                    if j == 4 and nxt:
                        dve.wait_ge(k_done, b + 2)
                        reach(dve, kk_ready, b + 1)
                        bc = lambda r: r[:].unsqueeze(1).to_broadcast([P, 2, S])
                        v.tensor_tensor(kc[:], m0[:].rearrange("p (u t) -> p u t", u=2), bc(rope_kc), ALU.mult)
                        v.tensor_tensor(ks[:], m1[:].rearrange("p (u t) -> p u t", u=2), bc(rope_ks), ALU.mult).then_inc(kc_done, 1)
                        dve.wait_ge(kc_done, b + 2)
                        for g in range(NKV):
                            r = slice((g % 2) * HD, (g % 2 + 1) * HD)
                            for half in range(2):
                                last = v.tensor_tensor(kk[nb][half * HD:(half + 1) * HD, g, :], kc[r, g // 2, :], ks[r, g // 2, :], ALU.add)
                        last.then_inc(kk_ready, 1)
                    if j == 5 and prev:
                        dve.wait_ge(rs2, b)
                        reach(dve, t2_done, b - 1)
                        reach(dve, hh_ready, b - 1)
                        reach(dve, xres_ready, b - 1)
                        reach(dve, ss_ready, b - 1)
                        for c in range(TPS):
                            last = v.tensor_scalar(xn2[:, c, :], x1[:, bass.ds(2 * b - 2 + c, 1), :].rearrange("p a d -> p (a d)"),
                                                   mv[:, 1, c, 0:1], rstd[:, 1, c:c + 1], ALU.subtract, ALU.mult)
                        last.then_inc(xn2_ready, 1)
                    if j == 7 and prev:
                        rows = x1[:, bass.ds(2 * b - 2, 2), :]
                        dve.wait_ge(xn2_ready, b)
                        v.tensor_tensor(rows, rows, xn2[:], ALU.add).then_inc(xres_ready, 1)
                        dve.wait_ge(r_ready, b)
                        reach(dve, hh_stored[nb], 8 * (b - 1 - nb))
                        for c in range(TPS):
                            last = v.tensor_scalar(hh[nb][:, c, :], xn2[:, c, :], rstd[:, 2, c:c + 1], None, ALU.mult)
                        last.then_inc(hh_ready, 1)
                        dve.wait_ge(lg_done, b)
                        for c in range(TPS):
                            last = v.tensor_scalar(logits[:, bass.ds(2 * b - 2 + c, 1), :].rearrange("p a e -> p (a e)"),
                                                   m1[:, c * E:(c + 1) * E], rstd[:, 2, c:c + 1], None, ALU.mult)
                        last.then_inc(lg_ready, 1)

            iterations(dve, body)


SCRATCH = {"slot_in": (SLOTS, D), "slot_out": (SLOTS, D), "kpad": (CH, P + S), "wtap": (P, TAPS, CH),
           "x2T": (B, P, 2 * S), "h_rows": (B, S, D)}


def in_turns(eng, count, ring, body):
    for i in range(ring):
        body(i, i)
    with eng.Fori(ring, count - ring + 1, ring) as i:
        for turn in range(ring):
            body(i + turn, turn)


def pairwise(eng, count, body):
    in_turns(eng, count, 2, body)


def route_and_convolve_block(nc, d, w):
    with ExitStack() as ctx:
        def sb(name, shape, dt=F32):
            return ctx.enter_context(nc.sbuf_tensor(name, shape, dt))

        def psum(name):
            return ctx.enter_context(nc.psum_tensor(name, [P, 512], F32))

        def sem(name):
            return ctx.enter_context(nc.semaphore(name))

        logits, slot, weight, tile_expert = w["logits"], w["slot"], w["weight"], w["tile_expert"]
        xs, w13h, w13l = w["xs"], w["w13h"], w["w13l"]
        full = [P, TILES, E]
        earlier, ones = sb("earlier_sb", [P, P]), sb("ones_sb", [P, P])
        eid, tid = sb("expert_minus", [P, E]), sb("tile_ids", [1, SLOT_TILES])
        scores, work, one0, one1, taken = (sb(n, full) for n in ("scores", "work", "is_first", "is_second", "is_taken"))
        scan_a, scan_b, before = scores, taken, sb("rank_before", full)
        top, low, tot = sb("top", [P, 3, TILES]), sb("low", [P, TILES]), sb("total", [P, TILES])
        cnt, cnt_i = sb("tiles_of", [P, 4, E]), sb("tiles_of_int", [P, E], I32)
        te = sb("tile_expert_f", [1, SLOT_TILES])
        bank_r, bank_t = psum("bank_rank"), psum("bank_total")
        wtap = sb("wtap", [P, TAPS, CH])
        cb = sb("conv_b_row", [1, CH])
        xp = [sb(f"x2T_back{i}", [P, S + TAPS - 1]) for i in range(2)]
        bank_x = [psum(f"bank_x{i}") for i in range(2)]
        hrow = [sb(f"route_rows{i}", [P, TPS, D]) for i in range(2)]
        idx = [sb(f"route_index{i}", [P, 2, TPS], I32) for i in range(2)]
        rmsw = sb("rms_w_experts", [P, 1])
        raw = [sb(f"w13_raw{i}", [P, 2, EI]) for i in range(2)]

        s_in, s_step = sem("s_route_loaded"), sem("s_route_step")
        s_sh, s_ex, s_oh, s_cnt = sem("s_shifted"), sem("s_exps"), sem("s_onehots"), sem("s_counts")
        s_slots, s_pad = sem("s_slots_ready"), sem("s_pad_zero")
        s_conv, s_w2 = sem("s_conv_loaded"), sem("s_w2_loaded")
        raw_loaded = [sem(f"w13_raw_loaded{i}") for i in range(2)]
        raw_scaled, high_ready, low_ready = sem("w13_scaled"), sem("w13_high_ready"), sem("w13_low_ready")
        xp_loaded = [sem(f"xp_loaded{i}") for i in range(2)]
        x_done, xs_ready = sem("x_done"), sem("xs_ready")
        row_loaded = [sem(f"route_row_loaded{i}") for i in range(2)]
        idx_ready = sem("route_index_ready")
        row_sent = [sem(f"route_row_sent{i}") for i in range(2)]
        consts = [(earlier[:], d["earlier"]), (ones[:], d["ones"]), (eid[:], d["expert_minus"]), (tid[:], d["tile_ids"]),
                  (rmsw[:], d["rms_w"])]
        conv = [(wtap[:], d["wtap"]), (cb[:], d["conv_b"].rearrange("(a n) -> a n", a=1))]
        block = ctx.enter_context(nc.Block())

        @block.sync
        def _(sp):
            for dst, src in consts:
                sp.dma_start(dst, src).then_inc(s_in, 16)
            for dst, src in conv:
                sp.dma_start(dst, src).then_inc(s_conv, 16)

            def load(b, par):
                reach(sp, x_done, b - 1)
                sp.dma_start(xp[par][:, 0:S], d["x2T"][bass.ds(b, 1), :, S:2 * S].rearrange("a p t -> p (a t)")).then_inc(xp_loaded[par], 16)
                reach(sp, row_sent[par], 32 * (b - par))
                sp.dma_start(hrow[par][:], d["h_rows"][bass.ds(b, 1)].rearrange("a (t p) d -> p (a t) d", p=P)).then_inc(row_loaded[par], 16)

            pairwise(sp, B, load)

        @block.gpsimd
        def _(pool):
            g = nc.gpsimd
            for i in range(2):
                g.memset(xp[i][:, S:], 0.0).then_inc(s_pad, 1)
            pool.wait_ge(s_slots, 2)

            def route(b, par):
                reach(pool, row_sent[par], 32 * (b - par))
                g.tensor_copy(idx[par][:], slot[:, :, bass.ds(2 * b, 2)]).then_inc(idx_ready, 1)
                wait_apart(pool, (s_pad, 2), (idx_ready, b + 1), (row_loaded[par], 8 * (b - par) + 16))
                for k in range(2):
                    for t in range(TPS):
                        g.indirect_dma_start(d["slot_in"], bass.IndirectOffsetOnAxis(ap=idx[par][:, k, t:t + 1], axis=0),
                                             hrow[par][:, t, :], None).then_inc(row_sent[par], 16)

            pairwise(pool, B, route)
            for par in range(2):
                pool.wait_ge(row_sent[par], 32 * B)

        @block.tensor
        def _(pe):
            t = nc.tensor
            pe.wait_ge(s_in, 16 * len(consts))
            pe.wait_ge(s_conv, 16 * len(conv))
            pe.wait_ge(s_pad, 2)

            def project(b, par):
                pe.wait_ge(xp_loaded[par], 8 * (b - par) + 16)
                reach(pe, xs_ready, b - 1)
                for c in range(TPS):
                    q = slice(c * CH, (c + 1) * CH)
                    for k in range(TAPS):
                        o = (TPS - 1 - c) * P + TAPS - 1 - k
                        t.matmul(bank_x[par][:, q], xp[par][:, o:o + P], wtap[:, k, :], start=(k == 0), stop=False)
                    last = t.matmul(bank_x[par][:, q], ones[0:1, :], cb[:], start=False, stop=True)
                last.then_inc(x_done, 1)

            project(0, 0)
            project(1, 1)
            flat = taken[:].rearrange("p t e -> p (t e)")
            pe.wait_ge(s_oh, 1)
            t.matmul(bank_r[:], earlier[:], flat, start=True, stop=True).then_inc(s_cnt, 1)
            t.matmul(bank_t[:], ones[:], flat, start=True, stop=True).then_inc(s_cnt, 1)
            with pe.Fori(2, B - 1, 2) as b:
                project(b, 0)
                project(b + 1, 1)

        @block.scalar
        def _(act):
            act.dma_start(w["w2"][:], d["w2T"]).then_inc(s_w2, 16)
            for e in range(E):
                if e >= 2:
                    act.wait_ge(low_ready, e - 1)
                for k, name in enumerate(("w1T", "w3T")):
                    act.dma_start(raw[e % 2][:, k, :], d[name][:, e, :]).then_inc(raw_loaded[e % 2], 16)
                if e == 1:
                    act.wait_ge(s_sh, 1)
                    nc.scalar.activation(scores[:], work[:], ACT.Exp).then_inc(s_ex, 1)

                    def silu(b, par):
                        act.wait_ge(x_done, b + 1)
                        nc.scalar.activation(xs[:, :, :, bass.ds(b, 1)].rearrange("p h c a -> p c (h a)"),
                                             bank_x[par][:].rearrange("p (c h) -> p c h", c=TPS), ACT.Silu).then_inc(xs_ready, 1)

                    pairwise(act, B, silu)
            act.wait_ge(s_w2, 16)

        @block.vector
        def _(dve):
            v = nc.vector
            step = Chain(dve, s_step)
            over_e = lambda a: a.unsqueeze(2).to_broadcast(full)
            over_t = lambda a: a.unsqueeze(1).to_broadcast(full)
            dve.wait_ge(s_in, 16 * len(consts))
            step(v.tensor_reduce(low[:], logits[:], AX.X, ALU.max))
            v.tensor_tensor(work[:], logits[:], over_e(low[:]), ALU.subtract).then_inc(s_sh, 1)
            dve.wait_ge(s_ex, 1)
            step(v.tensor_reduce(tot[:], scores[:], AX.X, ALU.add))
            step(v.reciprocal(tot[:], tot[:]))
            step(v.tensor_tensor(scores[:], scores[:], over_e(tot[:]), ALU.mult))
            for k, pick in ((0, one0), (1, one1)):
                step(v.tensor_reduce(top[:, k, :], scores[:], AX.X, ALU.max))
                step(v.tensor_tensor(work[:], scores[:], over_e(top[:, k, :]), ALU.is_equal))
                step(v.tensor_tensor(work[:], work[:], over_t(eid[:]), ALU.mult))
                step(v.tensor_reduce(low[:], work[:], AX.X, ALU.min))
                step(v.tensor_tensor(pick[:], over_t(eid[:]), over_e(low[:]), ALU.is_equal))
                if k == 0:
                    step(v.scalar_tensor_tensor(scores[:].rearrange("p t e -> p (t e)"), pick[:].rearrange("p t e -> p (t e)"), -2.0,
                                                scores[:].rearrange("p t e -> p (t e)"), ALU.mult, ALU.add))
            v.tensor_tensor(taken[:], one0[:], one1[:], ALU.add).then_inc(s_oh, 1)
            step(v.tensor_tensor(top[:, 2, :], top[:, 0, :], top[:, 1, :], ALU.add))
            step(v.reciprocal(top[:, 2, :], top[:, 2, :]))
            for k in range(2):
                step(v.tensor_tensor(weight[:, k, :], top[:, k, :], top[:, 2, :], ALU.mult))
            dve.wait_ge(s_cnt, 2)
            step(v.tensor_copy(before[:], bank_r[:].rearrange("p (t e) -> p t e", e=E)))
            step(v.tensor_copy(scan_a[:], bank_t[:].rearrange("p (t e) -> p t e", e=E)))
            step(v.tensor_tensor(before[:], before[:], scan_a[:], ALU.subtract))
            src, dst, n = scan_a, scan_b, 1
            while n < TILES:
                step(v.tensor_copy(dst[:, 0:n, :], src[:, 0:n, :]))
                step(v.tensor_tensor(dst[:, n:, :], src[:, n:, :], src[:, :TILES - n, :], ALU.add))
                src, dst, n = dst, src, 2 * n
            step(v.tensor_tensor(before[:], before[:], src[:], ALU.add))
            step(v.tensor_scalar(cnt[:, 0, :], src[:, TILES - 1, :], float(P - 1), None, ALU.add))
            step(v.tensor_copy(cnt_i[:], cnt[:, 0, :]))
            step(v.tensor_scalar(cnt_i[:], cnt_i[:], P.bit_length() - 1, None, ALU.arith_shift_right))
            step(v.tensor_copy(cnt[:, 0, :], cnt_i[:]))
            step(v.tensor_copy(cnt[:, 1, :], cnt[:, 0, :]))
            for e in range(1, E):
                step(v.tensor_tensor(cnt[:, 1, e:e + 1], cnt[:, 1, e:e + 1], cnt[:, 1, e - 1:e], ALU.add))
            step(v.tensor_tensor(cnt[:, 2, :], cnt[:, 1, :], cnt[:, 0, :], ALU.subtract))
            step(v.tensor_scalar(cnt[:, 2, :], cnt[:, 2, :], float(P), None, ALU.mult))
            step(v.tensor_tensor(before[:], before[:], over_t(cnt[:, 2, :]), ALU.add))
            for k, pick in ((0, one0), (1, one1)):
                step(v.tensor_tensor(work[:], before[:], pick[:], ALU.mult))
                step(v.tensor_reduce(low[:], work[:], AX.X, ALU.add))
                v.tensor_copy(slot[:, k, :], low[:]).then_inc(s_slots, 1)
            step(v.tensor_scalar(te[:], tid[:], cnt[0:1, 1, 0:1], None, ALU.is_ge))
            for e in range(1, E - 1):
                step(v.scalar_tensor_tensor(te[:], tid[:], cnt[0:1, 1, e:e + 1], te[:], ALU.is_ge, ALU.add))
            step(v.tensor_copy(tile_expert[:], te[:]))
            for e in range(E):
                r = raw[e % 2]
                dve.wait_ge(raw_loaded[e % 2], 32 * (e // 2 + 1))
                v.tensor_scalar(r[:], r[:], rmsw[:, 0:1], None, ALU.mult).then_inc(raw_scaled, 1)
                dve.wait_ge(raw_scaled, e + 1)
                v.tensor_copy(w13h[:, e, :, :], r[:]).then_inc(high_ready, 1)
                dve.wait_ge(high_ready, e + 1)
                v.tensor_tensor(w13l[:, e, :, :], r[:], w13h[:, e, :, :].bitcast(F32), ALU.subtract).then_inc(low_ready, 1)


def experts_block(nc, d, w):
    with ExitStack() as ctx:
        def sb(name, shape, dt=F32):
            return ctx.enter_context(nc.sbuf_tensor(name, shape, dt))

        def psum(name):
            return ctx.enter_context(nc.psum_tensor(name, [P, 512], F32))

        def sem(name):
            return ctx.enter_context(nc.semaphore(name))

        w13h, w13l, w2 = w["w13h"], w["w13l"], w["w2"]
        ident = sb("ident_experts", [P, P])
        RING = 4
        hrow = [sb(f"slot_rows{i}", [P, D]) for i in range(RING)]
        hTh = [sb(f"slot_rowsT_high{i}", [P, P], F32R) for i in range(2)]
        hTl = [sb(f"slot_rowsT_low{i}", [P, P], F32R) for i in range(2)]
        si = [sb(f"silu_a{i}", [P, EI]) for i in range(2)]
        ac = [sb(f"hidden{i}", [P, EI]) for i in range(2)]
        aT = [sb(f"hiddenT{i}", [EC, ES, P]) for i in range(2)]
        orow = [sb(f"slot_result{i}", [P, D]) for i in range(2)]
        bank_a = [psum(f"bank_a{i}") for i in range(2)]
        bank_g = [psum(f"bank_g{i}") for i in range(2)]
        bank_h, bank_t = psum("bank_rowsT"), psum("bank_hiddenT")
        bank_o = [psum(f"bank_result{i}") for i in range(2)]
        HALF = S // 2
        wr, wi = sb("w_re", [P, NS, S]), sb("w_im", [P, NS, HALF])
        PART = HALF // 2
        pr, pi = sb("prod_re", [P, NS, PART]), sb("prod_im", [P, NS, PART])
        zz, zt = sb("z_power", [P, 2, NS]), sb("z_square", [P, 3, NS])
        kpad = sb("kpad_sb", [P, P + S])
        dskip = sb("d_skip_sb", [P, CB])

        s_in = sem("s_experts_const")
        row_loaded = [sem(f"slot_row_loaded{i}") for i in range(RING)]
        stored = [sem(f"slot_result_stored{i}") for i in range(2)]
        s_k, s_kstep, s_kout = sem("s_kernel_ready"), sem("s_kernel_step"), sem("s_kernel_stored")
        ht_done, high_ready, hT_ready, ag_done, si_ready, ac_ready, at_done, aT_ready, o_done, o_ready = (
            sem(n) for n in ("ht_done", "hT_high_ready", "hT_ready", "ag_done", "si_ready", "ac_ready", "at_done", "aT_ready",
                             "slot_done", "slot_ready"))
        block = ctx.enter_context(nc.Block())
        M = SLOT_TILES

        def iterations(eng, body):
            def at(m, phase):
                static = isinstance(m, int)
                body(m, phase, not static or m + 1 < M, not static or 0 <= m < M, not static or 1 <= m <= M,
                     not static or 2 <= m <= M + 1)

            for m in range(-1, 3):
                at(m, m % 4)
            with eng.Fori(3, M - 4, 4) as m:
                for u in range(4):
                    at(m + u, (3 + u) % 4)
            for m in range(M - 1, M + 2):
                at(m, m % 4)

        @block.sync
        def _(sp):
            sp.dma_start(ident[:], d["ident"]).then_inc(s_in, 16)
            sp.dma_start(dskip[:], d["D_skip"]).then_inc(s_in, 16)
            slots_in = d["slot_in"].rearrange("(m p) d -> m p d", p=P)
            slots_out = d["slot_out"].rearrange("(m p) d -> m p d", p=P)

            def load(m, ring):
                reach(sp, ht_done, m - RING + 1)
                sp.dma_start(hrow[ring][:], slots_in[bass.ds(m, 1)].rearrange("a p d -> p (a d)")).then_inc(row_loaded[ring], 16)

            def body(m, ph, ahead, first, turn, second):
                if isinstance(m, int) and m < 0:
                    load(0, 0)
                    load(1, 1)
                if not isinstance(m, int) or m + 3 < M:
                    load(m + 3, (ph + 3) % RING)
                if second:
                    par = ph % 2
                    sp.wait_ge(o_ready, m - 1)
                    sp.dma_start(slots_out[bass.ds(m - 2, 1)].rearrange("a p d -> p (a d)"), orow[par][:]).then_inc(stored[par], 16)

            for m in range(-1, 3):
                body(m, m % 4, True, True, True, m >= 2)
            with sp.Fori(3, M - 8, 4) as m:
                for u in range(4):
                    body(m + u, (3 + u) % 4, True, True, True, True)
            for m in range(M - 5, M + 2):
                body(m, m % 4, True, True, True, True)
            for par in range(2):
                sp.wait_ge(stored[par], 8 * M)

        @block.tensor
        def _(pe):
            t = nc.tensor
            pe.wait_ge(s_in, 32)

            def expert(m):
                return pe.value_load(w["tile_expert"][0:1, bass.ds(m, 1)], min_val=0, max_val=E - 1)

            def body(m, ph, ahead, first, turn, second):
                par = ph % 2
                if first:
                    e = expert(m)
                    pe.wait_ge(hT_ready, m + 1)
                    reach(pe, ac_ready, m - 1)
                    for k, bank in enumerate((bank_a[par], bank_g[par])):
                        wh = w13h[:, bass.ds(e, 1), k, :].rearrange("p a i -> p (a i)")
                        wl = w13l[:, bass.ds(e, 1), k, :].rearrange("p a i -> p (a i)")
                        t.matmul(bank[:, 0:EI], hTh[par][:], wh, start=True, stop=False)
                        t.matmul(bank[:, 0:EI], hTh[par][:], wl, start=False, stop=False)
                        last = t.matmul(bank[:, 0:EI], hTl[par][:], wh, start=False, stop=True)
                    last.then_inc(ag_done, 1)
                if ahead:
                    ring = (ph + 1) % RING
                    pe.wait_ge(row_loaded[ring], 4 * (m + 1 - ring) + 16)
                    reach(pe, hT_ready, m + 1)
                    t.transpose(bank_h[:, 0:P], hrow[ring][:], ident[:]).then_inc(ht_done, 1)
                if turn:
                    pe.wait_ge(ac_ready, m)
                    reach(pe, aT_ready, m - 1)
                    for k in range(ES):
                        last = t.transpose(bank_t[0:EC, k * P:(k + 1) * P], ac[1 - par][:, k * EC:(k + 1) * EC], ident[:])
                    last.then_inc(at_done, 1)
                if second:
                    e = expert(m - 2)
                    pe.wait_ge(aT_ready, m - 1)
                    reach(pe, o_ready, m - 3)
                    for k in range(ES):
                        last = t.matmul(bank_o[par][:, 0:P], aT[par][:, k, :], w2[:, bass.ds(e, 1), k, :].rearrange("p a n -> p (a n)"),
                                        start=(k == 0), stop=(k == ES - 1))
                    last.then_inc(o_done, 1)

            iterations(pe, body)

        @block.scalar
        def _(act):
            a = nc.scalar

            def body(m, ph, ahead, first, turn, second):
                par = ph % 2
                if first:
                    act.wait_ge(ag_done, m + 1)
                    reach(act, ac_ready, m - 1)
                    a.activation(si[par][:], bank_a[par][:, 0:EI], ACT.Silu).then_inc(si_ready, 1)
                if ahead:
                    act.wait_ge(ht_done, m + 2)
                    reach(act, ag_done, m)
                    a.activation(hTh[1 - par][:], bank_h[:, 0:P], ACT.Copy).then_inc(high_ready, 1)
                if turn:
                    act.wait_ge(at_done, m)
                    reach(act, o_done, m - 2)
                    a.activation(aT[1 - par][:].rearrange("p k t -> p (k t)"), bank_t[0:EC, :], ACT.Copy).then_inc(aT_ready, 1)

            iterations(act, body)

        @block.vector
        def _(dve):
            v = nc.vector

            def body(m, ph, ahead, first, turn, second):
                par = ph % 2
                if ahead:
                    dve.wait_ge(high_ready, m + 2)
                    reach(dve, ag_done, m)
                    v.tensor_tensor(hTl[1 - par][:], bank_h[:, 0:P], hTh[1 - par][:].bitcast(F32), ALU.subtract).then_inc(hT_ready, 1)
                if first:
                    dve.wait_ge(si_ready, m + 1)
                    reach(dve, at_done, m - 1)
                    v.tensor_tensor(ac[par][:], bank_g[par][:, 0:EI], si[par][:], ALU.mult).then_inc(ac_ready, 1)
                if second:
                    dve.wait_ge(o_done, m - 1)
                    reach(dve, stored[par], 8 * (m - 2 - par))
                    v.tensor_copy(orow[par][:], bank_o[par][:, 0:P]).then_inc(o_ready, 1)

            iterations(dve, body)

        @block.gpsimd
        def _(pool):
            g = nc.gpsimd
            step = Chain(pool, s_kstep)
            poles = w["poles"]
            pool.wait_ge(s_in, 32)
            step(g.memset(kpad[:, 0:P], 0.0))
            for c in range(CB):
                q = slice(c * NS, (c + 1) * NS)
                step(g.tensor_copy(zz[:], poles[:, 0:2, q]))
                step(g.tensor_copy(wr[:, :, 0], poles[:, 2, q]))
                step(g.tensor_copy(wi[:, :, 0], poles[:, 3, q]))
                n = 1
                while n < S:
                    for lo in range(0, n, PART):
                        size = min(n, PART)
                        src, dst = slice(lo, lo + size), slice(n + lo, n + lo + size)
                        z_re, z_im = (zz[:, i, :].unsqueeze(2).to_broadcast([P, NS, size]) for i in range(2))
                        e, f = pr[:, :, 0:size], pi[:, :, 0:size]
                        step(g.tensor_tensor(e, wr[:, :, src], z_re, ALU.mult))
                        step(g.tensor_tensor(f, wi[:, :, src], z_im, ALU.mult))
                        step(g.tensor_tensor(wr[:, :, dst], e, f, ALU.subtract))
                        if n < HALF:
                            step(g.tensor_tensor(e, wr[:, :, src], z_im, ALU.mult))
                            step(g.tensor_tensor(f, wi[:, :, src], z_re, ALU.mult))
                            step(g.tensor_tensor(wi[:, :, dst], e, f, ALU.add))
                    if n < HALF:
                        step(g.tensor_tensor(zt[:, 0:2, :], zz[:], zz[:], ALU.mult))
                        step(g.tensor_tensor(zt[:, 2, :], zz[:, 0, :], zz[:, 1, :], ALU.mult))
                        step(g.tensor_tensor(zz[:, 0, :], zt[:, 0, :], zt[:, 1, :], ALU.subtract))
                        step(g.tensor_tensor(zz[:, 1, :], zt[:, 2, :], zt[:, 2, :], ALU.add))
                    n *= 2
                m = NS // 2
                while m > 1:
                    step(g.tensor_tensor(wr[:, 0:m, :], wr[:, 0:m, :], wr[:, m:2 * m, :], ALU.add))
                    m //= 2
                step(g.tensor_tensor(kpad[:, P:], wr[:, 0, :], wr[:, 1, :], ALU.add))
                step(g.tensor_tensor(kpad[:, P:P + 1], kpad[:, P:P + 1], dskip[:, c:c + 1], ALU.add))
                pool.dma_start(d["kpad"][c * P:(c + 1) * P, :], kpad[:]).then_inc(s_kout, 16)
                pool.wait_ge(s_kout, 16 * (c + 1))


def mix_and_combine_block(nc, d, w):
    with ExitStack() as ctx:
        def sb(name, shape, dt=F32):
            return ctx.enter_context(nc.sbuf_tensor(name, shape, dt))

        def psum(name):
            return ctx.enter_context(nc.psum_tensor(name, [P, 512], F32))

        def sem(name):
            return ctx.enter_context(nc.semaphore(name))

        x1, slot, weight, xs = w["x1"], w["slot"], w["weight"], w["xs"]
        HALVES, TB = CH // P, TPS * B
        LB = 4
        wz = sb("w_in_z", [P, HALVES, P])
        wout = sb("w_outT", [P, HALVES, D])
        ident = sb("ident_mixer", [P, P])
        xp = [sb(f"x2T_mix{i}", [P, S]) for i in range(2)]
        zs = sb("gate_z", [P, HALVES, TPS, B, P])
        RING = 4
        tt = [sb(f"toeplitz{i}", [P, GB, S]) for i in range(RING)]
        xg = [w["logits"][:].rearrange("p t e -> p (t e)"), sb("conv_out_group", [P, GB * TB])[:]]
        ys = xs[:].rearrange("p (i a) c b -> p i (a c b)", a=HALVES)
        flat = [tt[i][:, 0:LB * P // S, :].rearrange("p a n -> p (a n)") for i in range(RING)]
        yl = [flat[i].rearrange("p (k i) -> p k i", k=LB) for i in range(2)]
        gT = [flat[2 + i].rearrange("p (a c t) -> p a c t", a=HALVES, c=TPS) for i in range(2)]
        got = [sb(f"gathered{i}", [P, 2, D]) for i in range(RING)]
        idx = [sb(f"gather_index{i}", [P, 2], I32) for i in range(RING)]
        minor = sb("gather_start", [P, 1])
        bank_z = [psum(f"bank_z{i}") for i in range(2)]
        bank_y = [psum(f"bank_y{i}") for i in range(2)]
        bank_t = [psum(f"bank_yT{i}") for i in range(2)]
        bank_m = [psum(f"bank_mix{i}") for i in range(2)]

        s_in, s_ready = sem("s_mixer_loaded"), sem("s_gather_start")
        xp_loaded = [sem(f"xp_mix_loaded{i}") for i in range(2)]
        t_loaded = [sem(f"toeplitz_loaded{i}") for i in range(RING)]
        xg_ready, z_done, z_ready, y_done, y_ready = (sem(n) for n in ("xg_ready", "z_done", "z_ready", "y_done", "y_ready"))
        yl_ready, yt_done, gated = sem("yl_ready"), sem("yt_done"), sem("gated_ready")
        gT_ready, mix_done, mix_added = sem("gT_ready"), sem("mix_done"), sem("mix_added")
        idx_ready = sem("gather_index_ready")
        gathered = [sem(f"gathered_sem{i}") for i in range(RING)]
        added0, added1, out_sent = sem("first_added"), sem("second_added"), sem("out_sent")
        loads = [(wz[:], d["W_zT"]), (wout[:], d["W_outT"]), (ident[:], d["ident"])]
        kp = d["kpad"]
        block = ctx.enter_context(nc.Block())

        @block.sync
        def _(sp):
            for dst, src in loads:
                sp.dma_start(dst, src).then_inc(s_in, 16)

            def load(g, turn):
                reach(sp, z_done, g - 1)
                sp.dma_start(xp[turn % 2][:], d["x2T"][bass.ds(g, 1), :, 0:S].rearrange("a p t -> p (a t)")).then_inc(xp_loaded[turn % 2], 16)
                reach(sp, y_done, g - RING + 1)
                rows = bass.AP(kp.tensor, g * (GB * (P + S)) + 1, [[1, P], [P + S, GB], [1, S]])
                sp.dma_start(tt[turn][:], rows).then_inc(t_loaded[turn], 16)

            in_turns(sp, GROUPS, RING, load)

            def store(b, par):
                sp.wait_ge(mix_added, b + 1)
                sp.dma_start(d["out"][bass.ds(b, 1)].rearrange("a (t p) d -> p (a t) d", p=P), x1[:, bass.ds(2 * b, 2), :]).then_inc(out_sent, 16)

            pairwise(sp, B, store)
            sp.wait_ge(out_sent, 16 * B)

        @block.gpsimd
        def _(pool):
            g = nc.gpsimd
            g.memset(minor[:], 0.0).then_inc(s_ready, 1)

            def gather(t, par):
                reach(pool, added1, t - RING + 1)
                g.tensor_copy(idx[par][:].unsqueeze(2), slot[:, :, bass.ds(t, 1)]).then_inc(idx_ready, 1)
                wait_apart(pool, (s_ready, 1), (idx_ready, t + 1))
                for k in range(2):
                    g.indirect_dma_start(got[par][:, k, :], None, d["slot_out"],
                                         bass.IndirectOffsetOnAxis(ap=idx[par][:, k:k + 1], axis=0)).then_inc(gathered[par], 16)

            in_turns(pool, TILES, RING, gather)

        @block.tensor
        def _(pe):
            t = nc.tensor
            pe.wait_ge(s_in, 16 * len(loads))

            def products(g, turn):
                par = turn % 2
                pe.wait_ge(xp_loaded[par], 8 * (g - par) + 16)
                reach(pe, z_ready, g - 1)
                for a in range(HALVES):
                    last = t.matmul(bank_z[par][:, a * S:(a + 1) * S], wz[:, a, :], xp[par][:], start=True, stop=True)
                last.then_inc(z_done, 1)
                pe.wait_ge(xg_ready, g + 1)
                pe.wait_ge(t_loaded[turn], 4 * (g - turn) + 16)
                reach(pe, y_ready, g - 1)
                for i in range(GB // HALVES):
                    out = bank_y[par][:, i * P:(i + 1) * P]
                    for a in range(HALVES):
                        h = HALVES * i + a
                        t.matmul(out[a * TB:(a + 1) * TB, :], xg[par][:, h * TB:(h + 1) * TB], tt[turn][:, h, 0:P],
                                 start=True, stop=False, skip_group_check=True)
                    for a in range(HALVES):
                        h = HALVES * i + a
                        last = t.matmul(out[a * TB + B:(a + 1) * TB, :], xg[par][:, h * TB:h * TB + B], tt[turn][:, h, P:S],
                                        start=False, stop=True, skip_group_check=True)
                last.then_inc(y_done, 1)

            in_turns(pe, GROUPS, RING, products)

            def turn_products(q, par):
                pe.wait_ge(yl_ready, q + 1)
                reach(pe, gated, q - 1)
                for k in range(LB):
                    last = t.transpose(bank_t[par][:, k * P:(k + 1) * P], yl[par][:, k, :], ident[:])
                last.then_inc(yt_done, 1)

            pairwise(pe, P // LB, turn_products)

            def output(b, par):
                pe.wait_ge(gT_ready, b + 1)
                reach(pe, mix_added, b - 1)
                for c in range(TPS):
                    for a in range(HALVES):
                        last = t.matmul(bank_m[par][:, c * P:(c + 1) * P], gT[par][:, a, c, :], wout[:, a, :],
                                        start=(a == 0), stop=(a == HALVES - 1))
                last.then_inc(mix_done, 1)

            pairwise(pe, B, output)

        @block.scalar
        def _(act):
            a = nc.scalar

            def stage(g, par):
                reach(act, y_done, g - 1)
                a.activation(xg[par], xs[:, bass.ds(g * GB, GB), :, :].rearrange("p h c b -> p (h c b)"), ACT.Copy).then_inc(xg_ready, 1)

            def silu(b, par):
                act.wait_ge(z_done, b + 1)
                a.activation(zs[:, :, :, bass.ds(b, 1), :].rearrange("p a c b t -> p a c (b t)"),
                             bank_z[par][:].rearrange("p (a c t) -> p a c t", a=HALVES, c=TPS), ACT.Silu).then_inc(z_ready, 1)

            stage(0, 0)
            stage(1, 1)
            silu(0, 0)
            with act.Fori(2, GROUPS - 1, 2) as g:
                stage(g, 0)
                silu(g - 1, 1)
                stage(g + 1, 1)
                silu(g, 0)
            silu(GROUPS - 1, 1)

            act.wait_ge(y_ready, GROUPS)

            def stage_products(q, par):
                reach(act, yt_done, q - 1)
                a.activation(yl[par], ys[:, :, bass.ds(q * LB, LB)].rearrange("p i k -> p k i"), ACT.Copy).then_inc(yl_ready, 1)

            pairwise(act, P // LB, stage_products)
            act.wait_ge(gated, P // LB)

            def stage_gated(b, par):
                reach(act, mix_done, b - 1)
                a.activation(gT[par], zs[:, :, :, bass.ds(b, 1), :].rearrange("p a c b t -> p a c (b t)"), ACT.Copy).then_inc(gT_ready, 1)

            pairwise(act, B, stage_gated)

        @block.vector
        def _(dve):
            v = nc.vector

            def combine(t, par):
                dve.wait_ge(gathered[par], 8 * (t - par) + 32)
                row = x1[:, bass.ds(t, 1), :].rearrange("p a d -> p (a d)")
                share = lambda k: weight[:, k, bass.ds(t, 1)]
                v.scalar_tensor_tensor(row, got[par][:, 0, :], share(0), row, ALU.mult, ALU.add).then_inc(added0, 1)
                dve.wait_ge(added0, t + 1)
                v.scalar_tensor_tensor(row, got[par][:, 1, :], share(1), row, ALU.mult, ALU.add).then_inc(added1, 1)

            def copy_y(g, par):
                dve.wait_ge(y_done, g + 1)
                v.tensor_copy(xs[:, bass.ds(g * GB, GB), :, :].rearrange("p h c b -> p (h c b)"), bank_y[par][:]).then_inc(y_ready, 1)
                for t in range(TPS):
                    combine(TPS * g + t, (TPS * par + t) % RING)

            pairwise(dve, GROUPS, copy_y)
            dve.wait_ge(z_ready, B)
            dve.wait_ge(added1, TILES)

            def gate(q, par):
                dve.wait_ge(yt_done, q + 1)
                here = zs[:, :, :, :, bass.ds(q * LB, LB)].rearrange("p a c b k -> p (a c b) k")
                v.tensor_tensor(here, bank_t[par][:].rearrange("p (k x) -> p x k", k=LB), here, ALU.mult).then_inc(gated, 1)

            pairwise(dve, P // LB, gate)

            def add(b, par):
                rows = x1[:, bass.ds(2 * b, 2), :]
                dve.wait_ge(mix_done, b + 1)
                v.tensor_tensor(rows, bank_m[par][:, 0:S].rearrange("p (t d) -> p t d", t=TPS), rows, ALU.add).then_inc(mix_added, 1)

            pairwise(dve, B, add)


def build_program(nc, d):
    with ExitStack() as ctx:
        def sb(name, shape, dt=F32):
            return ctx.enter_context(nc.sbuf_tensor(name, shape, dt))

        w = {"x1": sb("x1", [P, TILES, D]), "logits": sb("logits", [P, TILES, E]),
             "slot": sb("slot_of_choice", [P, 2, TILES], I32), "weight": sb("choice_weight", [P, 2, TILES]),
             "poles": sb("poles", [P, 4, CB * NS]),
             "tile_expert": sb("tile_expert", [1, SLOT_TILES], I32)}
        with ExitStack() as first:
            w["bw1T"] = first.enter_context(nc.sbuf_tensor("bw1T", [P, HID], F32))
            w["bw2T"] = first.enter_context(nc.sbuf_tensor("bw2T", [P, HID], F32))
            setup_block(nc, d, w)
            layer0_block(nc, d, w)
        w["xs"] = sb("conv_out", [P, CH, TPS, B])
        with ExitStack() as moe:
            w["w13h"] = moe.enter_context(nc.sbuf_tensor("w13_high", [P, E, 2, EI], F32R))
            w["w13l"] = moe.enter_context(nc.sbuf_tensor("w13_low", [P, E, 2, EI], F32R))
            w["w2"] = moe.enter_context(nc.sbuf_tensor("w2T", [EC, E, ES, D], F32))
            route_and_convolve_block(nc, d, w)
            experts_block(nc, d, w)
        mix_and_combine_block(nc, d, w)


def shape_constants():
    t = np.arange(S, dtype=np.float64)
    inv = 1.0 / 10000.0 ** (np.arange(0, HD, 2, dtype=np.float64) / HD)
    ang = np.concatenate([np.outer(t, inv)] * 2, axis=-1).T
    cos, sin = np.cos(ang), np.sin(ang)
    sin = np.concatenate([-sin[:HD // 2], sin[HD // 2:]])
    slope = 2.0 ** (-8.0 / NH * (np.arange(NH) + 1))
    lag = t[None, :] - np.arange(P)[:, None]
    m = np.where(lag >= 0, np.exp(-slope[:, None, None] * np.maximum(lag, 0)), 0.0)
    m = np.concatenate([m, m[:, :, :P]], axis=2).transpose(1, 0, 2)
    f = lambda a: np.ascontiguousarray(a, dtype=np.float32)
    return {"rope_q": f(np.concatenate([cos, sin])), "rope_kc": f(np.concatenate([cos, cos])),
            "rope_ks": f(np.concatenate([sin, sin])), "decay": f(m), "ident": np.eye(P, dtype=np.float32),
            "flip": f(np.eye(P)[::-1]),
            "expert_minus": f(np.broadcast_to(np.arange(E) - E, (P, E))), "tile_ids": f(np.arange(SLOT_TILES)[None]),
            "earlier": f(np.triu(np.ones((P, P)), 1)), "ones": np.ones((P, P), np.float32)}


def layout(i):
    g = {k: np.asarray(v) for k, v in i.items()}
    turned = (np.arange(HD) + HD // 2) % HD
    wq = g["L0_attn_Wq"].reshape(NH, HD, D)
    wk = g["L0_attn_Wk"].reshape(NKV, HD, D)
    both = np.concatenate([wq, wq[:, turned]], axis=1)
    kb = np.concatenate([wk.reshape(2, P, D), wk[:, turned].reshape(2, P, D)])
    c = np.ascontiguousarray
    return {
        "x": c(g["L0_attn_x"]), "wq": c(both.transpose(2, 0, 1)), "wk": c(kb.transpose(2, 0, 1)),
        "wv": c(g["L0_attn_Wv"].T), "wo": c(g["L0_attn_Wo"].T.reshape(PAIRS, P, D).transpose(1, 0, 2)),
        "ffn_w1": c(g["L0_ffn_w1"]), "ffn_b1": c(g["L0_ffn_b1"].reshape(HB, P).T), "ffn_w2": c(g["L0_ffn_w2"]), "ffn_b2": c(g["L0_ffn_b2"]),
        "W_inT": c(g["L1_attn_W_in"].T), "conv_wT": c(g["L1_attn_conv_w"].T), "conv_b": c(g["L1_attn_conv_b"]),
        "log_dt": c(g["L1_attn_log_dt"].reshape(CB, P).T), "log_A_real": c(g["L1_attn_log_A_real"]), "A_imag": c(g["L1_attn_A_imag"]),
        "C_re": c(g["L1_attn_C_re"]), "C_im": c(g["L1_attn_C_im"]), "D_skip": c(g["L1_attn_D"].reshape(CB, P).T),
        "W_zT": c(g["L1_attn_W_in"][CH:].reshape(P, CH // P, D).transpose(2, 1, 0)), "W_outT": c(g["L1_attn_W_out"].T.reshape(P, CH // P, D)),
        "rms_w": c(g["L1_ffn_rms_weight"].reshape(P, 1)), "gateT": c(g["L1_ffn_gate_w"].T),
        "w1T": c(g["L1_ffn_w1"].transpose(2, 0, 1)), "w3T": c(g["L1_ffn_w3"].transpose(2, 0, 1)),
        "w2T": c(g["L1_ffn_w2"].reshape(E, D, ES, EC).transpose(3, 0, 2, 1)),
    }


def kernel(**inputs):
    import concourse.bacc as bacc
    from concourse.bass_utils import run_bass_kernel_spmd

    nc = bacc.Bacc("TRN2", target_bir_lowering=False, num_devices=1)
    arrays = {f"in_{k}": v for k, v in {**layout(inputs), **shape_constants()}.items()}
    d = {k[3:]: nc.dram_tensor(k, v.shape, mybir.dt.from_np(v.dtype), kind="ExternalInput").ap() for k, v in arrays.items()}
    for name, shape in SCRATCH.items():
        d[name] = nc.dram_tensor(f"scratch_{name}", shape, F32, kind="Internal").ap()
    d["out"] = nc.dram_tensor("out_x", (B, S, D), F32, kind="ExternalOutput").ap()
    build_program(nc, d)
    r = run_bass_kernel_spmd(nc, [arrays], core_ids=[0])
    return r.results[0]["out_x"]
```

```python
import math
from contextlib import ExitStack

import concourse.bass as bass
import concourse.mybir as mybir
import numpy as np

F32 = mybir.dt.float32
F32R = mybir.dt.float32r
I32 = mybir.dt.int32
ALU = mybir.AluOpType
ACT = mybir.ActivationFunctionType
AX = mybir.AxisListType

P = 128
B, S, D = 32, 256, 128
TILES = B * S // P
TPS = S // P
NH, NKV, HD = 16, 4, 64
PAIRS = NH // 2
HID = 512
HB = HID // P
CH, NS, TAPS = 256, 8, 4
CB = CH // P
E, EI = 8, 448
EC = 112
ES = EI // EC
SLOT_TILES = 2 * TILES + E
SLOTS = SLOT_TILES * P
SCW = S + P
EPS_LN, EPS_RMS = 1e-5, 1e-6
GB = 8
GROUPS = CH // GB


def reach(eng, semaphore, value):
    if isinstance(value, int) and value <= 0:
        return
    eng.wait_ge(semaphore, value)


def wait_apart(eng, started, *waits):
    counts = [(s, v if isinstance(v, int) else eng.to_reg(v)) for s, v in waits]
    eng.wait_ge(*started)
    for semaphore, value in counts:
        reach(eng, semaphore, value)


class Chain:

    def __init__(self, eng, semaphore):
        self.eng, self.semaphore, self.count = eng, semaphore, 0

    def __call__(self, instruction):
        self.count += 1
        instruction.then_inc(self.semaphore, 1)
        self.eng.wait_ge(self.semaphore, self.count)


def layer0_loads(ctx, nc, d, w):
    def sb(name, shape, dt=F32):
        return ctx.enter_context(nc.sbuf_tensor(name, shape, dt))

    wq, wk, wv = sb("wq_pairs", [P, PAIRS, P]), sb("wk_stack", [P, 4, P]), sb("wvT", [P, NKV * HD])
    wqh, wkh, wvh = sb("wq_high", [P, PAIRS, P], F32R), sb("wk_high", [P, 4, P], F32R), sb("wv_high", [P, NKV * HD], F32R)
    wql, wkl, wvl = sb("wq_low", [P, PAIRS, P], F32R), sb("wk_low", [P, 4, P], F32R), sb("wv_low", [P, NKV * HD], F32R)
    wo = sb("woT", [P, PAIRS, D])
    rope_q = sb("rope_q", [P, S])
    rope_kc, rope_ks = sb("rope_k_cos", [P, S]), sb("rope_k_sin", [P, S])
    decay = sb("decay", [P, PAIRS, 2 * SCW])
    b1, b2 = sb("b1_cols", [P, HB]), sb("b2_rows", [P, D])
    gate = sb("gateT", [P, E])
    rmsw = sb("rms_w", [P, 1])
    ident = sb("ident", [P, P])
    flip = sb("flip", [P, P])
    w["layer0"] = (wq, wqh, wql, wk, wkh, wkl, wv, wvh, wvl, wo, rope_q, rope_kc, rope_ks, decay, b1, b2, gate, rmsw, ident, flip)
    w["s_weights"], w["s_x"] = (ctx.enter_context(nc.semaphore(n)) for n in ("s_weights", "s_x_loaded"))
    w["layer0_loads"] = [(wq[:], d["wq"]), (wk[:], d["wk"]), (wv[:], d["wv"]), (wo[:], d["wo"]),
             (rope_q[:], d["rope_q"]), (rope_kc[:], d["rope_kc"]), (rope_ks[:], d["rope_ks"]),
             (decay[:], d["decay"]), (b1[:], d["ffn_b1"]),
             (b2[:], d["ffn_b2"].partition_broadcast(P)),
             (gate[:], d["gateT"]), (rmsw[:], d["rms_w"]),
             (ident[:], d["ident"]), (flip[:], d["flip"])]


def setup_block(nc, d, w):
    with ExitStack() as ctx:
        def sb(name, shape, dt=F32):
            return ctx.enter_context(nc.sbuf_tensor(name, shape, dt))

        def sem(name):
            return ctx.enter_context(nc.semaphore(name))

        w1 = sb("w1_rows", [P, HB, D])
        w2 = sb("w2_rows", [P, HID])
        ta, tb = sb("sign_pos", [P, HID]), sb("sign_neg", [P, HID])
        alpha = sb("alpha", [P, HB + 1])
        bw = sb("bw_rows", [P, 2, HID])
        ident = sb("ident_setup", [P, P])
        s4, aim, cre, cim = w["s4"], w["a_imag"], w["c_re"], w["c_im"]
        ld = sb("log_dt_sb", [P, CB])
        lar = sb("log_a_real_sb", [P, CB, NS])
        dt = sb("dt_sb", [P, CB])
        turns = sb("turns", [P, CB * NS], I32)
        pt = [ctx.enter_context(nc.psum_tensor(f"bw_turn{i}", [P, HID], F32)) for i in range(2)]

        s_in, s_step = sem("s_setup_loaded"), sem("s_setup_step")
        s_bw, s_turn = sem("s_bw_ready"), sem("s_bw_turned")
        s_exp, s_sinarg, s_sin, s_areal = sem("s_exp"), sem("s_sin_args"), sem("s_sin"), sem("s_a_real")
        s_cp = sem("s_bw_copied")
        loads = [
            (w1[:], d["ffn_w1"].rearrange("(c p) d -> p c d", p=P)), (w2[:], d["ffn_w2"]),
            (ident[:], d["ident"]),
            (ld[:], d["log_dt"]),
            (lar[:], d["log_A_real"].rearrange("(c p) n -> p c n", p=P)),
            (aim[:], d["A_imag"].rearrange("(c p) n -> p c n", p=P)),
            (cre[:], d["C_re"].rearrange("(c p) n -> p c n", p=P)),
            (cim[:], d["C_im"].rearrange("(c p) n -> p c n", p=P)),
        ]
        block = ctx.enter_context(nc.Block())

        @block.sync
        def _(sp):
            xr = d["x"].rearrange("b (t p) d -> p (b t) d", p=P)
            for dst, src in loads:
                sp.dma_start(dst, src).then_inc(s_in, 16)
            for q in range(8):
                a = q * TILES // 8
                sp.dma_start(w["x1"][:, a:a + TILES // 8, :], xr[:, a:a + TILES // 8, :]).then_inc(w["s_x"], 16)
                if q == 0:
                    for dst, src in w["layer0_loads"]:
                        sp.dma_start(dst, src).then_inc(w["s_weights"], 16)

        @block.tensor
        def _(pe):
            pe.wait_ge(s_in, 16 * len(loads))
            pe.wait_ge(s_bw, 2)
            for m in range(2):
                for c in range(HB):
                    last = nc.tensor.transpose(pt[m][:, c * P:(c + 1) * P], bw[:, m, c * P:(c + 1) * P], ident[:])
                last.then_inc(s_turn, 1)

        @block.scalar
        def _(act):
            act.wait_ge(s_in, 16 * len(loads))
            nc.scalar.activation(dt[:], ld[:], ACT.Exp).then_inc(s_exp, 1)
            nc.scalar.activation(s4[:, 0, :], lar[:].rearrange("p c n -> p (c n)"), ACT.Exp).then_inc(s_exp, 1)
            act.wait_ge(s_areal, 1)
            nc.scalar.activation(s4[:, 4, :], s4[:, 2, :], ACT.Exp).then_inc(s_exp, 1)
            act.wait_ge(s_sinarg, 1)
            nc.scalar.activation(s4[:, 7, :], s4[:, 5, :], ACT.Sin).then_inc(s_sin, 1)
            nc.scalar.activation(s4[:, 8, :], s4[:, 6, :], ACT.Sin).then_inc(s_sin, 1)
            act.wait_ge(s_turn, 1)
            nc.scalar.activation(w["bw1T"][:], pt[0][:], ACT.Copy).then_inc(s_cp, 1)
            act.wait_ge(s_turn, 2)
            nc.scalar.activation(w["bw2T"][:], pt[1][:], ACT.Copy).then_inc(s_cp, 1)

        @block.vector
        def _(dve):
            v = nc.vector
            step = Chain(dve, s_step)
            dve.wait_ge(s_in, 16 * len(loads))
            rows = w1[:].rearrange("p c d -> p (c d)")
            step(v.scalar_tensor_tensor(ta[:], rows, -1.0, rows, ALU.mult, ALU.max))
            step(v.tensor_reduce(alpha[:, 0:HB], ta[:].rearrange("p (c d) -> p c d", c=HB), AX.X, ALU.add))
            step(v.scalar_tensor_tensor(tb[:], w2[:], -1.0, w2[:], ALU.mult, ALU.max))
            step(v.tensor_reduce(alpha[:, HB:HB + 1], tb[:], AX.X, ALU.add))
            step(v.tensor_scalar(alpha[:, 0:HB], alpha[:, 0:HB], 1.0 / D, None, ALU.mult))
            step(v.tensor_scalar(alpha[:, HB:HB + 1], alpha[:, HB:HB + 1], 1.0 / HID, None, ALU.mult))
            for m, src in ((0, w1[:].rearrange("p c d -> p (c d)")), (1, w2[:])):
                step(v.tensor_scalar(ta[:], src, 0.0, None, ALU.is_gt))
                step(v.tensor_scalar(tb[:], src, 0.0, None, ALU.is_lt))
                step(v.tensor_tensor(ta[:], ta[:], tb[:], ALU.subtract))
                for c in range(HB):
                    a = alpha[:, c:c + 1] if m == 0 else alpha[:, HB:HB + 1]
                    q = slice(c * P, (c + 1) * P)
                    step(v.scalar_tensor_tensor(tb[:, q], ta[:, q], a, src[:, q], ALU.mult, ALU.subtract))
                v.tensor_tensor(bw[:, m, :], tb[:], src, ALU.add).then_inc(s_bw, 1)
                dve.wait_ge(s_bw, m + 1)

            half = lambda i, c: s4[:, i, c * NS:(c + 1) * NS]
            dve.wait_ge(s_exp, 2)
            step(v.tensor_scalar(s4[:, 1, :], s4[:, 0, :], -1.0, None, ALU.mult))
            for c in range(CB):
                step(v.tensor_scalar(half(2, c), half(1, c), dt[:, c:c + 1], None, ALU.mult))
                step(v.tensor_scalar(half(3, c), aim[:, c, :], dt[:, c:c + 1], None, ALU.mult))
            v.tensor_copy(s4[:, 9, :], s4[:, 2, :]).then_inc(s_areal, 1)
            hi, lo = 6.28125, 2 * math.pi - 6.28125
            for out, shift in ((5, 0.0), (6, math.pi / 2)):
                step(v.tensor_scalar(s4[:, 10, :], s4[:, 3, :], 1.0 / (2 * math.pi), shift / (2 * math.pi), ALU.mult, ALU.add))
                step(v.tensor_copy(turns[:], s4[:, 10, :]))
                step(v.tensor_copy(s4[:, 10, :], turns[:]))
                step(v.scalar_tensor_tensor(s4[:, 11, :], s4[:, 10, :], -hi, s4[:, 3, :], ALU.mult, ALU.add))
                step(v.scalar_tensor_tensor(s4[:, 11, :], s4[:, 10, :], -lo, s4[:, 11, :], ALU.mult, ALU.add))
                step(v.tensor_scalar(s4[:, 11, :], s4[:, 11, :], shift, 3.1415925, ALU.add, ALU.min))
                step(v.tensor_scalar(s4[:, out, :], s4[:, 11, :], -3.1415925, None, ALU.max))
            v.tensor_copy(s4[:, 12, :], s4[:, 5, :]).then_inc(s_sinarg, 1)


def finish_poles(v, step, w):
    s4, aim, cre, cim, poles = w["s4"], w["a_imag"], w["c_re"], w["c_im"], w["poles"]
    flat = lambda t: t[:].rearrange("p c n -> p (c n)")
    step(v.tensor_tensor(s4[:, 13, :], s4[:, 4, :], s4[:, 8, :], ALU.mult))
    step(v.tensor_tensor(s4[:, 14, :], s4[:, 4, :], s4[:, 7, :], ALU.mult))
    step(v.tensor_scalar(s4[:, 15, :], s4[:, 13, :], -1.0, None, ALU.add))
    step(v.tensor_tensor(s4[:, 16, :], flat(cre), s4[:, 15, :], ALU.mult))
    step(v.tensor_tensor(s4[:, 17, :], flat(cim), s4[:, 14, :], ALU.mult))
    step(v.tensor_tensor(s4[:, 16, :], s4[:, 16, :], s4[:, 17, :], ALU.subtract))
    step(v.tensor_tensor(s4[:, 17, :], flat(cre), s4[:, 14, :], ALU.mult))
    step(v.tensor_tensor(s4[:, 18, :], flat(cim), s4[:, 15, :], ALU.mult))
    step(v.tensor_tensor(s4[:, 17, :], s4[:, 17, :], s4[:, 18, :], ALU.add))
    step(v.tensor_tensor(s4[:, 18, :], s4[:, 1, :], s4[:, 1, :], ALU.mult))
    step(v.tensor_tensor(s4[:, 19, :], flat(aim), flat(aim), ALU.mult))
    step(v.tensor_tensor(s4[:, 18, :], s4[:, 18, :], s4[:, 19, :], ALU.add))
    step(v.reciprocal(s4[:, 19, :], s4[:, 18, :]))
    step(v.tensor_scalar(s4[:, 19, :], s4[:, 19, :], 2.0, None, ALU.mult))
    step(v.tensor_tensor(s4[:, 10, :], s4[:, 16, :], s4[:, 1, :], ALU.mult))
    step(v.tensor_tensor(s4[:, 11, :], s4[:, 17, :], flat(aim), ALU.mult))
    step(v.tensor_tensor(s4[:, 10, :], s4[:, 10, :], s4[:, 11, :], ALU.add))
    step(v.tensor_tensor(poles[:, 2, :], s4[:, 10, :], s4[:, 19, :], ALU.mult))
    step(v.tensor_tensor(s4[:, 10, :], s4[:, 17, :], s4[:, 1, :], ALU.mult))
    step(v.tensor_tensor(s4[:, 11, :], s4[:, 16, :], flat(aim), ALU.mult))
    step(v.tensor_tensor(s4[:, 10, :], s4[:, 10, :], s4[:, 11, :], ALU.subtract))
    step(v.tensor_tensor(poles[:, 3, :], s4[:, 10, :], s4[:, 19, :], ALU.mult))
    step(v.tensor_copy(poles[:, 0, :], s4[:, 13, :]))
    step(v.tensor_copy(poles[:, 1, :], s4[:, 14, :]))


def layer0_block(nc, d, w):
    with ExitStack() as ctx:
        def sb(name, shape, dt=F32):
            return ctx.enter_context(nc.sbuf_tensor(name, shape, dt))

        def psum(name, shape=(P, 512)):
            return ctx.enter_context(nc.psum_tensor(name, list(shape), F32))

        def sem(name):
            return ctx.enter_context(nc.semaphore(name))

        x1, logits = w["x1"], w["logits"]
        wq, wqh, wql, wk, wkh, wkl, wv, wvh, wvl, wo, rope_q, rope_kc, rope_ks, decay, b1, b2, gate, rmsw, ident, flip = w["layer0"]
        bw1h, bw1l = w["bw1h"], w["bw1l"]
        loads, s_w, s_x = w["layer0_loads"], w["s_weights"], w["s_x"]
        mhalf = sb("minus_half", [P, TPS])
        zero = sb("zero_rows", [P, 8, D])
        xn, xn2 = sb("xn", [P, TPS, D]), sb("xn2", [P, TPS, D])
        sq = sb("squares", [P, TPS, D])
        st, mv = sb("ln_stats", [P, 2, TPS, 6]), sb("ln_mean_var", [P, 2, TPS, 2])
        ve, rstd = sb("ln_var_eps", [P, 3, TPS]), sb("ln_rstd", [P, 3, TPS])
        ss = sb("square_sums", [P, TPS])
        xnTh, xnTl = ([sb(f"xnT_{n}{i}", [P, S], F32R) for i in range(2)] for n in ("high", "low"))
        x2T = [sb(f"x2T{i}", [P, 2 * S]) for i in range(2)]
        hh = [sb(f"h_rows{i}", [P, TPS, D]) for i in range(2)]
        kc, ks = sb("k_cos", [P, 2, S]), sb("k_sin", [P, 2, S])
        kf = sb("k_twice", [P, NKV, S])
        kkh, kkl = ([sb(f"k_twice_{n}{i}", [P, NKV, S], F32R) for i in range(2)] for n in ("high", "low"))
        vv = [sb(f"v_rows{i}", [P, TPS, NKV * HD]) for i in range(2)]
        gh = [sb(f"gelu_h{i}", [P, HB, S]) for i in range(2)]
        oT = [sb(f"attn_outT{i}", [P, PAIRS, S]) for i in range(2)]
        qd = [sb(f"q_twice{i}", [P, 2, S]) for i in range(2)]
        qs = [sb(f"q_stack{i}", [P, 2, S]) for i in range(2)]
        qh, ql = ([sb(f"q_stack_{n}{i}", [P, 2, S], F32R) for i in range(4)] for n in ("high", "low"))
        pp = [sb(f"probs{i}", [P, 2 * SCW]) for i in range(2)]

        bank_q = psum("bank_q")
        bank_s = [psum(f"bank_s{i}") for i in range(2)]
        bank_av = [psum(f"bank_av{i}") for i in range(2)]
        m0, m1, bank_o = psum("bank_m0"), psum("bank_m1"), psum("bank_out")

        s_zero, s_zeroed = sem("s_zero_ready"), sem("s_slots_zeroed")
        s_c, s_gate = sem("s_exponent_ready"), sem("s_gate_ready")
        q_done, qs_ready = sem("q_done"), sem("qs_ready")
        qd_ready, qh_ready, ql_ready = sem("q_twice_ready"), sem("q_high_ready"), sem("q_low_ready")
        s_done, mask_ready = sem("s_done"), sem("mask_ready")
        s_split, xh_ready = sem("s_weights_split"), sem("xnT_high_ready")
        kf_ready, kh_ready = sem("k_sum_ready"), sem("k_high_ready")
        kd_ready = [sem(f"k_twice_ready{i}") for i in range(2)]
        av_done, ot_ready = sem("av_done"), sem("ot_ready")
        f_done, gh_ready = sem("f_done"), sem("gh_ready")
        o_done = sem("o_done")
        t_done, xnT_ready = sem("t_done"), sem("xnT_ready")
        k_done, kc_done = sem("k_done"), sem("kc_done")
        kk_ready = sem("kk_ready")
        vp_done, v_ready = sem("vp_done"), sem("v_ready")
        t2_done, x2T_ready = sem("t2_done"), sem("x2T_ready")
        lg_done, lg_ready = sem("lg_done"), sem("lg_ready")
        st1, agg1, ve1, rs1, xn_ready = sem("st1"), sem("agg1"), sem("ve1"), sem("rstd1_ready"), sem("xn_ready")
        xres_ready = sem("xres_ready")
        x1a, x1b = sem("x1_sum"), sem("x1_biased")
        st2, agg2, ve2, rs2, xn2_ready = sem("st2"), sem("agg2"), sem("ve2"), sem("rstd2_ready"), sem("xn2_ready")
        ss_ready, ve3, r_ready, hh_ready = sem("ss_ready"), sem("ve3"), sem("r_ready"), sem("hh_ready")
        x2T_stored, hh_stored = ([sem(f"{n}_stored{i}") for i in range(2)] for n in ("x2T", "hh"))

        block = ctx.enter_context(nc.Block())

        def iterations(eng, body):
            body(-1, 1, cur=False, prev=False, nxt=True)
            body(0, 0, cur=True, prev=False, nxt=True)
            body(1, 1, cur=True, prev=True, nxt=True)
            body(2, 0, cur=True, prev=True, nxt=True)
            with eng.Fori(3, B - 2, 2) as b:
                body(b, 1, cur=True, prev=True, nxt=True)
                body(b + 1, 0, cur=True, prev=True, nxt=True)
            body(B - 1, 1, cur=True, prev=True, nxt=False)
            body(B, 0, cur=False, prev=True, nxt=False)

        @block.sync
        def _(sp):
            sp.wait_ge(s_zero, 1)
            slots = d["slot_in"].rearrange("(m p) d -> m p d", p=P)
            share = SLOT_TILES // B

            def clear(first, count):
                sp.dma_start(slots[bass.ds(first, count)].rearrange("m p d -> p m d"), zero[:, 0:count, :]).then_inc(s_zeroed, 16)

            def body(b, par, cur, prev, nxt):
                if nxt:
                    sp.wait_ge(kf_ready, b + 2)
                    for to, start in ((HD, HD // 2), (HD + HD // 2, 0)):
                        sp.dma_start(kf[to:to + HD // 2], kf[start:start + HD // 2]).then_inc(kd_ready[1 - par], 16)
                if not prev:
                    return
                sp.wait_ge(x2T_ready, b)
                sp.dma_start(d["x2T"][bass.ds(b - 1, 1)].rearrange("a p t -> p (a t)"), x2T[1 - par][:]).then_inc(x2T_stored[1 - par], 16)
                sp.wait_ge(hh_ready, b)
                sp.dma_start(d["h_rows"][bass.ds(b - 1, 1)].rearrange("a (t p) d -> p (a t) d", p=P),
                             hh[1 - par][:]).then_inc(hh_stored[1 - par], 16)
                clear((b - 1) * share, share)

            iterations(sp, body)
            clear(B * share, SLOT_TILES - B * share)
            sp.wait_ge(s_zeroed, 16 * (B + 1))
            for stored in x2T_stored + hh_stored:
                sp.wait_ge(stored, 16 * (B // 2))

        @block.gpsimd
        def _(pool):
            g = nc.gpsimd
            g.memset(mhalf[:], -0.5).then_inc(s_c, 1)
            g.memset(zero[:], 0.0).then_inc(s_zero, 1)
            pool.wait_ge(s_c, 1)
            pool.wait_ge(s_w, 16 * len(loads))

            def rsqrt(n, src, add, counted, value, ready):
                if n < 2:
                    g.tensor_scalar(ve[:, n, :], src, add, None, ALU.add).then_inc(counted, 1)
                else:
                    g.tensor_scalar(ve[:, n, :], src, 1.0 / D, add, ALU.mult, ALU.add).then_inc(counted, 1)
                pool.wait_ge(counted, value)
                g.tensor_tensor(rstd[:, n, :], ve[:, n, :], mhalf[:], ALU.pow).then_inc(ready, 1)

            def body(b, par, cur, prev, nxt):
                nb = 1 - par
                for j in range(PAIRS):
                    n = b * PAIRS + j
                    def lower_keys(at, sequence, ready, groups):
                        pool.wait_ge(kh_ready, 2 * sequence + ready)
                        g.tensor_tensor(kkl[at][:, groups], kf[:, groups], kkh[at][:, groups].bitcast(F32), ALU.subtract).then_inc(kk_ready, 1)

                    if j == 7 and nxt:
                        lower_keys(nb, b + 1, 1, slice(0, 1))
                    if j == 0 and cur:
                        lower_keys(par, b, 2, slice(1, 2))
                        lower_keys(par, b, 2, slice(2, NKV))
                    if j == 1 and nxt:
                        wait_apart(pool, (s_c, 1), (agg1, b + 2), (xn_ready, b + 1))
                        rsqrt(0, mv[:, 0, :, 1], EPS_LN, ve1, b + 2, rs1)
                    if j == 4 and prev:
                        wait_apart(pool, (s_c, 1), (agg2, b), (xn2_ready, b - 1))
                        rsqrt(1, mv[:, 1, :, 1], EPS_LN, ve2, b, rs2)
                    if j == 7 and prev:
                        wait_apart(pool, (s_c, 1), (ss_ready, b), (hh_ready, b - 1), (lg_ready, b - 1))
                        rsqrt(2, ss[:], EPS_RMS, ve3, b, r_ready)
                    if (cur and j < PAIRS - 2) or (nxt and j >= PAIRS - 2):
                        nq = (j + 2) % 4
                        pool.wait_ge(qh_ready, n + 3)
                        g.tensor_tensor(ql[nq][:], qs[j % 2][:], qh[nq][:].bitcast(F32), ALU.subtract).then_inc(ql_ready, 1)

            iterations(pool, body)

        @block.tensor
        def _(pe):
            t = nc.tensor
            pe.wait_ge(s_w, 16 * len(loads))
            pe.wait_ge(s_gate, 1)

            def product(out, high, low, other_high, other_low):
                t.matmul(out, high, other_high, start=True, stop=False)
                t.matmul(out, high, other_low, start=False, stop=False)
                return t.matmul(out, low, other_high, start=False, stop=True)

            def body(b, par, cur, prev, nxt):
                nb = 1 - par
                for j in range(PAIRS):
                    n = b * PAIRS + j
                    if cur:
                        if j in (0, 2, 4):
                            pe.wait_ge(kk_ready, 3 * b + 1 + j // 2)
                        pe.wait_ge(ql_ready, n + 1)
                        group = 2 * j // (NH // NKV)
                        for c in range(TPS):
                            keys = slice(c * P, (c + 1) * P)
                            reach(pe, mask_ready, 2 * n - 1 + c)
                            product(bank_s[c][:, 0:2 * (S - c * P)], kkh[par][:, group, keys], kkl[par][:, group, keys],
                                    qh[j % 4][:, :, c * P:S], ql[j % 4][:, :, c * P:S]).then_inc(s_done, 1)
                    if (cur and j < PAIRS - 3) or (nxt and j >= PAIRS - 3):
                        near = j < PAIRS - 3
                        at, nj = (par, j + 3) if near else (nb, j + 3 - PAIRS)
                        if j == PAIRS - 3:
                            pe.wait_ge(xnT_ready, b + 2)
                        reach(pe, qd_ready, n + 3)
                        product(bank_q[:, 0:S], wqh[:, nj, :], wql[:, nj, :],
                                xnTh[at][:], xnTl[at][:]).then_inc(q_done, 1)
                    if (cur and j > 0) or (prev and j == 0):
                        pj, vb, vseq = (j - 1, vv[par], b) if j else (PAIRS - 1, vv[nb], b - 1)
                        reach(pe, mask_ready, 2 * n)
                        reach(pe, ot_ready, n - 2)
                        if j < 2:
                            pe.wait_ge(v_ready, vseq + 1)
                        bank = bank_av[(j + 1) % 2]
                        for c in range(TPS):
                            for h in range(2):
                                g = (2 * pj + h) // (NH // NKV)
                                cols = slice(0, S) if c == 0 else slice(P, S)
                                wide = S - c * P
                                rhs = pp[pj % 2][:, 2 * S * c + h * wide:2 * S * c + (h + 1) * wide]
                                last = t.matmul(bank[h * HD:(h + 1) * HD, cols], vb[:, c, g * HD:(g + 1) * HD], rhs,
                                                start=(c == 0), stop=(c == 1), skip_group_check=True)
                        last.then_inc(av_done, 1)
                    if j in (4, 5) and cur:
                        if j == 4:
                            reach(pe, x1a, b)
                        else:
                            pe.wait_ge(gh_ready, 2 * b + 1)
                        for c in range(2):
                            rows = slice((2 * (j - 4) + c) * P, (2 * (j - 4) + c + 1) * P)
                            last = product(bank_o[:, c * S:(c + 1) * S], bw1h[:, rows], bw1l[:, rows], xnTh[par][:], xnTl[par][:])
                        last.then_inc(f_done, 1)
                    if j in (0, 2) and prev:
                        if j == 0:
                            pe.wait_ge(gh_ready, 2 * b)
                        q = slice(j // 2 * P, (j // 2 + 1) * P)
                        for k in range(HB):
                            t.matmul(bank_o[:, q], gh[nb][:, k, q], w["bw2T"][:, k * P:(k + 1) * P], start=(k == 0), stop=False)
                    if j in (1, 2) and prev:
                        if j == 1:
                            pe.wait_ge(ot_ready, PAIRS * b)
                        q = slice((j - 1) * P, j * P)
                        for k in range(PAIRS):
                            last = t.matmul(bank_o[:, q], oT[nb][:, k, q], wo[:, k, :], start=False, stop=(k == PAIRS - 1))
                        if j == 2:
                            last.then_inc(o_done, 1)
                    if j == 2 and nxt:
                        pe.wait_ge(xn_ready, b + 2)
                        reach(pe, v_ready, b + 1)
                        for c in range(TPS):
                            last = t.transpose(m0[:, c * P:(c + 1) * P], xn[:, c, :], ident[:])
                        last.then_inc(t_done, 1)
                    if j == 3 and nxt:
                        pe.wait_ge(xnT_ready, b + 2)
                        reach(pe, lg_ready, b - 1)
                        for c in range(4):
                            last = product((m0, m1)[c // 2][:, (c % 2) * S:(c % 2 + 1) * S], wkh[:, c, :], wkl[:, c, :],
                                           xnTh[nb][:], xnTl[nb][:])
                        last.then_inc(k_done, 1)
                    if j == 6 and prev:
                        pe.wait_ge(xn2_ready, b)
                        for c in range(TPS):
                            t.transpose(m1[:, c * P:(c + 1) * P], xn2[:, c, :], ident[:])
                            back = S + (TPS - 1 - c) * P
                            last = t.transpose(m1[:, back:back + P], xn2[:, c, :], flip[:])
                        last.then_inc(t2_done, 1)
                    if j == 7 and nxt:
                        pe.wait_ge(kc_done, b + 2)
                        for c in range(TPS):
                            q = slice(c * P, (c + 1) * P)
                            last = product(m0[:, c * S:(c + 1) * S], xnTh[nb][:, q], xnTl[nb][:, q], wvh[:], wvl[:])
                        last.then_inc(vp_done, 1)
                    if j == 7 and prev:
                        pe.wait_ge(x2T_ready, b)
                        for c in range(TPS):
                            last = t.matmul(m1[:, c * E:(c + 1) * E], x2T[nb][:, c * P:(c + 1) * P], gate[:], start=True, stop=True)
                        last.then_inc(lg_done, 1)

            iterations(pe, body)

        @block.scalar
        def _(act):
            a = nc.scalar
            act.wait_ge(s_w, 16 * len(loads))

            def body(b, par, cur, prev, nxt):
                nb = 1 - par
                for j in range(PAIRS):
                    n = b * PAIRS + j
                    if (cur and j < PAIRS - 3) or (nxt and j >= PAIRS - 3):
                        act.wait_ge(q_done, n + 4)
                        reach(act, qs_ready, n + 2)
                        for h in range(2):
                            for half in range(2):
                                last = a.activation(qd[(j + 1) % 2][half * HD:(half + 1) * HD, h, :],
                                                    bank_q[h * HD:(h + 1) * HD, 0:S], ACT.Copy)
                        last.then_inc(qd_ready, 1)
                    if (cur and j < PAIRS - 2) or (nxt and j >= PAIRS - 2):
                        act.wait_ge(qs_ready, n + 3)
                        reach(act, s_done, 2 * n - 2)
                        a.activation(qh[(j + 2) % 4][:], qs[j % 2][:], ACT.Copy).then_inc(qh_ready, 1)
                    if (cur and j > 0) or (prev and j == 0):
                        pj, dst = (j - 1, oT[par]) if j else (PAIRS - 1, oT[nb])
                        act.wait_ge(av_done, n)
                        if j == 1:
                            reach(act, o_done, b - 1)
                        a.activation(dst[:, pj, :], bank_av[(j + 1) % 2][:, 0:S], ACT.Copy).then_inc(ot_ready, 1)
                    if j in (4, 5) and cur:
                        act.wait_ge(f_done, 2 * b + j - 3)
                        reach(act, o_done, b - 1)
                        for c in range(2):
                            k = 2 * (j - 4) + c
                            last = a.activation(gh[par][:, k, :], bank_o[:, c * S:(c + 1) * S], ACT.Gelu, bias=b1[:, k:k + 1])
                        last.then_inc(gh_ready, 1)
                    if j == 2 and nxt:
                        act.wait_ge(t_done, b + 2)
                        a.activation(xnTh[nb][:], m0[:, 0:S], ACT.Copy).then_inc(xh_ready, 1)
                    def upper_keys(groups):
                        a.activation(kkh[nb][:, groups], kf[:, groups], ACT.Copy).then_inc(kh_ready, 1)

                    if j == 6 and nxt:
                        act.wait_ge(kd_ready[nb], 16 * (b + 1 - nb) + 32)
                        upper_keys(slice(0, 1))
                    if j == 6 and prev:
                        act.wait_ge(t2_done, b)
                        reach(act, lg_done, b - 2)
                        reach(act, x2T_stored[nb], 8 * (b - 1 - nb))
                        a.activation(x2T[nb][:], m1[:], ACT.Copy).then_inc(x2T_ready, 1)
                        reach(act, r_ready, b - 1)
                        reach(act, ss_ready, b - 1)
                        for c in range(TPS):
                            last = a.activation(sq[:, c, :], xn2[:, c, :], ACT.Square, accum_out=ss[:, c:c + 1])
                        last.then_inc(ss_ready, 1)
                    if j == 7 and nxt:
                        upper_keys(slice(1, NKV))
                        act.wait_ge(vp_done, b + 2)
                        a.activation(vv[nb][:].rearrange("p t n -> p (t n)"), m0[:], ACT.Copy).then_inc(v_ready, 1)

            iterations(act, body)

        @block.vector
        def _(dve):
            v = nc.vector
            dve.wait_ge(s_w, 16 * len(loads))
            parts = ((wk, wkh, wkl), (wv, wvh, wvl), (wq, wqh, wql), (w["bw1T"], bw1h, bw1l))
            for whole, high, low in parts:
                v.tensor_copy(high[:], whole[:]).then_inc(s_split, 1)
            for i, (whole, high, low) in enumerate(parts):
                dve.wait_ge(s_split, i + 1)
                v.tensor_tensor(low[:], whole[:], high[:].bitcast(F32), ALU.subtract)
            v.tensor_scalar(gate[:], gate[:], rmsw[:, 0:1], None, ALU.mult).then_inc(s_gate, 1)

            def body(b, par, cur, prev, nxt):
                nb = 1 - par
                for j in range(PAIRS):
                    n = b * PAIRS + j
                    def mask(c):
                        columns = slice(2 * S * c, 2 * S * c + 2 * (S - c * P))
                        dve.wait_ge(s_done, 2 * n + c + 1)
                        if c == 0:
                            reach(dve, av_done, n - 1)
                        v.tensor_tensor(pp[j % 2][:, columns], bank_s[c][:, 0:2 * (S - c * P)], decay[:, j, columns],
                                        ALU.mult).then_inc(mask_ready, 1)

                    if cur:
                        mask(0)
                    if (cur and j < PAIRS - 2) or (nxt and j >= PAIRS - 2):
                        dve.wait_ge(qd_ready, n + 3)
                        reach(dve, ql_ready, n + 1)
                        v.tensor_tensor(qs[j % 2][:], qd[j % 2][:],
                                        rope_q[:].unsqueeze(1).to_broadcast([P, 2, S]), ALU.mult).then_inc(qs_ready, 1)
                    if cur:
                        mask(1)
                    if j == 0 and nxt:
                        wait_apart(dve, (s_x, 128), (rs1, b + 1), (agg1, b + 1))
                        for c in range(TPS):
                            last = v.bn_stats(st[:, 0, c, :], x1[:, bass.ds(2 * b + 2 + c, 1), :].rearrange("p a d -> p (a d)"))
                        last.then_inc(st1, 1)
                        wait_apart(dve, (s_x, 128), (st1, b + 2), (xn_ready, b + 1))
                        for c in range(TPS):
                            last = v.bn_aggr(mv[:, 0, c, :], st[:, 0, c, :])
                        last.then_inc(agg1, 1)
                    if j == 1 and nxt:
                        dve.wait_ge(rs1, b + 2)
                        reach(dve, t_done, b + 1)
                        for c in range(TPS):
                            last = v.tensor_scalar(xn[:, c, :], x1[:, bass.ds(2 * b + 2 + c, 1), :].rearrange("p a d -> p (a d)"),
                                                   mv[:, 0, c, 0:1], rstd[:, 0, c:c + 1], ALU.subtract, ALU.mult)
                        last.then_inc(xn_ready, 1)
                    if j == 2 and prev:
                        rows = x1[:, bass.ds(2 * b - 2, 2), :]
                        dve.wait_ge(xn_ready, b)
                        v.tensor_tensor(rows, rows, b2[:].unsqueeze(1).to_broadcast([P, TPS, D]), ALU.add).then_inc(x1b, 1)
                    if j == 3 and prev:
                        rows = x1[:, bass.ds(2 * b - 2, 2), :]
                        dve.wait_ge(o_done, b)
                        dve.wait_ge(x1b, b)
                        v.tensor_tensor(rows, bank_o[:, 0:S].rearrange("p (t d) -> p t d", t=TPS), rows, ALU.add).then_inc(x1a, 1)
                        wait_apart(dve, (s_x, 128), (x1a, b), (agg2, b - 1))
                        for c in range(TPS):
                            last = v.bn_stats(st[:, 1, c, :], x1[:, bass.ds(2 * b - 2 + c, 1), :].rearrange("p a d -> p (a d)"))
                        last.then_inc(st2, 1)
                        wait_apart(dve, (s_x, 128), (st2, b), (xn2_ready, b - 1), (rs2, b - 1))
                        for c in range(TPS):
                            last = v.bn_aggr(mv[:, 1, c, :], st[:, 1, c, :])
                        last.then_inc(agg2, 1)
                    if j == 2 and nxt:
                        dve.wait_ge(xh_ready, b + 2)
                        v.tensor_tensor(xnTl[nb][:], m0[:, 0:S], xnTh[nb][:].bitcast(F32), ALU.subtract).then_inc(xnT_ready, 1)
                    if j == 4 and nxt:
                        dve.wait_ge(k_done, b + 2)
                        reach(dve, kf_ready, b + 1)
                        bc = lambda r: r[:].unsqueeze(1).to_broadcast([P, 2, S])
                        v.tensor_tensor(kc[:], m0[:].rearrange("p (u t) -> p u t", u=2), bc(rope_kc), ALU.mult)
                        v.tensor_tensor(ks[:], m1[:].rearrange("p (u t) -> p u t", u=2), bc(rope_ks), ALU.mult).then_inc(kc_done, 1)
                    if j == 5 and nxt:
                        dve.wait_ge(kc_done, b + 2)
                        reach(dve, kk_ready, 3 * (b + 1))
                        for half in range(2):
                            r = slice(half * HD, (half + 1) * HD)
                            last = v.tensor_tensor(kf[0:HD].rearrange("p (u g) t -> p g u t", g=2)[:, half], kc[r], ks[r], ALU.add)
                        last.then_inc(kf_ready, 1)
                    if j == 5 and prev:
                        dve.wait_ge(rs2, b)
                        reach(dve, t2_done, b - 1)
                        reach(dve, hh_ready, b - 1)
                        reach(dve, xres_ready, b - 1)
                        reach(dve, ss_ready, b - 1)
                        for c in range(TPS):
                            last = v.tensor_scalar(xn2[:, c, :], x1[:, bass.ds(2 * b - 2 + c, 1), :].rearrange("p a d -> p (a d)"),
                                                   mv[:, 1, c, 0:1], rstd[:, 1, c:c + 1], ALU.subtract, ALU.mult)
                        last.then_inc(xn2_ready, 1)
                    if j == 7 and prev:
                        rows = x1[:, bass.ds(2 * b - 2, 2), :]
                        dve.wait_ge(xn2_ready, b)
                        v.tensor_tensor(rows, rows, xn2[:], ALU.add).then_inc(xres_ready, 1)
                        dve.wait_ge(r_ready, b)
                        reach(dve, hh_stored[nb], 8 * (b - 1 - nb))
                        for c in range(TPS):
                            last = v.tensor_scalar(hh[nb][:, c, :], xn2[:, c, :], rstd[:, 2, c:c + 1], None, ALU.mult)
                        last.then_inc(hh_ready, 1)
                        dve.wait_ge(lg_done, b)
                        for c in range(TPS):
                            last = v.tensor_scalar(logits[:, bass.ds(2 * b - 2 + c, 1), :].rearrange("p a e -> p (a e)"),
                                                   m1[:, c * E:(c + 1) * E], rstd[:, 2, c:c + 1], None, ALU.mult)
                        last.then_inc(lg_ready, 1)

            iterations(dve, body)


SCRATCH = {"slot_in": (SLOTS, D), "slot_out": (SLOTS, D), "kpad": (CH, P + S),
           "x2T": (B, P, 2 * S), "h_rows": (B, S, D)}


def in_turns(eng, count, ring, body):
    for i in range(ring):
        body(i, i)
    with eng.Fori(ring, count - ring + 1, ring) as i:
        for turn in range(ring):
            body(i + turn, turn)


def pairwise(eng, count, body):
    in_turns(eng, count, 2, body)


def route_and_convolve_block(nc, d, w):
    with ExitStack() as ctx:
        def sb(name, shape, dt=F32):
            return ctx.enter_context(nc.sbuf_tensor(name, shape, dt))

        def psum(name):
            return ctx.enter_context(nc.psum_tensor(name, [P, 512], F32))

        def sem(name):
            return ctx.enter_context(nc.semaphore(name))

        logits, slot, weight, tile_expert = w["logits"], w["slot"], w["weight"], w["tile_expert"]
        xs, w13h, w13l = w["xs"], w["w13h"], w["w13l"]
        full = [P, TILES, E]
        earlier, ones = sb("earlier_sb", [P, P]), sb("ones_sb", [P, P])
        eid, tid = sb("expert_minus", [P, E]), sb("tile_ids", [1, SLOT_TILES])
        scores, work, one0, one1, taken = (sb(n, full) for n in ("scores", "work", "is_first", "is_second", "is_taken"))
        scan_a, scan_b, before = scores, taken, sb("rank_before", full)
        top, low, tot = sb("top", [P, 3, TILES]), sb("low", [P, TILES]), sb("total", [P, TILES])
        cnt, cnt_i = sb("tiles_of", [P, 4, E]), sb("tiles_of_int", [P, E], I32)
        te = sb("tile_expert_f", [1, SLOT_TILES])
        bank_r, bank_t = psum("bank_rank"), psum("bank_total")
        win, cw = sb("win_x", [P, CH]), sb("conv_w_bc", [P, TAPS, CH])
        wtap = sb("wtap", [P, TAPS, CH])
        cb = sb("conv_b_row", [1, CH])
        xp = [sb(f"x2T_back{i}", [P, S + TAPS - 1]) for i in range(2)]
        bank_x = [psum(f"bank_x{i}") for i in range(2)]
        hrow = [sb(f"route_rows{i}", [P, TPS, D]) for i in range(2)]
        idx = [sb(f"route_index{i}", [P, 2, TPS], I32) for i in range(2)]
        rmsw = sb("rms_w_experts", [P, 1])
        raw = w13l[:].bitcast(F32)

        s_in, s_step = sem("s_route_loaded"), sem("s_route_step")
        s_sh, s_ex, s_oh, s_cnt = sem("s_shifted"), sem("s_exps"), sem("s_onehots"), sem("s_counts")
        s_slots, s_pad = sem("s_slots_ready"), sem("s_pad_zero")
        s_conv, s_tap, s_w2 = sem("s_conv_loaded"), sem("s_taps_ready"), sem("s_w2_loaded")
        raw_loaded = sem("w13_raw_loaded")
        raw_scaled, high_ready, low_ready = sem("w13_scaled"), sem("w13_high_ready"), sem("w13_low_ready")
        xp_loaded = [sem(f"xp_loaded{i}") for i in range(2)]
        x_done, xs_ready = sem("x_done"), sem("xs_ready")
        row_loaded = [sem(f"route_row_loaded{i}") for i in range(2)]
        idx_ready = sem("route_index_ready")
        row_sent = [sem(f"route_row_sent{i}") for i in range(2)]
        consts = [(earlier[:], d["earlier"]), (ones[:], d["ones"]), (eid[:], d["expert_minus"]), (tid[:], d["tile_ids"]),
                  (rmsw[:], d["rms_w"])]
        conv = [(win[:], d["W_inT"][:, 0:CH]), (cw[:], d["conv_wT"].partition_broadcast(P)), (cb[:], d["conv_b"].rearrange("(a n) -> a n", a=1))]
        block = ctx.enter_context(nc.Block())

        @block.sync
        def _(sp):
            for dst, src in conv:
                sp.dma_start(dst, src).then_inc(s_conv, 16)
            for dst, src in consts:
                sp.dma_start(dst, src).then_inc(s_in, 16)

            def load(b, par):
                reach(sp, x_done, b - 1)
                sp.dma_start(xp[par][:, 0:S], d["x2T"][bass.ds(b, 1), :, S:2 * S].rearrange("a p t -> p (a t)")).then_inc(xp_loaded[par], 16)
                reach(sp, row_sent[par], 32 * (b - par))
                sp.dma_start(hrow[par][:], d["h_rows"][bass.ds(b, 1)].rearrange("a (t p) d -> p (a t) d", p=P)).then_inc(row_loaded[par], 16)

            pairwise(sp, B, load)

        @block.gpsimd
        def _(pool):
            g = nc.gpsimd
            for i in range(2):
                g.memset(xp[i][:, S:], 0.0).then_inc(s_pad, 1)
            pool.wait_ge(s_slots, 2)

            def route(b, par):
                reach(pool, row_sent[par], 32 * (b - par))
                g.tensor_copy(idx[par][:], slot[:, :, bass.ds(2 * b, 2)]).then_inc(idx_ready, 1)
                wait_apart(pool, (s_pad, 2), (idx_ready, b + 1), (row_loaded[par], 8 * (b - par) + 16))
                for k in range(2):
                    for t in range(TPS):
                        g.indirect_dma_start(d["slot_in"], bass.IndirectOffsetOnAxis(ap=idx[par][:, k, t:t + 1], axis=0),
                                             hrow[par][:, t, :], None).then_inc(row_sent[par], 16)

            pairwise(pool, B, route)
            for par in range(2):
                pool.wait_ge(row_sent[par], 32 * B)

        @block.tensor
        def _(pe):
            t = nc.tensor
            pe.wait_ge(s_in, 16 * len(consts))
            pe.wait_ge(s_tap, 1)
            pe.wait_ge(s_pad, 2)

            def project(b, par):
                pe.wait_ge(xp_loaded[par], 8 * (b - par) + 16)
                reach(pe, xs_ready, b - 1)
                for c in range(TPS):
                    q = slice(c * CH, (c + 1) * CH)
                    for k in range(TAPS):
                        o = (TPS - 1 - c) * P + TAPS - 1 - k
                        t.matmul(bank_x[par][:, q], xp[par][:, o:o + P], wtap[:, k, :], start=(k == 0), stop=False)
                    last = t.matmul(bank_x[par][:, q], ones[0:1, :], cb[:], start=False, stop=True)
                last.then_inc(x_done, 1)

            project(0, 0)
            project(1, 1)
            flat = taken[:].rearrange("p t e -> p (t e)")
            pe.wait_ge(s_oh, 1)
            t.matmul(bank_r[:], earlier[:], flat, start=True, stop=True).then_inc(s_cnt, 1)
            t.matmul(bank_t[:], ones[:], flat, start=True, stop=True).then_inc(s_cnt, 1)
            with pe.Fori(2, B - 1, 2) as b:
                project(b, 0)
                project(b + 1, 1)

        @block.scalar
        def _(act):
            act.wait_ge(s_sh, 1)
            nc.scalar.activation(scores[:], work[:], ACT.Exp).then_inc(s_ex, 1)
            for par in range(2):
                act.wait_ge(xp_loaded[par], 16)
            for k, name in enumerate(("w1T", "w3T")):
                act.dma_start(raw[:, :, k, :], d[name]).then_inc(raw_loaded, 16)
            act.dma_start(w["w2"][:], d["w2T"]).then_inc(s_w2, 16)

            def silu(b, par):
                act.wait_ge(x_done, b + 1)
                nc.scalar.activation(xs[:, :, :, bass.ds(b, 1)].rearrange("p h c a -> p c (h a)"),
                                     bank_x[par][:].rearrange("p (c h) -> p c h", c=TPS), ACT.Silu).then_inc(xs_ready, 1)

            pairwise(act, B, silu)
            act.wait_ge(s_w2, 16)

        @block.vector
        def _(dve):
            v = nc.vector
            step = Chain(dve, s_step)
            over_e = lambda a: a.unsqueeze(2).to_broadcast(full)
            over_t = lambda a: a.unsqueeze(1).to_broadcast(full)
            dve.wait_ge(s_in, 16 * len(consts))
            dve.wait_ge(s_conv, 16 * len(conv))
            for t in range(TAPS):
                last = v.tensor_tensor(wtap[:, t, :], win[:], cw[:, t, :], ALU.mult)
            last.then_inc(s_tap, 1)
            step(v.tensor_reduce(low[:], logits[:], AX.X, ALU.max))
            v.tensor_tensor(work[:], logits[:], over_e(low[:]), ALU.subtract).then_inc(s_sh, 1)
            dve.wait_ge(s_ex, 1)
            step(v.tensor_reduce(tot[:], scores[:], AX.X, ALU.add))
            step(v.reciprocal(tot[:], tot[:]))
            step(v.tensor_tensor(scores[:], scores[:], over_e(tot[:]), ALU.mult))
            for k, pick in ((0, one0), (1, one1)):
                step(v.tensor_reduce(top[:, k, :], scores[:], AX.X, ALU.max))
                step(v.tensor_tensor(work[:], scores[:], over_e(top[:, k, :]), ALU.is_equal))
                step(v.tensor_tensor(work[:], work[:], over_t(eid[:]), ALU.mult))
                step(v.tensor_reduce(low[:], work[:], AX.X, ALU.min))
                step(v.tensor_tensor(pick[:], over_t(eid[:]), over_e(low[:]), ALU.is_equal))
                if k == 0:
                    step(v.scalar_tensor_tensor(scores[:].rearrange("p t e -> p (t e)"), pick[:].rearrange("p t e -> p (t e)"), -2.0,
                                                scores[:].rearrange("p t e -> p (t e)"), ALU.mult, ALU.add))
            v.tensor_tensor(taken[:], one0[:], one1[:], ALU.add).then_inc(s_oh, 1)
            step(v.tensor_tensor(top[:, 2, :], top[:, 0, :], top[:, 1, :], ALU.add))
            step(v.reciprocal(top[:, 2, :], top[:, 2, :]))
            for k in range(2):
                step(v.tensor_tensor(weight[:, k, :], top[:, k, :], top[:, 2, :], ALU.mult))
            dve.wait_ge(s_cnt, 2)
            step(v.tensor_copy(before[:], bank_r[:].rearrange("p (t e) -> p t e", e=E)))
            step(v.tensor_copy(scan_a[:], bank_t[:].rearrange("p (t e) -> p t e", e=E)))
            step(v.tensor_tensor(before[:], before[:], scan_a[:], ALU.subtract))
            src, dst, n = scan_a, scan_b, 1
            while n < TILES:
                step(v.tensor_copy(dst[:, 0:n, :], src[:, 0:n, :]))
                step(v.tensor_tensor(dst[:, n:, :], src[:, n:, :], src[:, :TILES - n, :], ALU.add))
                src, dst, n = dst, src, 2 * n
            step(v.tensor_tensor(before[:], before[:], src[:], ALU.add))
            step(v.tensor_scalar(cnt[:, 0, :], src[:, TILES - 1, :], float(P - 1), None, ALU.add))
            step(v.tensor_copy(cnt_i[:], cnt[:, 0, :]))
            step(v.tensor_scalar(cnt_i[:], cnt_i[:], P.bit_length() - 1, None, ALU.arith_shift_right))
            step(v.tensor_copy(cnt[:, 0, :], cnt_i[:]))
            step(v.tensor_copy(cnt[:, 1, :], cnt[:, 0, :]))
            for e in range(1, E):
                step(v.tensor_tensor(cnt[:, 1, e:e + 1], cnt[:, 1, e:e + 1], cnt[:, 1, e - 1:e], ALU.add))
            step(v.tensor_tensor(cnt[:, 2, :], cnt[:, 1, :], cnt[:, 0, :], ALU.subtract))
            step(v.tensor_scalar(cnt[:, 2, :], cnt[:, 2, :], float(P), None, ALU.mult))
            step(v.tensor_tensor(before[:], before[:], over_t(cnt[:, 2, :]), ALU.add))
            for k, pick in ((0, one0), (1, one1)):
                step(v.tensor_tensor(work[:], before[:], pick[:], ALU.mult))
                step(v.tensor_reduce(low[:], work[:], AX.X, ALU.add))
                v.tensor_copy(slot[:, k, :], low[:]).then_inc(s_slots, 1)
            step(v.tensor_scalar(te[:], tid[:], cnt[0:1, 1, 0:1], None, ALU.is_ge))
            for e in range(1, E - 1):
                step(v.scalar_tensor_tensor(te[:], tid[:], cnt[0:1, 1, e:e + 1], te[:], ALU.is_ge, ALU.add))
            step(v.tensor_copy(tile_expert[:], te[:]))
            dve.wait_ge(raw_loaded, 32)
            for e in range(E):
                v.tensor_scalar(raw[:, e], raw[:, e], rmsw[:, 0:1], None, ALU.mult).then_inc(raw_scaled, 1)
                dve.wait_ge(raw_scaled, e + 1)
                v.tensor_copy(w13h[:, e], raw[:, e]).then_inc(high_ready, 1)
                dve.wait_ge(high_ready, e + 1)
                v.tensor_tensor(w13l[:, e], raw[:, e], w13h[:, e].bitcast(F32), ALU.subtract).then_inc(low_ready, 1)
            finish_poles(v, step, w)


def experts_block(nc, d, w):
    with ExitStack() as ctx:
        def sb(name, shape, dt=F32):
            return ctx.enter_context(nc.sbuf_tensor(name, shape, dt))

        def psum(name):
            return ctx.enter_context(nc.psum_tensor(name, [P, 512], F32))

        def sem(name):
            return ctx.enter_context(nc.semaphore(name))

        w13h, w13l, w2 = w["w13h"], w["w13l"], w["w2"]
        ident = sb("ident_experts", [P, P])
        RING = 4
        hrow = [sb(f"slot_rows{i}", [P, D]) for i in range(RING)]
        hTh = [sb(f"slot_rowsT_high{i}", [P, P], F32R) for i in range(2)]
        hTl = [sb(f"slot_rowsT_low{i}", [P, P], F32R) for i in range(2)]
        si = [sb(f"silu_a{i}", [P, EI]) for i in range(2)]
        ac = [sb(f"hidden{i}", [P, EI]) for i in range(2)]
        aT = [sb(f"hiddenT{i}", [EC, ES, P]) for i in range(2)]
        orow = [sb(f"slot_result{i}", [P, D]) for i in range(2)]
        bank_a = [psum(f"bank_a{i}") for i in range(2)]
        bank_g = [psum(f"bank_g{i}") for i in range(2)]
        bank_h, bank_t = psum("bank_rowsT"), psum("bank_hiddenT")
        bank_o = [psum(f"bank_result{i}") for i in range(2)]
        HALF = S // 2
        wr, wi = sb("w_re", [P, NS, S]), sb("w_im", [P, NS, HALF])
        PART = HALF // 2
        pr, pi = sb("prod_re", [P, NS, PART]), sb("prod_im", [P, NS, PART])
        zz, zt = sb("z_power", [P, 2, NS]), sb("z_square", [P, 3, NS])
        kpad = sb("kpad_sb", [P, P + S])
        dskip = sb("d_skip_sb", [P, CB])

        s_in = sem("s_experts_const")
        row_loaded = [sem(f"slot_row_loaded{i}") for i in range(RING)]
        stored = [sem(f"slot_result_stored{i}") for i in range(2)]
        s_kstep, s_kout = sem("s_kernel_step"), sem("s_kernel_stored")
        ht_done, high_ready, hT_ready, ag_done, si_ready, ac_ready, at_done, aT_ready, o_done, o_ready = (
            sem(n) for n in ("ht_done", "hT_high_ready", "hT_ready", "ag_done", "si_ready", "ac_ready", "at_done", "aT_ready",
                             "slot_done", "slot_ready"))
        block = ctx.enter_context(nc.Block())
        M = SLOT_TILES

        def iterations(eng, body, expert=None):
            def steps(start, count, phase):
                known = {}

                def number(u):
                    m = start + u
                    if u not in known and (not isinstance(m, int) or 0 <= m < M):
                        known[u] = expert(m)
                    return known.get(u)

                for u in range(count):
                    m = start + u
                    static = isinstance(m, int)
                    parts = (not static or m + 1 < M, not static or 0 <= m < M, not static or 1 <= m <= M,
                             not static or 2 <= m <= M + 1)
                    if expert:
                        body(m, (phase + u) % 4, *parts, number(u), lambda: number(u - 2),
                             lambda: number(u + 1) if u + 1 < count else None)
                    else:
                        body(m, (phase + u) % 4, *parts)

            steps(-1, 4, 3)
            count = 12 if expert else 4
            with eng.Fori(3, M - count, count) as m:
                steps(m, count, 3)
            steps(M - 1, 3, 3)

        @block.sync
        def _(sp):
            sp.dma_start(ident[:], d["ident"]).then_inc(s_in, 16)
            sp.dma_start(dskip[:], d["D_skip"]).then_inc(s_in, 16)
            slots_in = d["slot_in"].rearrange("(m p) d -> m p d", p=P)
            slots_out = d["slot_out"].rearrange("(m p) d -> m p d", p=P)

            def load(m, ring):
                reach(sp, ht_done, m - RING + 1)
                sp.dma_start(hrow[ring][:], slots_in[bass.ds(m, 1)].rearrange("a p d -> p (a d)")).then_inc(row_loaded[ring], 16)

            def body(m, ph, ahead, first, turn, second):
                if isinstance(m, int) and m < 0:
                    load(0, 0)
                    load(1, 1)
                if not isinstance(m, int) or m + 3 < M:
                    load(m + 3, (ph + 3) % RING)
                if second:
                    par = ph % 2
                    sp.wait_ge(o_ready, m - 1)
                    sp.dma_start(slots_out[bass.ds(m - 2, 1)].rearrange("a p d -> p (a d)"), orow[par][:]).then_inc(stored[par], 16)

            for m in range(-1, 3):
                body(m, m % 4, True, True, True, m >= 2)
            with sp.Fori(3, M - 8, 4) as m:
                for u in range(4):
                    body(m + u, (3 + u) % 4, True, True, True, True)
            for m in range(M - 5, M + 2):
                body(m, m % 4, True, True, True, True)
            for par in range(2):
                sp.wait_ge(stored[par], 8 * M)

        @block.tensor
        def _(pe):
            t = nc.tensor
            pe.wait_ge(s_in, 32)

            def body(m, ph, ahead, first, turn, second, e, read_last, read_next):
                par = ph % 2
                if first:
                    pe.wait_ge(hT_ready, m + 1)
                    reach(pe, ac_ready, m - 1)
                    for k, bank in enumerate((bank_a[par], bank_g[par])):
                        wh = w13h[:, bass.ds(e, 1), k, :].rearrange("p a i -> p (a i)")
                        wl = w13l[:, bass.ds(e, 1), k, :].rearrange("p a i -> p (a i)")
                        t.matmul(bank[:, 0:EI], hTh[par][:], wh, start=True, stop=False)
                        t.matmul(bank[:, 0:EI], hTh[par][:], wl, start=False, stop=False)
                        last = t.matmul(bank[:, 0:EI], hTl[par][:], wh, start=False, stop=True)
                    last.then_inc(ag_done, 1)
                e = read_last()
                if ahead:
                    ring = (ph + 1) % RING
                    pe.wait_ge(row_loaded[ring], 4 * (m + 1 - ring) + 16)
                    reach(pe, hT_ready, m + 1)
                    t.transpose(bank_h[:, 0:P], hrow[ring][:], ident[:]).then_inc(ht_done, 1)
                if turn:
                    pe.wait_ge(ac_ready, m)
                    reach(pe, aT_ready, m - 1)
                    for k in range(ES):
                        last = t.transpose(bank_t[0:EC, k * P:(k + 1) * P], ac[1 - par][:, k * EC:(k + 1) * EC], ident[:])
                    last.then_inc(at_done, 1)
                read_next()
                if second:
                    pe.wait_ge(aT_ready, m - 1)
                    reach(pe, o_ready, m - 3)
                    for k in range(ES):
                        last = t.matmul(bank_o[par][:, 0:P], aT[par][:, k, :], w2[:, bass.ds(e, 1), k, :].rearrange("p a n -> p (a n)"),
                                        start=(k == 0), stop=(k == ES - 1))
                    last.then_inc(o_done, 1)

            iterations(pe, body, lambda m: pe.value_load(w["tile_expert"][0:1, bass.ds(m, 1)], min_val=0, max_val=E - 1))

        @block.scalar
        def _(act):
            a = nc.scalar

            def body(m, ph, ahead, first, turn, second):
                par = ph % 2
                if first:
                    act.wait_ge(ag_done, m + 1)
                    reach(act, ac_ready, m - 1)
                    a.activation(si[par][:], bank_a[par][:, 0:EI], ACT.Silu).then_inc(si_ready, 1)
                if ahead:
                    act.wait_ge(ht_done, m + 2)
                    reach(act, ag_done, m)
                    a.activation(hTh[1 - par][:], bank_h[:, 0:P], ACT.Copy).then_inc(high_ready, 1)
                if turn:
                    act.wait_ge(at_done, m)
                    reach(act, o_done, m - 2)
                    a.activation(aT[1 - par][:].rearrange("p k t -> p (k t)"), bank_t[0:EC, :], ACT.Copy).then_inc(aT_ready, 1)

            iterations(act, body)

        @block.vector
        def _(dve):
            v = nc.vector

            def body(m, ph, ahead, first, turn, second):
                par = ph % 2
                if ahead:
                    dve.wait_ge(high_ready, m + 2)
                    reach(dve, ag_done, m)
                    v.tensor_tensor(hTl[1 - par][:], bank_h[:, 0:P], hTh[1 - par][:].bitcast(F32), ALU.subtract).then_inc(hT_ready, 1)
                if first:
                    dve.wait_ge(si_ready, m + 1)
                    reach(dve, at_done, m - 1)
                    v.tensor_tensor(ac[par][:], bank_g[par][:, 0:EI], si[par][:], ALU.mult).then_inc(ac_ready, 1)
                if second:
                    dve.wait_ge(o_done, m - 1)
                    reach(dve, stored[par], 8 * (m - 2 - par))
                    v.tensor_copy(orow[par][:], bank_o[par][:, 0:P]).then_inc(o_ready, 1)

            iterations(dve, body)

        @block.gpsimd
        def _(pool):
            g = nc.gpsimd
            step = Chain(pool, s_kstep)
            poles = w["poles"]
            pool.wait_ge(s_in, 32)
            step(g.memset(kpad[:, 0:P], 0.0))
            for c in range(CB):
                q = slice(c * NS, (c + 1) * NS)
                step(g.tensor_copy(zz[:], poles[:, 0:2, q]))
                step(g.tensor_copy(wr[:, :, 0], poles[:, 2, q]))
                step(g.tensor_copy(wi[:, :, 0], poles[:, 3, q]))
                n = 1
                while n < S:
                    for lo in range(0, n, PART):
                        size = min(n, PART)
                        src, dst = slice(lo, lo + size), slice(n + lo, n + lo + size)
                        z_re, z_im = (zz[:, i, :].unsqueeze(2).to_broadcast([P, NS, size]) for i in range(2))
                        e, f = pr[:, :, 0:size], pi[:, :, 0:size]
                        step(g.tensor_tensor(e, wr[:, :, src], z_re, ALU.mult))
                        step(g.tensor_tensor(f, wi[:, :, src], z_im, ALU.mult))
                        step(g.tensor_tensor(wr[:, :, dst], e, f, ALU.subtract))
                        if n < HALF:
                            step(g.tensor_tensor(e, wr[:, :, src], z_im, ALU.mult))
                            step(g.tensor_tensor(f, wi[:, :, src], z_re, ALU.mult))
                            step(g.tensor_tensor(wi[:, :, dst], e, f, ALU.add))
                    if n < HALF:
                        step(g.tensor_tensor(zt[:, 0:2, :], zz[:], zz[:], ALU.mult))
                        step(g.tensor_tensor(zt[:, 2, :], zz[:, 0, :], zz[:, 1, :], ALU.mult))
                        step(g.tensor_tensor(zz[:, 0, :], zt[:, 0, :], zt[:, 1, :], ALU.subtract))
                        step(g.tensor_tensor(zz[:, 1, :], zt[:, 2, :], zt[:, 2, :], ALU.add))
                    n *= 2
                m = NS // 2
                while m > 1:
                    step(g.tensor_tensor(wr[:, 0:m, :], wr[:, 0:m, :], wr[:, m:2 * m, :], ALU.add))
                    m //= 2
                step(g.tensor_tensor(kpad[:, P:], wr[:, 0, :], wr[:, 1, :], ALU.add))
                step(g.tensor_tensor(kpad[:, P:P + 1], kpad[:, P:P + 1], dskip[:, c:c + 1], ALU.add))
                pool.dma_start(d["kpad"][c * P:(c + 1) * P, :], kpad[:]).then_inc(s_kout, 16)
                pool.wait_ge(s_kout, 16 * (c + 1))


def mix_and_combine_block(nc, d, w):
    with ExitStack() as ctx:
        def sb(name, shape, dt=F32):
            return ctx.enter_context(nc.sbuf_tensor(name, shape, dt))

        def psum(name):
            return ctx.enter_context(nc.psum_tensor(name, [P, 512], F32))

        def sem(name):
            return ctx.enter_context(nc.semaphore(name))

        x1, slot, weight, xs = w["x1"], w["slot"], w["weight"], w["xs"]
        HALVES, TB = CH // P, TPS * B
        LB = 4
        wz = sb("w_in_z", [P, HALVES, P])
        wout = sb("w_outT", [P, HALVES, D])
        ident = sb("ident_mixer", [P, P])
        xp = [sb(f"x2T_mix{i}", [P, S]) for i in range(2)]
        zs = sb("gate_z", [P, HALVES, TPS, B, P])
        RING = 4
        tt = [sb(f"toeplitz{i}", [P, GB, S]) for i in range(RING)]
        xg = [w["logits"][:].rearrange("p t e -> p (t e)"), sb("conv_out_group", [P, GB * TB])[:]]
        ys = xs[:].rearrange("p (i a) c b -> p i (a c b)", a=HALVES)
        flat = [tt[i][:, 0:LB * P // S, :].rearrange("p a n -> p (a n)") for i in range(RING)]
        yl = [flat[i].rearrange("p (k i) -> p k i", k=LB) for i in range(2)]
        gT = [flat[2 + i].rearrange("p (a c t) -> p a c t", a=HALVES, c=TPS) for i in range(2)]
        got = [sb(f"gathered{i}", [P, 2, D]) for i in range(RING)]
        idx = [sb(f"gather_index{i}", [P, 2], I32) for i in range(RING)]
        bank_z = [psum(f"bank_z{i}") for i in range(2)]
        bank_y = [psum(f"bank_y{i}") for i in range(2)]
        bank_t = [psum(f"bank_yT{i}") for i in range(2)]
        bank_m = [psum(f"bank_mix{i}") for i in range(2)]

        s_in, s_ready = sem("s_mixer_loaded"), sem("s_gather_start")
        xp_loaded = [sem(f"xp_mix_loaded{i}") for i in range(2)]
        t_loaded = [sem(f"toeplitz_loaded{i}") for i in range(RING)]
        xg_ready, z_done, z_ready, y_done, y_ready = (sem(n) for n in ("xg_ready", "z_done", "z_ready", "y_done", "y_ready"))
        yl_ready, yt_done, gated = sem("yl_ready"), sem("yt_done"), sem("gated_ready")
        gT_ready, mix_done, mix_added = sem("gT_ready"), sem("mix_done"), sem("mix_added")
        idx_ready = sem("gather_index_ready")
        gathered = [sem(f"gathered_sem{i}") for i in range(RING)]
        added0, added1, out_sent = sem("first_added"), sem("second_added"), sem("out_sent")
        loads = [(wz[:], d["W_zT"]), (wout[:], d["W_outT"]), (ident[:], d["ident"])]
        kp = d["kpad"]
        block = ctx.enter_context(nc.Block())

        @block.sync
        def _(sp):
            for dst, src in loads:
                sp.dma_start(dst, src).then_inc(s_in, 16)

            def load(g, turn):
                reach(sp, z_done, g - 1)
                sp.dma_start(xp[turn % 2][:], d["x2T"][bass.ds(g, 1), :, 0:S].rearrange("a p t -> p (a t)")).then_inc(xp_loaded[turn % 2], 16)
                reach(sp, y_done, g - RING + 1)
                rows = bass.AP(kp.tensor, g * (GB * (P + S)) + 1, [[1, P], [P + S, GB], [1, S]])
                sp.dma_start(tt[turn][:], rows).then_inc(t_loaded[turn], 16)

            in_turns(sp, GROUPS, RING, load)

            def store(b, par):
                sp.wait_ge(mix_added, b + 1)
                sp.dma_start(d["out"][bass.ds(b, 1)].rearrange("a (t p) d -> p (a t) d", p=P), x1[:, bass.ds(2 * b, 2), :]).then_inc(out_sent, 16)

            pairwise(sp, B, store)
            sp.wait_ge(out_sent, 16 * B)

        @block.gpsimd
        def _(pool):
            g = nc.gpsimd
            g.memset(got[0][:, 0, 0:1], 0.0).then_inc(s_ready, 1)

            def gather(t, par):
                reach(pool, added1, t - RING + 1)
                g.tensor_copy(idx[par][:].unsqueeze(2), slot[:, :, bass.ds(t, 1)]).then_inc(idx_ready, 1)
                wait_apart(pool, (s_ready, 1), (idx_ready, t + 1))
                for k in range(2):
                    g.indirect_dma_start(got[par][:, k, :], None, d["slot_out"],
                                         bass.IndirectOffsetOnAxis(ap=idx[par][:, k:k + 1], axis=0)).then_inc(gathered[par], 16)

            in_turns(pool, TILES, RING, gather)

        @block.tensor
        def _(pe):
            t = nc.tensor
            pe.wait_ge(s_in, 16 * len(loads))

            def products(g, turn):
                par = turn % 2
                pe.wait_ge(xp_loaded[par], 8 * (g - par) + 16)
                reach(pe, z_ready, g - 1)
                for a in range(HALVES):
                    last = t.matmul(bank_z[par][:, a * S:(a + 1) * S], wz[:, a, :], xp[par][:], start=True, stop=True)
                last.then_inc(z_done, 1)
                pe.wait_ge(xg_ready, g + 1)
                pe.wait_ge(t_loaded[turn], 4 * (g - turn) + 16)
                reach(pe, y_ready, g - 1)
                for i in range(GB // HALVES):
                    out = bank_y[par][:, i * P:(i + 1) * P]
                    for a in range(HALVES):
                        h = HALVES * i + a
                        t.matmul(out[a * TB:(a + 1) * TB, :], xg[par][:, h * TB:(h + 1) * TB], tt[turn][:, h, 0:P],
                                 start=True, stop=False, skip_group_check=True)
                    for a in range(HALVES):
                        h = HALVES * i + a
                        last = t.matmul(out[a * TB + B:(a + 1) * TB, :], xg[par][:, h * TB:h * TB + B], tt[turn][:, h, P:S],
                                        start=False, stop=True, skip_group_check=True)
                last.then_inc(y_done, 1)

            in_turns(pe, GROUPS, RING, products)

            def turn_products(q, par):
                pe.wait_ge(yl_ready, q + 1)
                reach(pe, gated, q - 1)
                for k in range(LB):
                    last = t.transpose(bank_t[par][:, k * P:(k + 1) * P], yl[par][:, k, :], ident[:])
                last.then_inc(yt_done, 1)

            pairwise(pe, P // LB, turn_products)

            def output(b, par):
                pe.wait_ge(gT_ready, b + 1)
                reach(pe, mix_added, b - 1)
                for c in range(TPS):
                    for a in range(HALVES):
                        last = t.matmul(bank_m[par][:, c * P:(c + 1) * P], gT[par][:, a, c, :], wout[:, a, :],
                                        start=(a == 0), stop=(a == HALVES - 1))
                last.then_inc(mix_done, 1)

            pairwise(pe, B, output)

        @block.scalar
        def _(act):
            a = nc.scalar

            def stage(g, par):
                reach(act, y_done, g - 1)
                a.activation(xg[par], xs[:, bass.ds(g * GB, GB), :, :].rearrange("p h c b -> p (h c b)"), ACT.Copy).then_inc(xg_ready, 1)

            def silu(b, par):
                act.wait_ge(z_done, b + 1)
                a.activation(zs[:, :, :, bass.ds(b, 1), :].rearrange("p a c b t -> p a c (b t)"),
                             bank_z[par][:].rearrange("p (a c t) -> p a c t", a=HALVES, c=TPS), ACT.Silu).then_inc(z_ready, 1)

            stage(0, 0)
            stage(1, 1)
            silu(0, 0)
            with act.Fori(2, GROUPS - 1, 2) as g:
                stage(g, 0)
                silu(g - 1, 1)
                stage(g + 1, 1)
                silu(g, 0)
            silu(GROUPS - 1, 1)

            act.wait_ge(y_ready, GROUPS)

            def stage_products(q, par):
                reach(act, yt_done, q - 1)
                a.activation(yl[par], ys[:, :, bass.ds(q * LB, LB)].rearrange("p i k -> p k i"), ACT.Copy).then_inc(yl_ready, 1)

            pairwise(act, P // LB, stage_products)
            act.wait_ge(gated, P // LB)

            def stage_gated(b, par):
                reach(act, mix_done, b - 1)
                a.activation(gT[par], zs[:, :, :, bass.ds(b, 1), :].rearrange("p a c b t -> p a c (b t)"), ACT.Copy).then_inc(gT_ready, 1)

            pairwise(act, B, stage_gated)

        @block.vector
        def _(dve):
            v = nc.vector

            def combine(t, par):
                dve.wait_ge(gathered[par], 8 * (t - par) + 32)
                row = x1[:, bass.ds(t, 1), :].rearrange("p a d -> p (a d)")
                share = lambda k: weight[:, k, bass.ds(t, 1)]
                v.scalar_tensor_tensor(row, got[par][:, 0, :], share(0), row, ALU.mult, ALU.add).then_inc(added0, 1)
                dve.wait_ge(added0, t + 1)
                v.scalar_tensor_tensor(row, got[par][:, 1, :], share(1), row, ALU.mult, ALU.add).then_inc(added1, 1)

            def copy_y(g, par):
                dve.wait_ge(y_done, g + 1)
                v.tensor_copy(xs[:, bass.ds(g * GB, GB), :, :].rearrange("p h c b -> p (h c b)"), bank_y[par][:]).then_inc(y_ready, 1)

            def in_eights(body):
                body(0)
                with dve.Fori(1, GROUPS // 8, 1) as i:
                    body(i)

            def groups(i):
                for u in range(8):
                    copy_y(i * 8 + u, u % 2)
                    for tile in range(3 * u // 2, 3 * (u + 1) // 2):
                        combine(i * 12 + tile, tile % RING)

            in_eights(groups)
            dve.wait_ge(z_ready, B)

            def gate(q, par):
                dve.wait_ge(yt_done, q + 1)
                here = zs[:, :, :, :, bass.ds(q * LB, LB)].rearrange("p a c b k -> p (a c b) k")
                v.tensor_tensor(here, bank_t[par][:].rearrange("p (k x) -> p x k", k=LB), here, ALU.mult).then_inc(gated, 1)

            pairwise(dve, P // LB, gate)

            def add(b, par):
                rows = x1[:, bass.ds(2 * b, 2), :]
                dve.wait_ge(mix_done, b + 1)
                dve.wait_ge(added1, 2 * b + 2)
                v.tensor_tensor(rows, bank_m[par][:, 0:S].rearrange("p (t d) -> p t d", t=TPS), rows, ALU.add).then_inc(mix_added, 1)

            def outputs(i):
                for u in range(8):
                    if u % 2:
                        combine(TILES * 3 // 4 + i * 4 + u // 2, u // 2)
                    add(i * 8 + u, u % 2)

            in_eights(outputs)


def build_program(nc, d):
    with ExitStack() as ctx:
        def sb(name, shape, dt=F32):
            return ctx.enter_context(nc.sbuf_tensor(name, shape, dt))

        w = {"x1": sb("x1", [P, TILES, D]), "logits": sb("logits", [P, TILES, E]),
             "slot": sb("slot_of_choice", [P, 2, TILES], I32), "weight": sb("choice_weight", [P, 2, TILES]),
             "poles": sb("poles", [P, 4, CB * NS]),
             "s4": sb("s4_small", [P, 20, CB * NS]), "a_imag": sb("a_imag_sb", [P, CB, NS]),
             "c_re": sb("c_re_sb", [P, CB, NS]), "c_im": sb("c_im_sb", [P, CB, NS]),
             "tile_expert": sb("tile_expert", [1, SLOT_TILES], I32)}
        with ExitStack() as first:
            w["bw1T"] = first.enter_context(nc.sbuf_tensor("bw1T", [P, HID], F32))
            w["bw1h"] = first.enter_context(nc.sbuf_tensor("bw1T_high", [P, HID], F32R))
            w["bw1l"] = first.enter_context(nc.sbuf_tensor("bw1T_low", [P, HID], F32R))
            w["bw2T"] = first.enter_context(nc.sbuf_tensor("bw2T", [P, HID], F32))
            layer0_loads(first, nc, d, w)
            setup_block(nc, d, w)
            layer0_block(nc, d, w)
        w["xs"] = sb("conv_out", [P, CH, TPS, B])
        with ExitStack() as moe:
            w["w13h"] = moe.enter_context(nc.sbuf_tensor("w13_high", [P, E, 2, EI], F32R))
            w["w13l"] = moe.enter_context(nc.sbuf_tensor("w13_low", [P, E, 2, EI], F32R))
            w["w2"] = moe.enter_context(nc.sbuf_tensor("w2T", [EC, E, ES, D], F32))
            route_and_convolve_block(nc, d, w)
            experts_block(nc, d, w)
        mix_and_combine_block(nc, d, w)


def shape_constants():
    t = np.arange(S, dtype=np.float64)
    inv = 1.0 / 10000.0 ** (np.arange(0, HD, 2, dtype=np.float64) / HD)
    ang = np.concatenate([np.outer(t, inv)] * 2, axis=-1).T
    cos, sin = np.cos(ang), np.sin(ang)
    sin = np.concatenate([-sin[:HD // 2], sin[HD // 2:]])
    slope = 2.0 ** (-8.0 / NH * (np.arange(NH) + 1))
    lag = t[None, :] - np.arange(P)[:, None]
    m = np.where(lag >= 0, np.exp(-slope[:, None, None] * np.maximum(lag, 0)), 0.0)
    pairs = lambda a: a.reshape(PAIRS, 2, P, -1).transpose(2, 0, 1, 3).reshape(P, PAIRS, -1)
    m = np.concatenate([pairs(m), pairs(m[:, :, :P])], axis=2)
    f = lambda a: np.ascontiguousarray(a, dtype=np.float32)
    return {"rope_q": f(np.concatenate([cos, -sin])), "rope_kc": f(np.concatenate([cos, cos])),
            "rope_ks": f(np.concatenate([sin, sin])), "decay": f(m), "ident": np.eye(P, dtype=np.float32),
            "flip": f(np.eye(P)[::-1]),
            "expert_minus": f(np.broadcast_to(np.arange(E) - E, (P, E))), "tile_ids": f(np.arange(SLOT_TILES)[None]),
            "earlier": f(np.triu(np.ones((P, P)), 1)), "ones": np.ones((P, P), np.float32)}


def layout(i):
    g = {k: np.asarray(v) for k, v in i.items()}
    turned = (np.arange(HD) + HD // 2) % HD
    wk = g["L0_attn_Wk"].reshape(NKV, HD, D)
    kb = np.concatenate([wk.reshape(2, P, D), wk[:, turned].reshape(2, P, D)])
    c = np.ascontiguousarray
    return {
        "x": c(g["L0_attn_x"]), "wq": c(g["L0_attn_Wq"].T.reshape(D, PAIRS, P)), "wk": c(kb.transpose(2, 0, 1)),
        "wv": c(g["L0_attn_Wv"].T), "wo": c(g["L0_attn_Wo"].T.reshape(PAIRS, P, D).transpose(1, 0, 2)),
        "ffn_w1": c(g["L0_ffn_w1"]), "ffn_b1": c(g["L0_ffn_b1"].reshape(HB, P).T), "ffn_w2": c(g["L0_ffn_w2"]), "ffn_b2": c(g["L0_ffn_b2"]),
        "W_inT": c(g["L1_attn_W_in"].T), "conv_wT": c(g["L1_attn_conv_w"].T), "conv_b": c(g["L1_attn_conv_b"]),
        "log_dt": c(g["L1_attn_log_dt"].reshape(CB, P).T), "log_A_real": c(g["L1_attn_log_A_real"]), "A_imag": c(g["L1_attn_A_imag"]),
        "C_re": c(g["L1_attn_C_re"]), "C_im": c(g["L1_attn_C_im"]), "D_skip": c(g["L1_attn_D"].reshape(CB, P).T),
        "W_zT": c(g["L1_attn_W_in"][CH:].reshape(P, CH // P, D).transpose(2, 1, 0)), "W_outT": c(g["L1_attn_W_out"].T.reshape(P, CH // P, D)),
        "rms_w": c(g["L1_ffn_rms_weight"].reshape(P, 1)), "gateT": c(g["L1_ffn_gate_w"].T),
        "w1T": c(g["L1_ffn_w1"].transpose(2, 0, 1)), "w3T": c(g["L1_ffn_w3"].transpose(2, 0, 1)),
        "w2T": c(g["L1_ffn_w2"].reshape(E, D, ES, EC).transpose(3, 0, 2, 1)),
    }


def kernel(**inputs):
    import concourse.bacc as bacc
    from concourse.bass_utils import run_bass_kernel_spmd

    nc = bacc.Bacc("TRN2", target_bir_lowering=False, num_devices=1)
    arrays = {f"in_{k}": v for k, v in {**layout(inputs), **shape_constants()}.items()}
    d = {k[3:]: nc.dram_tensor(k, v.shape, mybir.dt.from_np(v.dtype), kind="ExternalInput").ap() for k, v in arrays.items()}
    for name, shape in SCRATCH.items():
        d[name] = nc.dram_tensor(f"scratch_{name}", shape, F32, kind="Internal").ap()
    d["out"] = nc.dram_tensor("out_x", (B, S, D), F32, kind="ExternalOutput").ap()
    build_program(nc, d)
    r = run_bass_kernel_spmd(nc, [arrays], core_ids=[0])
    return r.results[0]["out_x"]
```
